# Optimizing a Trainium2 kernel written in Bass

```python
import numpy as np
import jax
import jax.numpy as jnp

def _softmax(x, axis=-1):
    return jax.nn.softmax(x, axis=axis)

def _gelu(x):
    return jax.nn.gelu(x, approximate=True)

def _silu(x):
    return jax.nn.silu(x)

def _sigmoid(x):
    return jax.nn.sigmoid(x)

def _layernorm(x, axis=-1, eps=1e-05):
    m = jnp.mean(x, axis=axis, keepdims=True)
    v = jnp.var(x, axis=axis, keepdims=True)
    return (x - m) / jnp.sqrt(v + eps)

def _scatter_add(tgt, idx, src, axis=0):
    return tgt.at[idx].add(src)

def _segment_sum(src, seg, n):
    return jax.ops.segment_sum(src, seg, n)
kernel_name = 'mk_adaln_d1_jaxref_r8_24d72a'

def setup_inputs(seed: int=0):
    np.random.seed(seed)
    _w = jnp.asarray

    def _L0_attn_setup():
        import jax, jax.numpy as jnp
        import numpy as np
        EMBED = 128
        HEADS = 16
        HD = EMBED // HEADS
        M = 32
        R = 2
        EPS = 1e-06
        C_CONST = 2.0 + EPS
        CHUNK = 64

        def _features(x, omega, quad_nodes, quad_weights):
            B, H, T, D = x.shape
            xn = x / jnp.maximum(jnp.linalg.norm(x, axis=-1, keepdims=True), 1e-12)
            proj = jnp.einsum('bhtd,rhdm->rbhtm', xn, omega)
            s = quad_nodes[:, None, None, None, None]
            sqrt_2s = jnp.sqrt(2.0 * jnp.maximum(s, 0.0))
            arg = jnp.clip(proj * sqrt_2s - s, -20.0, 20.0)
            feat = jnp.exp(arg) / np.sqrt(M).astype(np.float32)
            feat = feat * jnp.sqrt(jnp.maximum(quad_weights, 0.0))[:, None, None, None, None]
            return jnp.transpose(feat, (1, 2, 3, 0, 4)).reshape(B, H, T, R * M)
        key = jax.random.key(seed)
        ks = jax.random.split(key, 4)
        B, T = (2, 256)
        x = jax.random.normal(ks[0], (B, T, EMBED), jnp.float32)
        Wqkv = jax.random.normal(ks[1], (EMBED, 3 * EMBED), jnp.float32) * 0.02
        bqkv = jnp.zeros((3 * EMBED,), jnp.float32)
        Wout = jax.random.normal(ks[2], (EMBED, EMBED), jnp.float32) * 0.02
        bout = jnp.zeros((EMBED,), jnp.float32)
        omega = jax.random.normal(ks[3], (R, HEADS, HD, M), jnp.float32)
        nodes, weights = np.polynomial.laguerre.laggauss(R)
        quad_nodes = jnp.asarray(nodes / C_CONST, jnp.float32)
        quad_weights = jnp.asarray(weights * (C_CONST / 4.0), jnp.float32)
        return {'x': x, 'Wqkv': Wqkv, 'bqkv': bqkv, 'Wout': Wout, 'bout': bout, 'omega': omega, 'quad_nodes': quad_nodes, 'quad_weights': quad_weights}
    _L0_attn_in = _L0_attn_setup()

    def _L0_ffn_setup():
        import jax, jax.numpy as jnp
        import numpy as np
        B, S, D = (2, 128, 128)
        H, HD = (16, 64)
        E_R = 31
        K_ACT = 3
        INTER = 128
        EPS = 1e-05
        BASE = 10000.0

        def _rmsnorm(x, gamma):
            rms = jnp.sqrt(jnp.mean(x * x, axis=-1, keepdims=True) + EPS)
            return x / rms * gamma

        def _rope(x, theta):
            seq = x.shape[2]
            angles = jnp.arange(seq, dtype=theta.dtype)[:, None] * theta
            cos = jnp.cos(angles)[None, None]
            sin = jnp.sin(angles)[None, None]
            x1, x2 = (x[..., 0::2], x[..., 1::2])
            return jnp.concatenate([x1 * cos - x2 * sin, x1 * sin + x2 * cos], axis=-1)

        def _forward(x, theta, gamma1, gamma2, q_w, q_b, k_w, k_b, v_w, v_b, o_w, o_b, router_w, router_b, sh_w1, sh_b1, sh_w2, sh_b2, re_w1, re_b1, re_w2, re_b2):
            b, s, d = x.shape
            xn = _rmsnorm(x, gamma1)
            q = (xn @ q_w + q_b).reshape(b, s, H, HD).transpose(0, 2, 1, 3)
            k = (xn @ k_w + k_b).reshape(b, s, H, HD).transpose(0, 2, 1, 3)
            v = (xn @ v_w + v_b).reshape(b, s, H, HD).transpose(0, 2, 1, 3)
            q = _rope(q, theta)
            k = _rope(k, theta)
            scale = 1.0 / np.sqrt(HD)
            scores = jnp.einsum('bhqd,bhkd->bhqk', q, k) * scale
            causal = jnp.tril(jnp.ones((s, s), dtype=bool))
            scores = jnp.where(causal, scores, -jnp.inf)
            attn = jax.nn.softmax(scores, axis=-1)
            ctx = jnp.einsum('bhqk,bhkd->bhqd', attn, v)
            ctx = ctx.transpose(0, 2, 1, 3).reshape(b, s, H * HD)
            attn_out = ctx @ o_w + o_b + xn
            an = _rmsnorm(attn_out, gamma2)
            shared = jax.nn.gelu(an @ sh_w1 + sh_b1, approximate=False) @ sh_w2 + sh_b2
            logits = an @ router_w + router_b
            aff = jax.nn.softmax(logits, axis=-1)
            topv, topi = jax.lax.top_k(aff, K_ACT)
            gates = jnp.sum(jax.nn.one_hot(topi, E_R, dtype=aff.dtype) * topv[..., None], axis=-2)
            h = jax.nn.gelu(jnp.einsum('bsd,edh->besh', an, re_w1) + re_b1[None, :, None, :], approximate=False)
            routed = jnp.einsum('bse,besh,ehd->bsd', gates, h, re_w2) + jnp.einsum('bse,ed->bsd', gates, re_b2)
            return shared + routed + an + attn_out
        key = jax.random.key(seed)
        ks = jax.random.split(key, 24)
        s = 0.02
        theta = BASE ** (-jnp.arange(HD // 2, dtype=jnp.float32) * 2.0 / HD)
        inp = {'x': jax.random.normal(ks[0], (B, S, D), jnp.float32), 'positions': jnp.arange(S, dtype=jnp.int32), 'theta': theta, 'gamma1': jnp.ones((D,), jnp.float32), 'gamma2': jnp.ones((D,), jnp.float32), 'q_w': jax.random.normal(ks[1], (D, H * HD), jnp.float32) * s, 'q_b': jnp.zeros((H * HD,), jnp.float32), 'k_w': jax.random.normal(ks[2], (D, H * HD), jnp.float32) * s, 'k_b': jnp.zeros((H * HD,), jnp.float32), 'v_w': jax.random.normal(ks[3], (D, H * HD), jnp.float32) * s, 'v_b': jnp.zeros((H * HD,), jnp.float32), 'o_w': jax.random.normal(ks[4], (H * HD, D), jnp.float32) * s, 'o_b': jnp.zeros((D,), jnp.float32), 'router_w': jax.random.normal(ks[5], (D, E_R), jnp.float32) * s, 'router_b': jnp.zeros((E_R,), jnp.float32), 'sh_w1': jax.random.normal(ks[6], (D, INTER), jnp.float32) * s, 'sh_b1': jnp.zeros((INTER,), jnp.float32), 'sh_w2': jax.random.normal(ks[7], (INTER, D), jnp.float32) * s, 'sh_b2': jnp.zeros((D,), jnp.float32), 're_w1': jax.random.normal(ks[8], (E_R, D, INTER), jnp.float32) * s, 're_b1': jnp.zeros((E_R, INTER), jnp.float32), 're_w2': jax.random.normal(ks[9], (E_R, INTER, D), jnp.float32) * s, 're_b2': jnp.zeros((E_R, D), jnp.float32)}
        return inp
    _L0_ffn_in = _L0_ffn_setup()
    _L0_c = _w((lambda *s: np.random.randn(*s).astype(np.float32) * 0.05)(8, 128))
    _L0_wmod = _w((lambda *s: np.random.randn(*s).astype(np.float32) * 0.05)(128, 6 * 128) * 128 ** (-0.5))
    _d = {'L0_attn_x': _L0_attn_in['x'], 'L0_attn_Wqkv': _L0_attn_in['Wqkv'], 'L0_attn_bqkv': _L0_attn_in['bqkv'], 'L0_attn_Wout': _L0_attn_in['Wout'], 'L0_attn_bout': _L0_attn_in['bout'], 'L0_attn_omega': _L0_attn_in['omega'], 'L0_attn_quad_nodes': _L0_attn_in['quad_nodes'], 'L0_attn_quad_weights': _L0_attn_in['quad_weights'], 'L0_ffn_positions': _L0_ffn_in['positions'], 'L0_ffn_theta': _L0_ffn_in['theta'], 'L0_ffn_gamma1': _L0_ffn_in['gamma1'], 'L0_ffn_gamma2': _L0_ffn_in['gamma2'], 'L0_ffn_q_w': _L0_ffn_in['q_w'], 'L0_ffn_q_b': _L0_ffn_in['q_b'], 'L0_ffn_k_w': _L0_ffn_in['k_w'], 'L0_ffn_k_b': _L0_ffn_in['k_b'], 'L0_ffn_v_w': _L0_ffn_in['v_w'], 'L0_ffn_v_b': _L0_ffn_in['v_b'], 'L0_ffn_o_w': _L0_ffn_in['o_w'], 'L0_ffn_o_b': _L0_ffn_in['o_b'], 'L0_ffn_router_w': _L0_ffn_in['router_w'], 'L0_ffn_router_b': _L0_ffn_in['router_b'], 'L0_ffn_sh_w1': _L0_ffn_in['sh_w1'], 'L0_ffn_sh_b1': _L0_ffn_in['sh_b1'], 'L0_ffn_sh_w2': _L0_ffn_in['sh_w2'], 'L0_ffn_sh_b2': _L0_ffn_in['sh_b2'], 'L0_ffn_re_w1': _L0_ffn_in['re_w1'], 'L0_ffn_re_b1': _L0_ffn_in['re_b1'], 'L0_ffn_re_w2': _L0_ffn_in['re_w2'], 'L0_ffn_re_b2': _L0_ffn_in['re_b2'], 'L0_c': _L0_c, 'L0_wmod': _L0_wmod}
    _x0 = _d['L0_attn_x']
    _d['L0_attn_x'] = jax.random.normal(jax.random.fold_in(jax.random.key(seed), 1), (8, 512, 128), dtype=_x0.dtype)
    del _x0
    return _d

def reference(L0_attn_x, L0_attn_Wqkv, L0_attn_bqkv, L0_attn_Wout, L0_attn_bout, L0_attn_omega, L0_attn_quad_nodes, L0_attn_quad_weights, L0_ffn_positions, L0_ffn_theta, L0_ffn_gamma1, L0_ffn_gamma2, L0_ffn_q_w, L0_ffn_q_b, L0_ffn_k_w, L0_ffn_k_b, L0_ffn_v_w, L0_ffn_v_b, L0_ffn_o_w, L0_ffn_o_b, L0_ffn_router_w, L0_ffn_router_b, L0_ffn_sh_w1, L0_ffn_sh_b1, L0_ffn_sh_w2, L0_ffn_sh_b2, L0_ffn_re_w1, L0_ffn_re_b1, L0_ffn_re_w2, L0_ffn_re_b2, L0_c, L0_wmod):

    def _L0_attn_ref(x, Wqkv, bqkv, Wout, bout, omega, quad_nodes, quad_weights):
        import jax, jax.numpy as jnp
        import numpy as np
        EMBED = 128
        HEADS = 16
        HD = EMBED // HEADS
        M = 32
        R = 2
        EPS = 1e-06
        C_CONST = 2.0 + EPS
        CHUNK = 64

        def _features(x, omega, quad_nodes, quad_weights):
            B, H, T, D = x.shape
            xn = x / jnp.maximum(jnp.linalg.norm(x, axis=-1, keepdims=True), 1e-12)
            proj = jnp.einsum('bhtd,rhdm->rbhtm', xn, omega)
            s = quad_nodes[:, None, None, None, None]
            sqrt_2s = jnp.sqrt(2.0 * jnp.maximum(s, 0.0))
            arg = jnp.clip(proj * sqrt_2s - s, -20.0, 20.0)
            feat = jnp.exp(arg) / np.sqrt(M).astype(np.float32)
            feat = feat * jnp.sqrt(jnp.maximum(quad_weights, 0.0))[:, None, None, None, None]
            return jnp.transpose(feat, (1, 2, 3, 0, 4)).reshape(B, H, T, R * M)
        B, T, C = x.shape
        qkv = x @ Wqkv + bqkv
        q, k, v = jnp.split(qkv, 3, axis=-1)
        resh = lambda t: t.reshape(B, T, HEADS, HD).transpose(0, 2, 1, 3)
        q, k, v = (resh(q), resh(k), resh(v))
        qf = _features(q, omega, quad_nodes, quad_weights)
        kf = _features(k, omega, quad_nodes, quad_weights)
        Fd = R * M
        nc = T // CHUNK
        to_chunks = lambda t, last: t.reshape(B, HEADS, nc, CHUNK, last).transpose(2, 0, 1, 3, 4)
        qc = to_chunks(qf, Fd)
        kc = to_chunks(kf, Fd)
        vc = to_chunks(v, HD)

        def step(carry, inp):
            kv_state, k_state = carry
            q_ch, k_ch, v_ch = inp
            kv_prod = jnp.einsum('bhtf,bhtd->bhtfd', k_ch, v_ch)
            kv_cur = jnp.cumsum(kv_prod, axis=2) + kv_state[:, :, None]
            k_cur = jnp.cumsum(k_ch, axis=2) + k_state[:, :, None]
            ctx = jnp.einsum('bhtf,bhtfd->bhtd', q_ch, kv_cur)
            den = jnp.maximum(jnp.einsum('bhtf,bhtf->bht', q_ch, k_cur), 1e-06)
            out_ch = ctx / den[..., None]
            return ((kv_cur[:, :, -1], k_cur[:, :, -1]), out_ch)
        init = (jnp.zeros((B, HEADS, Fd, HD), jnp.float32), jnp.zeros((B, HEADS, Fd), jnp.float32))
        _, outs = jax.lax.scan(step, init, (qc, kc, vc))
        out = outs.transpose(1, 2, 0, 3, 4).reshape(B, HEADS, T, HD)
        out = out.transpose(0, 2, 1, 3).reshape(B, T, C)
        return out @ Wout + bout

    def _L0_ffn_ref(x, positions, theta, gamma1, gamma2, q_w, q_b, k_w, k_b, v_w, v_b, o_w, o_b, router_w, router_b, sh_w1, sh_b1, sh_w2, sh_b2, re_w1, re_b1, re_w2, re_b2):
        import jax, jax.numpy as jnp
        import numpy as np
        B, S, D = (2, 128, 128)
        H, HD = (16, 64)
        E_R = 31
        K_ACT = 3
        INTER = 128
        EPS = 1e-05
        BASE = 10000.0

        def _rmsnorm(x, gamma):
            rms = jnp.sqrt(jnp.mean(x * x, axis=-1, keepdims=True) + EPS)
            return x / rms * gamma

        def _rope(x, theta):
            seq = x.shape[2]
            angles = jnp.arange(seq, dtype=theta.dtype)[:, None] * theta
            cos = jnp.cos(angles)[None, None]
            sin = jnp.sin(angles)[None, None]
            x1, x2 = (x[..., 0::2], x[..., 1::2])
            return jnp.concatenate([x1 * cos - x2 * sin, x1 * sin + x2 * cos], axis=-1)

        def _forward(x, theta, gamma1, gamma2, q_w, q_b, k_w, k_b, v_w, v_b, o_w, o_b, router_w, router_b, sh_w1, sh_b1, sh_w2, sh_b2, re_w1, re_b1, re_w2, re_b2):
            b, s, d = x.shape
            xn = _rmsnorm(x, gamma1)
            q = (xn @ q_w + q_b).reshape(b, s, H, HD).transpose(0, 2, 1, 3)
            k = (xn @ k_w + k_b).reshape(b, s, H, HD).transpose(0, 2, 1, 3)
            v = (xn @ v_w + v_b).reshape(b, s, H, HD).transpose(0, 2, 1, 3)
            q = _rope(q, theta)
            k = _rope(k, theta)
            scale = 1.0 / np.sqrt(HD)
            scores = jnp.einsum('bhqd,bhkd->bhqk', q, k) * scale
            causal = jnp.tril(jnp.ones((s, s), dtype=bool))
            scores = jnp.where(causal, scores, -jnp.inf)
            attn = jax.nn.softmax(scores, axis=-1)
            ctx = jnp.einsum('bhqk,bhkd->bhqd', attn, v)
            ctx = ctx.transpose(0, 2, 1, 3).reshape(b, s, H * HD)
            attn_out = ctx @ o_w + o_b + xn
            an = _rmsnorm(attn_out, gamma2)
            shared = jax.nn.gelu(an @ sh_w1 + sh_b1, approximate=False) @ sh_w2 + sh_b2
            logits = an @ router_w + router_b
            aff = jax.nn.softmax(logits, axis=-1)
            topv, topi = jax.lax.top_k(aff, K_ACT)
            gates = jnp.sum(jax.nn.one_hot(topi, E_R, dtype=aff.dtype) * topv[..., None], axis=-2)
            h = jax.nn.gelu(jnp.einsum('bsd,edh->besh', an, re_w1) + re_b1[None, :, None, :], approximate=False)
            routed = jnp.einsum('bse,besh,ehd->bsd', gates, h, re_w2) + jnp.einsum('bse,ed->bsd', gates, re_b2)
            return shared + routed + an + attn_out
        del positions
        return _forward(x, theta, gamma1, gamma2, q_w, q_b, k_w, k_b, v_w, v_b, o_w, o_b, router_w, router_b, sh_w1, sh_b1, sh_w2, sh_b2, re_w1, re_b1, re_w2, re_b2)
    x = L0_attn_x
    mod = (_silu(L0_c) @ L0_wmod).reshape(L0_c.shape[0], 6, 1, -1)
    sa, ca, ga, sb, cb, gb = (mod[:, 0], mod[:, 1], mod[:, 2], mod[:, 3], mod[:, 4], mod[:, 5])
    ga = (2 * (ga >= 0) - 1) * jnp.maximum(jnp.abs(ga), 0.25)
    gb = (2 * (gb >= 0) - 1) * jnp.maximum(jnp.abs(gb), 0.25)
    h = _layernorm(x, axis=-1) * (1 + ca) + sa
    x = x + ga * _L0_attn_ref(h, L0_attn_Wqkv, L0_attn_bqkv, L0_attn_Wout, L0_attn_bout, L0_attn_omega, L0_attn_quad_nodes, L0_attn_quad_weights)
    h = _layernorm(x, axis=-1) * (1 + cb) + sb
    x = x + gb * _L0_ffn_ref(h, L0_ffn_positions, L0_ffn_theta, L0_ffn_gamma1, L0_ffn_gamma2, L0_ffn_q_w, L0_ffn_q_b, L0_ffn_k_w, L0_ffn_k_b, L0_ffn_v_w, L0_ffn_v_b, L0_ffn_o_w, L0_ffn_o_b, L0_ffn_router_w, L0_ffn_router_b, L0_ffn_sh_w1, L0_ffn_sh_b1, L0_ffn_sh_w2, L0_ffn_sh_b2, L0_ffn_re_w1, L0_ffn_re_b1, L0_ffn_re_w2, L0_ffn_re_b2)
    return x

_drawn_inputs = setup_inputs


def setup_inputs(seed=0):
    import zlib

    import numpy as np

    out = dict(_drawn_inputs(seed))
    spreads = {'L0_attn_bqkv': (0.0, 0.8),
     'L0_attn_bout': (0.0, 0.304),
     'L0_ffn_gamma1': (1.0, 0.2),
     'L0_ffn_gamma2': (1.0, 0.2),
     'L0_ffn_q_b': (0.0, 0.8),
     'L0_ffn_k_b': (0.0, 0.8),
     'L0_ffn_v_b': (0.0, 0.296),
     'L0_ffn_o_b': (0.0, 0.1),
     'L0_ffn_router_b': (0.0, 0.8),
     'L0_ffn_sh_b1': (0.0, 0.8),
     'L0_ffn_sh_b2': (0.0, 0.343),
     'L0_ffn_re_b1': (0.0, 0.8),
     'L0_ffn_re_b2': (0.0, 0.8)}
    factors = {'L0_attn_Wqkv': 8.0,
     'L0_attn_Wout': 8.0,
     'L0_attn_omega': 8.0,
     'L0_attn_quad_nodes': 8.0,
     'L0_attn_quad_weights': 8.0,
     'L0_ffn_theta': 8.0,
     'L0_ffn_q_w': 8.0,
     'L0_ffn_k_w': 8.0,
     'L0_ffn_v_w': 7.299,
     'L0_ffn_router_w': 8.0,
     'L0_ffn_sh_w1': 8.0,
     'L0_ffn_sh_w2': 8.0,
     'L0_ffn_re_w1': 8.0,
     'L0_ffn_re_w2': 8.0}
    for name, (base, spread) in spreads.items():
        noise = np.random.default_rng([zlib.crc32(name.encode()), seed]).standard_normal(out[name].shape)
        drawn = base * np.exp(spread * noise) if base else spread * noise
        out[name] = jnp.asarray(drawn.astype(out[name].dtype))
    for name, factor in factors.items():
        out[name] = (out[name] * factor).astype(out[name].dtype)
    return out
```

```python
from contextlib import ExitStack

import numpy as np

import concourse.bass as bass
from concourse import mybir

F32 = mybir.dt.float32
BF16 = mybir.dt.bfloat16
U32 = mybir.dt.uint32
ALU = mybir.AluOpType
ACT = mybir.ActivationFunctionType
AX = mybir.AxisListType.X

P = 128
D = 128
NB, SEQ = 8, 512
TB = SEQ // P
NT = NB * TB
AH, AHD = 16, 8
FEAT = 64
APAIR = AH // 2
HALF = 2
HP = APAIR // HALF
HH = AH // HALF
PAIR = 8
UNITS = NB * PAIR
NE = 32
TOPK = 3
CLIP = 20.0
EXP_LOW = float(np.exp(-CLIP))
BIG = 1e30

C_ID, C_MASKA, C_MASKB, C_IOTA, C_EIOTA, C_KEEP, C_SIGN, C_END = np.cumsum(
    [0, P, P, SEQ, SEQ, NE, NT, 1]).tolist()
R_BQKV, R_BOUT, R_G1, R_G2, R_OB, R_RB, R_END = np.cumsum([0, 3 * D, D, D, D, D, NE]).tolist()
K_NODE, K_WEIGHT, K_THETA, K_QKV, K_B1, K_END = np.cumsum([0, 1, 1, 1, PAIR * 5, NE]).tolist()

SU_COS, SU_NODE, SU_STEPS = 18, 19, 24
ROUND = 12582912.0
_HI = 6.28125
_MID = float(np.uint32(int(np.float32(2 * np.pi - _HI).view(np.uint32)) & 0xFFFFF000).view(np.float32))
TWO_PI = (_HI, _MID, float(np.float32(2 * np.pi - _HI - _MID)))
PI_UNDER = 3.1415925



def one(t, i):
    return t[:, bass.ds(i, 1), :].squeeze(1)


def wait_apart(eng, sem, value):
    eng.wait_ge(sem, value)
    eng.nop(nofuse=True)


def build_block(nc, a, out):
    ctx = ExitStack()
    with ctx:
        def sb(name, shape, dt=F32, where=ctx):
            return where.enter_context(nc.sbuf_tensor(name, shape, dt))

        def sem(name):
            return ctx.enter_context(nc.semaphore(name))

        bank = [ctx.enter_context(nc.psum_tensor(f"bank{i}", [P, 512], F32)) for i in range(8)]

        x_all = sb("x_all", [P, NT, D])
        mod_all = sb("mod_all", [P, NB, 6, D])
        slab_q = sb("slab_q", [P, NT * P])
        slab_k = sb("slab_k", [P, NT * P])
        slab_v = sb("slab_v", [P, NT * D])
        slab_x = sb("slab_x", [P, NT * P])
        ao_all = sb("ao_all", [P, NT, D])
        const = sb("const", [P, C_END])
        rows = sb("rows", [P, R_END])
        cols = sb("cols", [P, K_END])
        wqkvb = sb("wqkvb", [P, PAIR, 5, P])
        wo = sb("wo", [P, PAIR, D])
        wa_qkv = sb("wa_qkv", [P, 3 * D])
        wa_out = sb("wa_out", [P, D])
        omega_bd = sb("omega_bd", [P, APAIR * P])
        rope = sb("rope", [P, 4, SEQ])
        sel_src = sb("sel_src", [3 * NE, NE])
        ident_bf = sb("ident_bf", [P, P], BF16)
        zeros_bf = sb("zeros_bf", [P, SEQ], BF16)
        wr = sb("wr", [P, NE - 1])
        b2 = sb("b2", [NE, D])
        small = sb("small", [P, 8])

        ident = const[:, C_ID:C_ID + P]
        mask_a = const[:, C_MASKA:C_MASKA + P]
        mask_b = const[:, C_MASKB:C_MASKB + SEQ]
        root2s, neg_s, wfeat, eps_col = (small[:, i:i + 1] for i in range(4))
        top = small[:, 4:5]
        v_all = slab_v[:].rearrange("p (n d) -> p n d", d=D)
        pt = slab_v[:].rearrange("p (h k q) -> p h k q", h=2, k=TB)
        gates3_all = slab_v[0:3 * NE, 0:NT * P // 2].bitcast(BF16)
        sel_all = slab_v[0:3 * NE, NT * P // 2:NT * P].bitcast(BF16).rearrange("p (e m) -> p e m", e=NE)
        w1_all = slab_q
        w2_all = slab_k[:].rearrange("p (e d) -> p e d", e=NE)

        wa = ExitStack()
        c_t = sb("c_t", [P, NB], where=wa)
        c_e = sb("c_e", [P, NB], where=wa)
        sil = sb("sil", [P, NB], where=wa)
        wmod = sb("wmod", [P, 6 * D], where=wa)
        angles = sb("angles", [P, 2, SEQ], where=wa)
        ang, turns = angles[:, 0], angles[:, 1]
        stats = sb("stats", [P, TB, 6], where=wa)
        mv = sb("mv", [P, TB, 2], where=wa)
        std = sb("std", [P, TB], where=wa)
        ms = sb("ms", [P, TB], where=wa)
        hrow = sb("hrow", [P, TB, D], where=wa)
        gabout = sb("gabout", [P, D], where=wa)
        h_t = sb("h_t", [P, SEQ], where=wa)
        qkv = sb("qkv", [P, TB, 3 * D], where=wa)
        sq_qkn = sb("sq_qkn", [P, 2, TB, 2 * D], where=wa)
        sq, qkn = sq_qkn[:, 0], sq_qkn[:, 1]
        ss = sb("ss", [P, TB, 2 * AH], where=wa)
        qf = qkv[:].rearrange("p t d -> p (t d)")[:, 0:HALF * HP * P].rearrange("p (j c q) -> p j c q", j=HALF, c=HP)
        kf = sb("kf", [P, HALF, HP, P], where=wa)
        kf_tok = angles[:].rearrange("p j (c f) -> p j c f", c=HP)
        v_one = sb("v_one", [P, AH, 32], where=wa)
        att_w = sq_qkn.rearrange("p j t d -> p (j t d)").rearrange("p (j r c q) -> p j r c q", j=HALF, r=2, c=HP)
        state = sb("state", [P, APAIR, 32], where=wa)
        o_t = sb("o_t", [P, 2 * P], where=wa)
        den = sb("den", [P, HH], where=wa)
        att = sb("att", [P, D], where=wa)
        att_t = sb("att_t", [P, P], where=wa)
        proj_tmp = sb("proj_tmp", [P, D], where=wa)
        xn_tok = hrow
        wa.close()
        wb = ExitStack()
        x_st = slab_k[:, 0:2 * SEQ].rearrange("p (j q) -> p j q", j=2)
        w_st = slab_k[:, 2 * SEQ:2 * SEQ + 10 * P].rearrange("p (j k d) -> p j k d", j=2, k=5)
        q_rot = sb("q_rot", [P, 2, SEQ], where=wb)
        k_rot = sb("k_rot", [P, 2, SEQ], where=wb)
        part = sb("part", [P, 4, SEQ], where=wb)
        prob = sb("prob", [P, 4, SEQ], where=wb)
        low = sb("low", [P, 4], where=wb)
        rsum = sb("rsum", [P, 4], where=wb)
        rinv = sb("rinv", [P, 4], where=wb)
        v_sb = sb("v_sb", [P, 2, TB, P], where=wb)
        ctx_t = sb("ctx_t", [P, SEQ], where=wb)
        wb.close()
        wt = ExitStack()
        t_ms = sb("t_ms", [P, TB], where=wt)
        t_tmp = sb("t_tmp", [P, TB, D], where=wt)
        an = sb("an", [P, TB, D], where=wt)
        an_t = sb("an_t", [P, SEQ], where=wt)
        logit = sb("logit", [P, TB, NE - 1], where=wt)
        aff = sb("aff", [P, TB, NE - 1], where=wt)
        red = sb("red", [P, TB], where=wt)
        top8 = sb("top8", [P, TB, 8], where=wt)
        idx8 = sb("idx8", [P, TB, 8], U32, where=wt)
        idxf = sb("idxf", [P, TB, TOPK], where=wt)
        onehot = sb("onehot", [P, TB, TOPK, NE - 1], where=wt)
        chosen = sb("chosen", [P, TB, NE - 1], where=wt)
        gates = sb("gates", [P, TB, NE], where=wt)
        rest = sb("rest", [P, TB, NE], where=wt)
        gates3 = sb("gates3", [P, TB, 3 * NE], BF16, where=wt)
        gates_t = sb("gates_t", [NE, SEQ], where=wt)
        w1_st = sb("w1_st", [P, 2, P], where=wt)
        hid = sb("hid", [P, 2, SEQ], where=wt)
        hid_g = sb("hid_g", [P, 2, SEQ], where=wt)
        y_sb = sb("y_sb", [P, 2, TB, D], where=wt)
        wt.close()

        ld_const, ld_mod, ld_x, ld_wa, ld_wb, ld_w1, ld_w2 = (
            sem(n) for n in ("ld_const", "ld_mod", "ld_x", "ld_wa", "ld_wb", "ld_w1", "ld_w2"))
        su_exp, su_dve, su_mod_mm, su_mod_ev, su_sin, su_pool, su_modfix = (
            sem(n) for n in ("su_exp", "su_dve", "su_mod_mm", "su_mod_ev", "su_sin", "su_pool", "su_modfix"))
        a_done, b_done, t_done_all = sem("a_done"), sem("b_done"), sem("t_done_all")

        block = ctx.enter_context(nc.Block())

        def phase_end(eng, s):
            eng.drain().then_inc(s, 1)

        a1_dve, ln_var, ln_std, h_ready, hT_done, hT_ready, qkv_done, qkv_ready, ss_ready, nrm_ready, \
            qkn_ready, qknT_done, qknT_saved, x_plus, v_saved = (
                sem("a1_" + n) for n in ("dve", "ln_var", "ln_std", "h_ready", "hT_done", "hT_ready",
                                         "qkv_done", "qkv_ready", "ss_ready", "nrm_ready", "qkn_ready",
                                         "qknT_done", "qknT_saved", "x_plus", "v_saved"))
        A1D = 6
        v_set, feat_done, min_done, exp_done, kf_ready, qw_ready, kT_done, kT_ready, aw_done, aw_ready, oT_done, \
            oT_ready, st_done, st_link, st_ready, o2_done, att_link, att_ready, attT_done, attT_ready, \
            wo_done, x1_link, x1_done = (
                sem("a2_" + n) for n in ("v_set", "feat_done", "min_done", "exp_done", "kf_ready", "qw_ready", "kT_done",
                                         "kT_ready", "aw_done", "aw_ready", "oT_done", "oT_ready", "st_done",
                                         "st_link", "st_ready", "o2_done", "att_link", "att_ready",
                                         "attT_done", "attT_ready", "wo_done", "x1_link", "x1_done"))
        a3_dve, a3_var, a3_std, a3_ms, a3_rms, xn_ready, xnT_done, xnT_saved, ao_set = (
            sem("a3_" + n) for n in ("dve", "var", "std", "ms", "rms", "xn_ready", "xnT_done", "xnT_saved",
                                     "ao_set"))
        a3_inv, nrm_inv = sem("a3_inv"), sem("a1_nrm_inv")
        A3D = 5
        st_in = [sem("b_staged0"), sem("b_staged1")]
        q_done, k_done, v_done, q_part, k_part, q_ready, k_ready, v_ready = (
            sem("b_" + n) for n in ("q_done", "k_done", "v_done", "q_part", "k_part", "q_ready", "k_ready",
                                    "v_ready"))
        s_done, s_min, p_exp, p_inv, p_ready, pT_done, pT_ready, c_done, c_ready, o_done, o_added = (
            sem("b_" + n) for n in ("s_done", "s_min", "p_exp", "p_inv", "p_ready", "pT_done", "pT_ready",
                                    "c_done", "c_ready", "o_done", "o_added"))
        t_dve, t_msd, t_rms, an_ready, anT_done, anT_ready, anT_saved, lg_done, lg_ready, ex_ready, g_ready, \
            gT_done, gT_ready, g3_ready, g3T_done, g3T_saved, b2_done = (
                sem("t_" + n) for n in ("dve", "ms", "rms", "an_ready", "anT_done", "anT_ready", "anT_saved",
                                        "lg_done", "lg_ready", "ex_ready", "g_ready", "gT_done", "gT_ready",
                                        "g3_ready", "g3T_done", "g3T_saved", "b2_done"))
        TD = 19
        base_link = sem("t_base_link")
        w1_in = [sem("c_w1_0"), sem("c_w1_1")]
        y_out = [sem("c_stored0"), sem("c_stored1")]
        hd_done, gb_done, gelu_done, hg_ready, y_part, y_done, y_link, y_ready = (
            sem("c_" + n) for n in ("hid_done", "gate_done", "gelu_done", "hg_ready", "y_part", "y_done",
                                    "y_link", "y_ready"))

        x_dram = a["x"].rearrange("b (t p) d -> p (b t) d", p=P)
        out_dram = out.rearrange("b (t p) d -> p (b t) d", p=P)

        @block.sync
        def _(sp):
            sp.dma_start(c_t[:], a["c_t"]).then_inc(ld_mod, 16)
            sp.dma_start(wmod[:], a["wmod"]).then_inc(ld_mod, 16)
            sp.dma_start(const[:], a["const"]).then_inc(ld_const, 16)
            sp.dma_start(rows[:], a["rows"]).then_inc(ld_const, 16)
            sp.dma_start(cols[:], a["cols"]).then_inc(ld_const, 16)
            sp.dma_start(sel_src[:], a["sel"]).then_inc(ld_const, 16)
            for h in range(2):
                sp.dma_start(x_all[:, h * NT // 2:(h + 1) * NT // 2, :],
                             x_dram[:, h * NT // 2:(h + 1) * NT // 2, :]).then_inc(ld_x, 16)
            sp.dma_start(wa_qkv[:], a["wa_qkv"]).then_inc(ld_wa, 16)
            sp.dma_start(wa_out[:], a["wa_out"]).then_inc(ld_wa, 16)
            sp.dma_start(omega_bd[:], a["omega_bd"]).then_inc(ld_wa, 16)
            sp.dma_start(wqkvb[:], a["wqkvb"]).then_inc(ld_wb, 16)
            sp.dma_start(wo[:], a["wo"]).then_inc(ld_wb, 16)
            sp.dma_start(wr[:], a["wr"]).then_inc(ld_wb, 16)
            sp.dma_start(b2[:], a["b2"]).then_inc(ld_wb, 16)
            sp.wait_ge(ld_wb, 64)
            phase_end(sp, a_done)
            sp.wait_ge(a_done, 5)
            sp.dma_start(w1_all[:], a["w1"]).then_inc(ld_w1, 16)
            def stage(u, par):
                sp.dma_start(x_st[:, par, :], slab_x[:, bass.ds(u // PAIR * SEQ, SEQ)]).then_inc(st_in[par], 16)
                sp.dma_start(w_st[:, par], wqkvb[:, bass.ds(u % PAIR, 1)].squeeze(1)).then_inc(st_in[par], 16)

            stage(0, 0)
            stage(1, 1)
            with sp.Fori(1, UNITS // 2) as i:
                for par in range(2):
                    sp.wait_ge(v_done, i * 2 + (par - 1))
                    stage(i * 2 + par, par)
            phase_end(sp, b_done)
            sp.wait_ge(b_done, 5)
            sp.dma_start(slab_k[:], a["w2"]).then_inc(ld_w2, 16)
            sp.wait_ge(t_done_all, 4)
            sp.wait_ge(ld_w1, 16)
            for e in range(2):
                sp.dma_start(w1_st[:, e, :], w1_all[:, e * P:(e + 1) * P]).then_inc(w1_in[e], 16)
            with sp.Fori(0, NB // 2) as bp:
                with sp.Fori(1, NE // 2) as e2:
                    for ee in range(2):
                        sp.wait_ge(hd_done, bp * (2 * NE) + e2 * 4 + (ee * 2 - 2))
                        sp.dma_start(w1_st[:, ee, :], w1_all[:, bass.ds((e2 * 2 + ee) * P, P)]).then_inc(w1_in[ee], 16)
                for ee in range(2):
                    sp.wait_ge(hd_done, bp * (2 * NE) + (2 * NE - 2 + ee * 2))
                    sp.dma_start(w1_st[:, ee, :], w1_all[:, ee * P:(ee + 1) * P]).then_inc(w1_in[ee], 16)
                for bb in range(2):
                    sp.wait_ge(y_ready, bp * 2 + (bb + 1))
                    sp.dma_start(out_dram[:, bass.ds(bp * (2 * TB) + bb * TB, TB), :], y_sb[:, bb]).then_inc(y_out[bb], 16)
            for bb in range(2):
                sp.wait_ge(y_out[bb], 16 * (NB // 2) + 16)
            for ee in range(2):
                sp.wait_ge(w1_in[ee], 16 * (NB // 2 * (NE // 2) + 1))

        @block.gpsimd
        def _(pool):
            nc.gpsimd.memset(state[:], 0.0).then_inc(st_ready, 2)
            nc.gpsimd.memset(v_one[:], 0.0).then_inc(su_pool, 1)
            pool.wait_ge(su_pool, 1)
            nc.gpsimd.memset(v_one[:, :, AHD:AHD + 1], 1.0).then_inc(su_pool, 1)
            nc.gpsimd.memset(zeros_bf[:], 0.0).then_inc(su_pool, 1)
            nc.gpsimd.memset(eps_col, 1e-5).then_inc(su_pool, 1)
            pool.wait_ge(ld_x, 32)
            pool.wait_ge(ld_const, 64)
            pool.wait_ge(su_modfix, 1)
            with pool.Fori(0, NB) as g:
                pool.wait_ge(h_ready, g + 1)
                ga = mod_all[:, bass.ds(g, 1), 2, :].squeeze(1)
                nc.gpsimd.tensor_tensor(gabout[:], ga, rows[:, R_BOUT:R_BOUT + D], ALU.mult).then_inc(x_plus, 1)
                pool.wait_ge(x_plus, g * 2 + 1)
                xg = x_all[:, bass.ds(g * TB, TB), :]
                nc.gpsimd.tensor_tensor(xg, xg, gabout[:].unsqueeze(1).to_broadcast([P, TB, D]), ALU.add).then_inc(x_plus, 1)
                pool.wait_ge(qkv_ready, g + 1)
                nc.gpsimd.tensor_copy(v_all[:, bass.ds(g * TB, TB), :], qkv[:, :, 2 * D:3 * D]).then_inc(v_saved, 1)

            def set_v(i):
                vt = v_all[:, bass.ds(i, 1), :].rearrange("p o (h d) -> p (o h) d", h=AH)
                nc.gpsimd.tensor_copy(v_one[:, :, 0:AHD], vt).then_inc(v_set, 1)

            def weigh_q(u, j):
                wait_apart(pool, exp_done, 2 * u + 1)
                nc.gpsimd.tensor_scalar(qf[:, j], qf[:, j], EXP_LOW, wfeat, ALU.max, ALU.mult).then_inc(qw_ready, 1)

            pool.wait_ge(v_saved, NB)
            pool.wait_ge(su_dve, SU_STEPS)
            set_v(0)
            weigh_q(0, 0)
            weigh_q(1, 1)
            with pool.Fori(1, NT) as i:
                weigh_q(i * HALF, 0)
                pool.wait_ge(st_done, i * 2)
                set_v(i)
                weigh_q(i * HALF + 1, 1)
            with pool.Fori(0, NB) as g:
                pool.wait_ge(xn_ready, g + 1)
                nc.gpsimd.tensor_tensor(ao_all[:, bass.ds(g * TB, TB), :], xn_tok[:],
                                        rows[:, R_OB:R_OB + D].unsqueeze(1).to_broadcast([P, TB, D]),
                                        ALU.add).then_inc(ao_set, 1)
            phase_end(pool, a_done)
            pool.wait_ge(a_done, 5)
            def add_parts(which, u, par):
                pool.wait_ge((q_part, k_part)[which], u + 1 + which)
                nc.gpsimd.tensor_tensor((q_rot, k_rot)[which][:, par, :], part[:, 2 * which, :],
                                        part[:, 2 * which + 1, :], ALU.add).then_inc((q_ready, k_ready)[which], 1)

            def scale(u, t):
                wait_apart(pool, p_inv, 4 * u + t + 1)
                for h in range(2):
                    s = t % 2 * 2 + h
                    pr = prob[:, s, 0:(t + 1) * P]
                    nc.gpsimd.tensor_scalar(pr, pr, rinv[:, s:s + 1], None, ALU.mult).then_inc(p_ready, 1)

            def unit(u, par, first, last):
                if not first:
                    scale(u - 1, 3)
                if not last:
                    add_parts(0, u + 1, 1 - par)
                scale(u, 0)
                if not last:
                    add_parts(1, u + 1, 1 - par)
                scale(u, 1)
                scale(u, 2)

            add_parts(0, 0, 0)
            add_parts(1, 0, 0)
            unit(0, 0, True, False)
            with pool.Fori(0, UNITS // 2 - 1) as i:
                unit(i * 2 + 1, 1, False, False)
                unit(i * 2 + 2, 0, False, False)
            unit(UNITS - 1, 1, False, True)
            scale(UNITS - 1, 3)
            phase_end(pool, b_done)
            pool.wait_ge(b_done, 5)
            with pool.Fori(0, NB) as b:
                pool.wait_ge(anT_ready, b + 1)
                nc.gpsimd.tensor_copy(slab_x[:, bass.ds(b * SEQ, SEQ)], an_t[:]).then_inc(anT_saved, 1)
            phase_end(pool, t_done_all)

        @block.scalar
        def _(act):
            act.wait_ge(ld_mod, 32)
            nc.scalar.activation(c_e[:], c_t[:], ACT.Exp, scale=-1.0).then_inc(su_exp, 1)
            for n in range(2 * NB):
                b, half = divmod(n, 2)
                act.wait_ge(su_mod_mm, n + 1)
                nc.scalar.activation(mod_all[:, b, 3 * half:3 * half + 3, :],
                                     bank[n % 8][:, 0:3 * D].rearrange("p (k d) -> p k d", k=3),
                                     ACT.Copy).then_inc(su_mod_ev, 1)
            act.wait_ge(su_dve, SU_COS)
            nc.scalar.activation(rope[:, 2, :], rope[:, 2, :], ACT.Sin).then_inc(su_sin, 1)
            nc.scalar.activation(rope[:, 3, :], rope[:, 3, :], ACT.Sin).then_inc(su_sin, 1)
            act.wait_ge(su_dve, SU_NODE)
            nc.scalar.activation(root2s, root2s, ACT.Sqrt).then_inc(su_sin, 1)
            act.wait_ge(su_pool, 4)
            with act.Fori(0, NB) as g:
                act.wait_ge(ln_var, g + 1)
                nc.scalar.activation(std[:], mv[:, :, 1], ACT.Sqrt, bias=eps_col).then_inc(ln_std, 1)
                act.wait_ge(hT_done, g + 1)
                nc.scalar.activation(h_t[:], bank[0][:], ACT.Copy).then_inc(hT_ready, 1)
                act.wait_ge(ss_ready, g + 1)
                nc.scalar.activation(ss[:], ss[:], ACT.Sqrt).then_inc(nrm_ready, 1)
                act.wait_ge(qknT_done, g * 2 + 1)
                nc.scalar.activation(slab_q[:, bass.ds(g * SEQ, SEQ)], bank[5][:], ACT.Copy).then_inc(qknT_saved, 1)
                act.wait_ge(qknT_done, g * 2 + 2)
                nc.scalar.activation(slab_k[:, bass.ds(g * SEQ, SEQ)], bank[6][:], ACT.Copy).then_inc(qknT_saved, 1)

            def exps(u, j):
                for n, f in enumerate((qf, kf)):
                    act.wait_ge(min_done, 2 * u + (n + 1))
                    nc.scalar.activation(f[:, j], f[:, j], ACT.Exp, bias=neg_s).then_inc(exp_done, 1)

            def a2_tile(i, first, last):
                for j in range(HALF):
                    u = i * HALF + j
                    act.wait_ge(kT_done, u + 1)
                    nc.scalar.activation(kf_tok[:, j].rearrange("p a b -> p (a b)"), bank[2][:],
                                         ACT.Copy).then_inc(kT_ready, 1)
                    if j == 0 or not last:
                        exps(u + 1, 1 - j)
                    if j == 0 and not first:
                        project(i - 1)

            def project(i):
                act.wait_ge(attT_done, i + 1)
                nc.scalar.activation(att_t[:], bank[6][:, 0:P], ACT.Copy).then_inc(attT_ready, 1)

            act.wait_ge(su_dve, SU_STEPS)
            act.wait_ge(su_sin, 3)
            act.wait_ge(v_saved, NB)
            exps(0, 0)
            a2_tile(0, True, False)
            with act.Fori(1, NT - 1) as i:
                a2_tile(i, False, False)
            a2_tile(NT - 1, False, True)
            project(NT - 1)
            with act.Fori(0, NB) as g:
                act.wait_ge(a3_var, g + 1)
                nc.scalar.activation(std[:], mv[:, :, 1], ACT.Sqrt, bias=eps_col).then_inc(a3_std, 1)
                act.wait_ge(a3_ms, g + 1)
                nc.scalar.activation(ms[:], ms[:], ACT.Sqrt, bias=eps_col).then_inc(a3_rms, 1)
                act.wait_ge(xnT_done, g + 1)
                nc.scalar.activation(slab_x[:, bass.ds(g * SEQ, SEQ)], bank[0][:], ACT.Copy).then_inc(xnT_saved, 1)
            phase_end(act, a_done)
            act.wait_ge(a_done, 5)
            def exp_p(u, t):
                for h in range(2):
                    s = t % 2 * 2 + h
                    act.wait_ge(s_min, 8 * u + 2 * t + h + 3)
                    pr = prob[:, s, 0:(t + 1) * P]
                    nc.scalar.activation(pr, pr, ACT.Exp, bias=low[:, s:s + 1], scale=-1.0,
                                         accum_out=rsum[:, s:s + 1]).then_inc(p_exp, 1)

            def save_pt(u, t):
                for h in range(2):
                    act.wait_ge(pT_done, 8 * u + 2 * t + h + 5)
                    nc.scalar.activation(pt[:, h, 0:t + 1, t * P:(t + 1) * P],
                                         bank[5 + h][:, 0:(t + 1) * P].rearrange("p (k q) -> p k q", q=P),
                                         ACT.Copy).then_inc(pT_ready, 1)

            def save_v(u, par):
                act.wait_ge(v_done, u + 1)
                nc.scalar.activation(v_sb[:, par].rearrange("p a b -> p (a b)"), bank[2][:],
                                     ACT.Copy).then_inc(v_ready, 1)

            def save_ctx(u):
                wait_apart(act, c_done, u + 1)
                vb = cols[:, K_QKV:K_QKV + PAIR * 5].rearrange("p (a k) -> p a k", k=5)[
                    :, bass.ds(u % PAIR, 1), 4]
                nc.scalar.activation(ctx_t[:], bank[7][:], ACT.Identity, bias=vb).then_inc(c_ready, 1)

            def unit(u, par, first, last):
                exp_p(u, 0)
                if not first:
                    save_pt(u - 1, 3)
                exp_p(u, 1)
                if not first:
                    save_ctx(u - 1)
                save_pt(u, 0)
                exp_p(u, 2)
                save_pt(u, 1)
                if not last:
                    save_v(u + 1, 1 - par)
                exp_p(u, 3)
                save_pt(u, 2)

            save_v(0, 0)
            unit(0, 0, True, False)
            with act.Fori(0, UNITS // 2 - 1) as i:
                unit(i * 2 + 1, 1, False, False)
                unit(i * 2 + 2, 0, False, False)
            unit(UNITS - 1, 1, False, True)
            save_pt(UNITS - 1, 3)
            save_ctx(UNITS - 1)
            phase_end(act, b_done)
            act.wait_ge(b_done, 5)
            with act.Fori(0, NB) as b:
                act.wait_ge(t_msd, b + 1)
                nc.scalar.activation(t_ms[:], t_ms[:], ACT.Sqrt, bias=eps_col, scale=1.0 / D).then_inc(t_rms, 1)
                act.wait_ge(anT_done, b + 1)
                nc.scalar.activation(an_t[:], bank[0][:], ACT.Copy).then_inc(anT_ready, 1)
                act.wait_ge(lg_ready, b + 1)
                nc.scalar.activation(logit[:], logit[:], ACT.Exp).then_inc(ex_ready, 1)
                act.wait_ge(gT_done, b + 1)
                nc.scalar.activation(gates_t[:], bank[3][0:NE, :], ACT.Copy).then_inc(gT_ready, 1)
                act.wait_ge(g3T_done, b + 1)
                nc.scalar.activation(gates3_all[:, bass.ds(b * SEQ, SEQ)], bank[4][0:3 * NE, 0:SEQ // 2].bitcast(BF16),
                                     ACT.Copy).then_inc(g3T_saved, 1)
            phase_end(act, t_done_all)
            act.wait_ge(t_done_all, 4)
            with act.Fori(0, NB // 2) as bp:
                with act.Fori(0, NE) as e:
                    for bb in range(2):
                        wait_apart(act, hd_done, bp * (2 * NE) + e * 2 + (bb + 1))
                        nc.scalar.activation(hid[:, bb, :], bank[bb][:], ACT.Gelu,
                                             bias=cols[:, bass.ds(K_B1 + e, 1)]).then_inc(gelu_done, 1)

        @block.tensor
        def _(pe):
            def mm(o, l, r, start=True, stop=True, **kw):
                return nc.tensor.matmul(o, l, r, start=start, stop=stop, **kw)

            pe.wait_ge(su_dve, 3)
            for n in range(2 * NB):
                b, half = divmod(n, 2)
                if n >= 8:
                    pe.wait_ge(su_mod_ev, n - 7)
                mm(bank[n % 8][:, 0:3 * D], sil[:, b:b + 1].to_broadcast([P, P]),
                   wmod[:, 3 * D * half:3 * D * (half + 1)]).then_inc(su_mod_mm, 1)
            pe.wait_ge(su_mod_ev, 2 * NB)
            pe.wait_ge(ld_wa, 48)
            with pe.Fori(0, NB) as g:
                pe.wait_ge(h_ready, g + 1)
                for t in range(TB):
                    m = nc.tensor.transpose(bank[0][:, t * P:(t + 1) * P], hrow[:, t, :], ident)
                m.then_inc(hT_done, 1)
                pe.wait_ge(hT_ready, g + 1)
                for t in range(TB):
                    mm(bank[1 + t][:, 0:3 * D], h_t[:, t * P:(t + 1) * P], wa_qkv[:]).then_inc(qkv_done, 1)
                pe.wait_ge(qkn_ready, g + 1)
                for n in range(2):
                    for t in range(TB):
                        m = nc.tensor.transpose(bank[5 + n][:, t * P:(t + 1) * P], qkn[:, t, n * D:(n + 1) * D], ident)
                    m.then_inc(qknT_done, 1)

            def feats(i, j):
                for n, src in enumerate((slab_q, slab_k)):
                    for c in range(HP):
                        p = j * HP + c
                        m = mm(bank[n][:, c * P:(c + 1) * P], omega_bd[:, p * P:(p + 1) * P],
                               src[:, bass.ds(i * P, P)])
                    m.then_inc(feat_done, 1)

            def a2_tile(i, first, last):
                for j in range(HALF):
                    u = i * HALF + j
                    pe.wait_ge(kf_ready, u + 1)
                    for c in range(HP):
                        m = nc.tensor.transpose(bank[2][:, c * P:(c + 1) * P], kf[:, j, c, :], ident)
                    m.then_inc(kT_done, 1)
                    pe.wait_ge(qw_ready, u + 1)
                    for par in range(2):
                        rs = slice(64 * par, 64 * par + 64)
                        for c in range(HP):
                            m = mm(bank[3 + par][:, c * P:(c + 1) * P], kf[rs, j, c, :], qf[rs, j, c, :])
                        m.then_inc(aw_done, 1)
                    if j == 0:
                        feats(i, 1)
                    elif not last:
                        feats(i + 1, 0)
                    if j == 0 and not first:
                        project(i - 1)
                    pe.wait_ge(v_set, i + 1)
                    pe.wait_ge(st_ready, u + 1)
                    pe.wait_ge(aw_ready, 2 * u + 2)
                    wait_apart(pe, att_ready, u + 1)
                    for slot in range(2):
                        for g in range(4):
                            h = slot * 4 + g
                            c, par = divmod(h, 2)
                            rs = slice(64 * par, 64 * par + 64)
                            mm(bank[5][32 * g:32 * g + 32, slot * P:(slot + 1) * P], state[rs, j * HP + c, :],
                               qf[rs, j, c, :], stop=False)
                        for g in range(4):
                            h = slot * 4 + g
                            c, par = divmod(h, 2)
                            m = mm(bank[5][32 * g:32 * g + 32, slot * P:(slot + 1) * P], v_one[:, j * HH + h, :],
                                   att_w[:, j, par, c, :], start=False)
                    m.then_inc(oT_done, 1)
                    pe.wait_ge(kT_ready, u + 1)
                    pe.wait_ge(st_ready, u + 2)
                    for c in range(HP):
                        h = j * HH + 2 * c
                        m = mm(bank[7][:, c * 18:(c + 1) * 18], kf_tok[:, j, c, :], v_one[:, h:h + 2, 0:9])
                    m.then_inc(st_done, 1)
                    pe.wait_ge(oT_ready, u + 1)
                    for slot in range(2):
                        m = nc.tensor.transpose(bank[5][:, (2 + slot) * P:(3 + slot) * P],
                                                o_t[:, slot * P:(slot + 1) * P], ident)
                    m.then_inc(o2_done, 1)
                pe.wait_ge(att_ready, i * 2 + 3)
                if not first:
                    pe.wait_ge(x1_done, i)
                nc.tensor.transpose(bank[6][:, 0:P], att[:], ident).then_inc(attT_done, 1)

            def project(i):
                pe.wait_ge(attT_ready, i + 1)
                mm(bank[6][:, P:2 * P], att_t[:], wa_out[:]).then_inc(wo_done, 1)

            pe.wait_ge(qknT_saved, 2 * NB)
            feats(0, 0)
            a2_tile(0, True, False)
            with pe.Fori(1, NT - 1) as i:
                a2_tile(i, False, False)
            a2_tile(NT - 1, False, True)
            project(NT - 1)
            with pe.Fori(0, NB) as g:
                pe.wait_ge(xn_ready, g + 1)
                for t in range(TB):
                    m = nc.tensor.transpose(bank[0][:, t * P:(t + 1) * P], xn_tok[:, t, :], ident)
                m.then_inc(xnT_done, 1)
            phase_end(pe, a_done)
            pe.wait_ge(a_done, 5)
            pe.wait_ge(ld_wb, 64)

            def project_q(u, par, uh):
                pe.wait_ge(st_in[par], uh * 32 + 32)
                pe.wait_ge(k_part, u + 1)
                for n in range(2):
                    m = mm(bank[n][:], w_st[:, par, n, :], x_st[:, par, :])
                m.then_inc(q_done, 1)

            def project_k(u, par):
                pe.wait_ge(q_part, u + 1)
                for n in range(2):
                    m = mm(bank[n][:], w_st[:, par, 2 + n, :], x_st[:, par, :])
                m.then_inc(k_done, 1)

            def project_v(u, par, first=False):
                if not first:
                    pe.wait_ge(o_added, u - 1)
                elif u == 1:
                    pe.wait_ge(v_ready, 1)
                for t in range(TB):
                    m = mm(bank[2][:, t * P:(t + 1) * P], x_st[:, par, t * P:(t + 1) * P], w_st[:, par, 4, :])
                m.then_inc(v_done, 1)

            def scores(u, par, t):
                for h in range(2):
                    pe.wait_ge(s_min, 8 * u + 2 * t + h + 1)
                    rs = slice(64 * h, 64 * h + 64)
                    mm(bank[3 + h][:, 0:(t + 1) * P], q_rot[rs, par, t * P:(t + 1) * P],
                       k_rot[rs, par, 0:(t + 1) * P]).then_inc(s_done, 1)

            def turn(u, t):
                for h in range(2):
                    pe.wait_ge(p_ready, 8 * u + 2 * t + h + 1)
                    pe.wait_ge(pT_ready, 8 * u + 2 * t + h + 1)
                    for k in range(t + 1):
                        m = nc.tensor.transpose(bank[5 + h][:, k * P:(k + 1) * P],
                                                prob[:, t % 2 * 2 + h, k * P:(k + 1) * P], ident)
                    m.then_inc(pT_done, 1)

            def context(u, par):
                pe.wait_ge(v_ready, u + 1)
                pe.wait_ge(pT_ready, 8 * u + 10)
                pe.wait_ge(c_ready, u + 1)
                for k in range(TB):
                    for h in range(2):
                        m = mm(bank[7][64 * h:64 * h + 64, k * P:SEQ], v_sb[:, par, k, 64 * h:64 * h + 64],
                               pt[:, h, k, k * P:SEQ], start=k == 0, stop=k == TB - 1)
                m.then_inc(c_done, 1)

            def output(u, last=False):
                pe.wait_ge(c_ready, u + 2)
                if not last:
                    pe.wait_ge(v_ready, u + 2)
                for t in range(TB):
                    m = mm(bank[2][:, t * P:(t + 1) * P], ctx_t[:, t * P:(t + 1) * P],
                           wo[:, bass.ds(u % PAIR, 1), :].squeeze(1))
                m.then_inc(o_done, 1)

            def unit(u, par, uh, uh_next, first, last):
                scores(u, par, 0)
                scores(u, par, 1)
                if not first:
                    turn(u - 1, 3)
                if not last:
                    project_q(u + 1, 1 - par, uh_next)
                if not first:
                    context(u - 1, 1 - par)
                turn(u, 0)
                scores(u, par, 2)
                if not last:
                    project_k(u + 1, 1 - par)
                turn(u, 1)
                if not first:
                    output(u - 1)
                if not last:
                    project_v(u + 1, 1 - par, first)
                scores(u, par, 3)
                turn(u, 2)

            def q_and_k_ready(u):
                pe.wait_ge(q_ready, u + 1)
                pe.wait_ge(k_ready, u + 1)

            project_q(0, 0, 0)
            project_k(0, 0)
            project_v(0, 0, True)
            q_and_k_ready(0)
            unit(0, 0, 0, 0, True, False)
            with pe.Fori(0, UNITS // 2 - 1) as i:
                q_and_k_ready(i * 2 + 1)
                unit(i * 2 + 1, 1, i, i + 1, False, False)
                q_and_k_ready(i * 2 + 2)
                unit(i * 2 + 2, 0, i + 1, i + 1, False, False)
            q_and_k_ready(UNITS - 1)
            unit(UNITS - 1, 1, UNITS // 2 - 1, 0, False, True)
            turn(UNITS - 1, 3)
            context(UNITS - 1, 1)
            output(UNITS - 1, True)
            phase_end(pe, b_done)
            pe.wait_ge(b_done, 5)
            with pe.Fori(0, NB) as b:
                pe.wait_ge(an_ready, b + 1)
                for t in range(TB):
                    m = nc.tensor.transpose(bank[0][:, t * P:(t + 1) * P], an[:, t, :], ident)
                m.then_inc(anT_done, 1)
                pe.wait_ge(anT_ready, b + 1)
                for t in range(TB):
                    m = mm(bank[1][:, t * NE:t * NE + NE - 1], an_t[:, t * P:(t + 1) * P], wr[:])
                m.then_inc(lg_done, 1)
                pe.wait_ge(g_ready, b + 1)
                for t in range(TB):
                    m = nc.tensor.transpose(bank[3][0:NE, t * P:(t + 1) * P], gates[:, t, :], ident)
                m.then_inc(gT_done, 1)
                pe.wait_ge(g3_ready, b + 1)
                for t in range(TB):
                    m = nc.tensor.transpose(bank[4][0:3 * NE, t * P // 2:(t + 1) * P // 2].bitcast(BF16),
                                            gates3[:, t, :], ident_bf[:])
                m.then_inc(g3T_done, 1)
                pe.wait_ge(gT_ready, b + 1)
                for t in range(TB):
                    m = mm(bank[2][:, t * P:(t + 1) * P], gates_t[:, t * P:(t + 1) * P], b2[:])
                m.then_inc(b2_done, 1)
            phase_end(pe, t_done_all)
            pe.wait_ge(t_done_all, 4)
            pe.wait_ge(ld_w2, 16)

            def up(bp, e, eh, ee, bb):
                n = bp * (2 * NE) + e * 2 + bb
                pe.wait_ge(w1_in[ee], bp * (16 * NE // 2) + eh * 16 + 16)
                pe.wait_ge(gelu_done, n + 1)
                pe.wait_ge(hg_ready, n + 1)
                mm(bank[bb][:], w1_st[:, ee, :], slab_x[:, bass.ds(bp * (2 * SEQ) + bb * SEQ, SEQ)]).then_inc(hd_done, 1)
                mm(bank[2 + bb][:], one(sel_all, e),
                   gates3_all[:, bass.ds(bp * (2 * SEQ) + bb * SEQ, SEQ)]).then_inc(gb_done, 1)

            def down(bp, e, bb):
                n = bp * (2 * NE) + e * 2 + bb
                pe.wait_ge(hg_ready, n + 3)
                for t in range(TB):
                    m = mm(bank[4 + bb][:, t * P:(t + 1) * P], hid_g[:, bb, t * P:(t + 1) * P],
                           one(w2_all, e), start=False, stop=False, skip_group_check=True)
                m.then_inc(y_part, 1)

            with pe.Fori(0, NB // 2) as bp:
                for bb in range(2):
                    pe.wait_ge(y_link, bp * 2 + (bb + 1))
                    mm(bank[4 + bb][:], zeros_bf[:, 0:P], zeros_bf[:], stop=False, skip_group_check=True)
                up(bp, 0, 0, 0, 0)
                up(bp, 0, 0, 0, 1)
                with pe.Fori(0, NE // 2 - 1) as e2:
                    for ee in range(2):
                        for bb in range(2):
                            down(bp, e2 * 2 + ee, bb)
                            up(bp, e2 * 2 + (ee + 1), e2 + (ee + 1) // 2, 1 - ee, bb)
                for bb in range(2):
                    down(bp, NE - 2, bb)
                    up(bp, NE - 1, NE // 2 - 1, 1, bb)
                for bb in range(2):
                    down(bp, NE - 1, bb)
                    mm(bank[4 + bb][:], zeros_bf[:, 0:P], zeros_bf[:], start=False, skip_group_check=True).then_inc(y_done, 1)

        @block.vector
        def _(dve):
            v = nc.vector

            def link(ins, s, at):
                ins.then_inc(s, 1)
                dve.wait_ge(s, at)

            dve.wait_ge(ld_mod, 32)
            dve.wait_ge(su_exp, 1)
            link(v.tensor_scalar(c_e[:], c_e[:], 1.0, None, ALU.add), su_dve, 1)
            link(v.reciprocal(c_e[:], c_e[:]), su_dve, 2)
            link(v.tensor_tensor(sil[:], c_t[:], c_e[:], ALU.mult), su_dve, 3)
            dve.wait_ge(ld_const, 64)
            link(v.tensor_scalar(ang, const[:, C_IOTA:C_IOTA + SEQ], cols[:, K_THETA:K_THETA + 1], None, ALU.mult), su_dve, 4)
            n = 4
            for k, quarter in ((2, 0.25), (3, 0.0)):
                r = rope[:, k, :]
                for src, s1, s2, o0, o1 in ((ang, 1 / (2 * np.pi), quarter, ALU.mult, ALU.add),
                                            (turns, ROUND, ROUND, ALU.add, ALU.subtract)):
                    n += 1
                    link(v.tensor_scalar(turns, src, float(s1), float(s2), o0, o1), su_dve, n)
                for w, part_2pi in enumerate(TWO_PI):
                    n += 1
                    link(v.scalar_tensor_tensor(r, turns, -part_2pi, ang if w == 0 else r, ALU.mult, ALU.add), su_dve, n)
                n += 1
                link(v.tensor_scalar(r, r, float(2 * np.pi * quarter), PI_UNDER, ALU.add, ALU.min), su_dve, n)
                n += 1
                link(v.tensor_scalar(r, r, -PI_UNDER, None, ALU.max), su_dve, n)
            assert n == SU_COS
            link(v.tensor_scalar(root2s, cols[:, K_NODE:K_NODE + 1], 0.0, 2.0, ALU.max, ALU.mult), su_dve, SU_NODE)
            link(v.tensor_scalar(neg_s, cols[:, K_NODE:K_NODE + 1], -1.0, None, ALU.mult), su_dve, SU_NODE + 1)
            link(v.tensor_scalar(wfeat, cols[:, K_WEIGHT:K_WEIGHT + 1], 0.0, 1.0 / 32, ALU.max, ALU.mult), su_dve, SU_NODE + 2)
            link(v.tensor_scalar(top, cols[:, K_NODE:K_NODE + 1], CLIP, None, ALU.add), su_dve, SU_NODE + 3)
            v.tensor_copy(ident_bf[:], ident)
            dve.wait_ge(su_sin, 2)
            link(v.tensor_scalar(rope[:, 3, :], rope[:, 3, :], const[:, C_SIGN:C_SIGN + 1], None, ALU.mult), su_dve, SU_NODE + 4)
            link(v.tensor_scalar(rope[:, 0:2, :], rope[:, 2:4, :], -0.125, None, ALU.mult), su_dve, SU_STEPS)
            dve.wait_ge(su_mod_ev, 2 * NB)
            v.tensor_scalar(mod_all[:, :, 1, :], mod_all[:, :, 1, :], 1.0, None, ALU.add)
            v.tensor_scalar(mod_all[:, :, 4, :], mod_all[:, :, 4, :], 1.0, None, ALU.add)
            sg = qkv[:].rearrange("p t d -> p (t d)")[:, 0:NB * D].rearrange("p (b d) -> p b d", d=D)
            mg = sq.rearrange("p t d -> p (t d)")[:, 0:NB * D].rearrange("p (b d) -> p b d", d=D)
            for w, k in enumerate((2, 5)):
                g = mod_all[:, :, k, :]
                link(v.tensor_scalar(sg, g, 0.0, 2.0, ALU.is_ge, ALU.mult), su_dve, SU_STEPS + 5 * w + 1)
                link(v.tensor_scalar(sg, sg, 1.0, None, ALU.subtract), su_dve, SU_STEPS + 5 * w + 2)
                link(v.scalar_tensor_tensor(mg, g, -1.0, g, ALU.mult, ALU.max), su_dve, SU_STEPS + 5 * w + 3)
                link(v.tensor_scalar(mg, mg, 0.25, None, ALU.max), su_dve, SU_STEPS + 5 * w + 4)
                link(v.tensor_tensor(g, mg, sg, ALU.mult), su_dve, SU_STEPS + 5 * w + 5)
            v.engine_nop().then_inc(su_modfix, 1)

            def layer_norm(g, chain, per, var, stdsem, shift, scale1):
                for t in range(TB):
                    m = v.bn_stats(stats[:, t, :], x_all[:, bass.ds(g * TB + t, 1), :].squeeze(1))
                m.then_inc(chain, 1)
                wait_apart(dve, chain, g * per + 1)
                for t in range(TB):
                    m = v.bn_aggr(mv[:, t, :], stats[:, t, :])
                m.then_inc(var, 1)
                dve.wait_ge(stdsem, g + 1)
                link(v.reciprocal(std[:], std[:]), chain, g * per + 2)
                for t in range(TB):
                    m = v.tensor_scalar(hrow[:, t, :], x_all[:, bass.ds(g * TB + t, 1), :].squeeze(1),
                                        mv[:, t, 0:1], std[:, t:t + 1], ALU.subtract, ALU.mult)
                link(m, chain, g * per + 3)
                link(v.tensor_tensor(hrow[:], hrow[:], mod_all[:, bass.ds(g, 1), scale1, :].to_broadcast([P, TB, D]),
                                     ALU.mult), chain, g * per + 4)
                return v.tensor_tensor(hrow[:], hrow[:], mod_all[:, bass.ds(g, 1), shift, :].to_broadcast([P, TB, D]), ALU.add)

            dve.wait_ge(ld_x, 32)
            with dve.Fori(0, NB) as g:
                layer_norm(g, a1_dve, A1D, ln_var, ln_std, 0, 1).then_inc(h_ready, 1)
                for t in range(TB):
                    dve.wait_ge(qkv_done, g * TB + (t + 1))
                    m = v.tensor_tensor(qkv[:, t, :], bank[1 + t][:, 0:3 * D], rows[:, R_BQKV:R_BQKV + 3 * D], ALU.add)
                m.then_inc(qkv_ready, 1)
                dve.wait_ge(qkv_ready, g + 1)
                qk = qkv[:, :, 0:2 * D]
                link(v.tensor_tensor(sq, qk, qk, ALU.mult), a1_dve, g * A1D + 5)
                link(v.tensor_reduce(ss[:], sq.rearrange("p t (h d) -> p t h d", d=AHD), AX, ALU.add), a1_dve, g * A1D + 6)
                v.tensor_scalar(ss[:], ss[:], 1e-24, None, ALU.max).then_inc(ss_ready, 1)
                dve.wait_ge(nrm_ready, g + 1)
                link(v.reciprocal(ss[:], ss[:]), nrm_inv, g + 1)
                v.tensor_tensor(qkn.rearrange("p t (h d) -> p t h d", d=AHD), qk.rearrange("p t (h d) -> p t h d", d=AHD),
                                ss[:].unsqueeze(3).to_broadcast([P, TB, 2 * AH, AHD]), ALU.mult).then_inc(qkn_ready, 1)
                dve.wait_ge(v_saved, g + 1)

            dve.sem_inc(att_ready, 1)
            dve.wait_ge(v_saved, NB)
            dve.wait_ge(su_sin, 3)

            def clip_above(u, j):
                for n, f in enumerate((qf, kf)):
                    dve.wait_ge(feat_done, 2 * u + (n + 1))
                    v.tensor_scalar(f[:, j], bank[n][:].rearrange("p (c q) -> p c q", q=P), root2s, top,
                                    ALU.mult, ALU.min).then_inc(min_done, 1)

            def clip_below(u, j):
                dve.wait_ge(exp_done, 2 * u + 2)
                v.tensor_scalar(kf[:, j], kf[:, j], EXP_LOW, None, ALU.max).then_inc(kf_ready, 1)

            def residual(i):
                dve.wait_ge(wo_done, i + 1)
                ga = mod_all[:, bass.ds(i // TB, 1), 2, :].squeeze(1)
                link(v.tensor_tensor(proj_tmp[:], bank[6][:, P:2 * P], ga, ALU.mult), x1_link, i + 1)
                xi = x_all[:, bass.ds(i, 1), :].squeeze(1)
                v.tensor_tensor(xi, xi, proj_tmp[:], ALU.add).then_inc(x1_done, 1)

            def a2_tile(i, first, last):
                for j in range(HALF):
                    u = i * HALF + j
                    for par in range(2):
                        dve.wait_ge(aw_done, 2 * u + (par + 1))
                        v.tensor_tensor(att_w[:, j, par], bank[3 + par][:].rearrange("p (c q) -> p c q", q=P),
                                        mask_a.unsqueeze(1).to_broadcast([P, HP, P]), ALU.mult).then_inc(aw_ready, 1)
                    if j == 0 or not last:
                        clip_above(u + 1, 1 - j)
                    if j == 0 and not first:
                        residual(i - 1)
                    dve.wait_ge(oT_done, u + 1)
                    v.tensor_copy(o_t[:], bank[5][:, 0:2 * P]).then_inc(oT_ready, 1)
                    dve.wait_ge(st_done, u + 1)
                    new = bank[7][:, 0:HP * 18].rearrange("p (c k) -> p c k", k=18)
                    for par in range(2):
                        rs = slice(64 * par, 64 * par + 64)
                        s = state[rs, j * HP:(j + 1) * HP, 0:9]
                        m = v.tensor_tensor(s, s, new[rs, :, 9 * par:9 * par + 9], ALU.add)
                    link(m, st_link, u + 1)
                    s = state[:, j * HP:(j + 1) * HP, 0:9]
                    v.tensor_scalar(s, s, const[:, bass.ds(C_KEEP + i, 1)], None, ALU.mult).then_inc(st_ready, 1)
                    if j == 0 or not last:
                        clip_below(u + 1, 1 - j)
                    if j == 0 and not first:
                        dve.wait_ge(attT_done, i)
                    dve.wait_ge(o2_done, u + 1)
                    o2 = bank[5][:, 2 * P:4 * P].rearrange("p (h k) -> p h k", k=32)
                    link(v.tensor_scalar(den[:], o2[:, :, AHD], 1e-6, None, ALU.max), att_link, 2 * u + 1)
                    link(v.reciprocal(den[:], den[:]), att_link, 2 * u + 2)
                    v.tensor_tensor(att[:, j * HH * AHD:(j + 1) * HH * AHD].rearrange("p (h d) -> p h d", d=AHD),
                                    o2[:, :, 0:AHD], den[:].unsqueeze(2).to_broadcast([P, HH, AHD]),
                                    ALU.mult).then_inc(att_ready, 1)

            clip_above(0, 0)
            clip_below(0, 0)
            a2_tile(0, True, False)
            with dve.Fori(1, NT - 1) as i:
                a2_tile(i, False, False)
            a2_tile(NT - 1, False, True)
            residual(NT - 1)
            dve.wait_ge(x1_done, NT)
            with dve.Fori(0, NB) as g:
                link(layer_norm(g, a3_dve, A3D, a3_var, a3_std, 3, 4), a3_dve, g * A3D + 5)
                for t in range(TB):
                    m = v.tensor_tensor_reduce(out=sq[:, t, 0:D], in0=hrow[:, t, :], in1=hrow[:, t, :], scale=1.0 / D,
                                               scalar=0.0, op0=ALU.mult, op1=ALU.add, accum_out=ms[:, t:t + 1])
                m.then_inc(a3_ms, 1)
                dve.wait_ge(a3_rms, g + 1)
                link(v.reciprocal(ms[:], ms[:]), a3_inv, g + 1)
                for t in range(TB):
                    m = v.scalar_tensor_tensor(xn_tok[:, t, :], hrow[:, t, :], ms[:, t:t + 1], rows[:, R_G1:R_G1 + D],
                                               ALU.mult, ALU.mult)
                m.then_inc(xn_ready, 1)
                dve.wait_ge(xnT_done, g + 1)
                dve.wait_ge(ao_set, g + 1)
            phase_end(dve, a_done)
            dve.wait_ge(a_done, 5)
            dve.sem_inc(s_min, 2)
            dve.sem_inc(k_part, 1)
            dve.sem_inc(pT_ready, 2)
            dve.sem_inc(c_ready, 1)
            dve.sem_inc(pT_done, 4)

            def rotate(which, u):
                done, part_ready = ((q_done, q_part), (k_done, k_part))[which]
                dve.wait_ge(done, u + 1)
                cb = cols[:, K_QKV:K_QKV + PAIR * 5].rearrange("p (a k) -> p a k", k=5)
                for n in range(2):
                    m = v.scalar_tensor_tensor(part[:, 2 * which + n, :], bank[n][:],
                                               cb[:, bass.ds(u % PAIR, 1), 2 * which + n], rope[:, 2 * which + n, :],
                                               ALU.add, ALU.mult)
                m.then_inc(part_ready, 1)

            def minimum(u, t):
                for h in range(2):
                    s = t % 2 * 2 + h
                    dve.wait_ge(s_done, 8 * u + 2 * t + h + 1)
                    wait_apart(dve, pT_done, 8 * u + 2 * t + h + 1)
                    n = (t + 1) * P
                    v.tensor_tensor_reduce(out=prob[:, s, 0:n], in0=bank[3 + h][:, 0:n], in1=mask_b[:, SEQ - n:SEQ],
                                           scale=1.0, scalar=3e38, op0=ALU.add, op1=ALU.min,
                                           accum_out=low[:, s:s + 1]).then_inc(s_min, 1)

            def invert(u, t):
                dve.wait_ge(p_exp, 8 * u + 2 * t + 2)
                s = t % 2 * 2
                v.reciprocal(rinv[:, s:s + 2], rsum[:, s:s + 2]).then_inc(p_inv, 1)

            def add_output(u):
                dve.wait_ge(o_done, u + 1)
                d = ao_all[:, bass.ds(u // PAIR * TB, TB), :]
                v.tensor_tensor(d, d, bank[2][:].rearrange("p (t d) -> p t d", d=D), ALU.add).then_inc(o_added, 1)

            def unit(u, par, first, last):
                minimum(u, 0)
                if not first:
                    invert(u - 1, 3)
                minimum(u, 1)
                if not last:
                    rotate(0, u + 1)
                invert(u, 0)
                minimum(u, 2)
                if not last:
                    rotate(1, u + 1)
                invert(u, 1)
                if not first:
                    add_output(u - 1)
                minimum(u, 3)
                invert(u, 2)

            rotate(0, 0)
            rotate(1, 0)
            unit(0, 0, True, False)
            with dve.Fori(0, UNITS // 2 - 1) as i:
                unit(i * 2 + 1, 1, False, False)
                unit(i * 2 + 2, 0, False, False)
            unit(UNITS - 1, 1, False, True)
            invert(UNITS - 1, 3)
            add_output(UNITS - 1)
            phase_end(dve, b_done)
            dve.wait_ge(b_done, 5)
            v.memset(gates[:, :, NE - 1:NE], 1.0)
            v.tensor_copy(sel_all, sel_src[:].unsqueeze(2).to_broadcast([3 * NE, NE, P]))
            with dve.Fori(0, NB) as b:
                base = b * TD
                ao_b = ao_all[:, bass.ds(b * TB, TB), :]
                ao_t = [ao_all[:, bass.ds(b * TB + t, 1), :].squeeze(1) for t in range(TB)]
                link(v.tensor_tensor(t_tmp[:], ao_b, ao_b, ALU.mult), t_dve, base + 1)
                v.tensor_reduce(t_ms[:], t_tmp[:], AX, ALU.add).then_inc(t_msd, 1)
                dve.wait_ge(t_rms, b + 1)
                link(v.reciprocal(t_ms[:], t_ms[:]), t_dve, base + 2)
                for t in range(TB):
                    m = v.scalar_tensor_tensor(an[:, t, :], ao_t[t], t_ms[:, t:t + 1], rows[:, R_G2:R_G2 + D],
                                               ALU.mult, ALU.mult)
                m.then_inc(an_ready, 1)
                dve.wait_ge(lg_done, b + 1)
                link(v.tensor_tensor(logit[:], bank[1][:, 0:TB * NE].rearrange("p (t e) -> p t e", e=NE)[:, :, 0:NE - 1],
                                     rows[:, R_RB:R_RB + NE - 1].unsqueeze(1).to_broadcast([P, TB, NE - 1]), ALU.add),
                     t_dve, base + 3)
                link(v.tensor_reduce(red[:], logit[:], AX, ALU.max), t_dve, base + 4)
                v.tensor_tensor(logit[:], logit[:], red[:].unsqueeze(2).to_broadcast([P, TB, NE - 1]),
                                ALU.subtract).then_inc(lg_ready, 1)
                dve.wait_ge(ex_ready, b + 1)
                link(v.tensor_reduce(red[:], logit[:], AX, ALU.add), t_dve, base + 5)
                link(v.reciprocal(red[:], red[:]), t_dve, base + 6)
                link(v.tensor_tensor(aff[:], logit[:], red[:].unsqueeze(2).to_broadcast([P, TB, NE - 1]), ALU.mult),
                     t_dve, base + 7)
                dve.nop(nofuse=True)
                for t in range(TB):
                    m = v.max(top8[:, t, :], aff[:, t, :])
                m.then_inc(t_dve, 1)
                wait_apart(dve, t_dve, base + 8)
                for t in range(TB):
                    m = v.max_index(idx8[:, t, :], top8[:, t, :], aff[:, t, :])
                link(m, t_dve, base + 9)
                link(v.tensor_copy(idxf[:], idx8[:, :, 0:TOPK]), t_dve, base + 10)
                for t in range(TB):
                    m = v.tensor_tensor(onehot[:, t],
                                        const[:, C_EIOTA:C_EIOTA + NE - 1].unsqueeze(1).to_broadcast([P, TOPK, NE - 1]),
                                        idxf[:, t, :].unsqueeze(2).to_broadcast([P, TOPK, NE - 1]), ALU.is_equal)
                link(m, t_dve, base + 11)
                link(v.tensor_tensor(chosen[:], onehot[:, :, 0, :], onehot[:, :, 1, :], ALU.add), t_dve, base + 12)
                link(v.tensor_tensor(chosen[:], chosen[:], onehot[:, :, 2, :], ALU.add), t_dve, base + 13)
                v.tensor_tensor(gates[:, :, 0:NE - 1], aff[:], chosen[:], ALU.mult).then_inc(g_ready, 1)
                dve.wait_ge(g_ready, b + 1)
                g3 = [gates3[:, :, k * NE:(k + 1) * NE] for k in range(3)]
                link(v.tensor_copy(g3[0], gates[:]), t_dve, base + 14)
                link(v.tensor_tensor(rest[:], gates[:], g3[0], ALU.subtract), t_dve, base + 15)
                link(v.tensor_copy(g3[1], rest[:]), t_dve, base + 16)
                link(v.tensor_tensor(rest[:], rest[:], g3[1], ALU.subtract), t_dve, base + 17)
                v.tensor_copy(g3[2], rest[:]).then_inc(g3_ready, 1)
                link(v.tensor_tensor(t_tmp[:], ao_b, an[:], ALU.add), t_dve, base + 18)
                dve.wait_ge(b2_done, b + 1)
                link(v.tensor_tensor(t_tmp[:], t_tmp[:], bank[2][:].rearrange("p (t d) -> p t d", d=D), ALU.add),
                     t_dve, base + 19)
                v.tensor_tensor(t_tmp[:], t_tmp[:], mod_all[:, bass.ds(b, 1), 5, :].to_broadcast([P, TB, D]),
                                ALU.mult).then_inc(base_link, 1)
                dve.wait_ge(base_link, b * 2 + 1)
                xb = x_all[:, bass.ds(b * TB, TB), :]
                link(v.tensor_tensor(xb, xb, t_tmp[:], ALU.add), base_link, b * 2 + 2)
                dve.wait_ge(anT_saved, b + 1)
            phase_end(dve, t_done_all)
            dve.wait_ge(t_done_all, 4)
            dve.sem_inc(hg_ready, 2)
            dve.sem_inc(gelu_done, 2)
            for bb in range(2):
                dve.sem_inc(y_out[bb], 16)
            dve.sem_inc(y_link, 2)
            with dve.Fori(0, NB // 2) as bp:
                with dve.Fori(0, NE) as e:
                    for bb in range(2):
                        n = bp * (2 * NE) + e * 2 + bb
                        dve.wait_ge(gelu_done, n + 3)
                        dve.wait_ge(gb_done, n + 1)
                        v.tensor_tensor(hid_g[:, bb, :], hid[:, bb, :], bank[2 + bb][:], ALU.mult).then_inc(hg_ready, 1)
                for bb in range(2):
                    dve.wait_ge(y_done, bp * 2 + (bb + 1))
                    dve.wait_ge(y_out[bb], bp * 16 + 16)
                    v.tensor_tensor(y_sb[:, bb], bank[4 + bb][:].rearrange("p (t d) -> p t d", d=D),
                                    mod_all[:, bass.ds(bp * 2 + bb, 1), 5, :].to_broadcast([P, TB, D]),
                                    ALU.mult).then_inc(y_link, 1)
                    dve.wait_ge(y_link, bp * 2 + (bb + 3))
                    v.tensor_tensor(y_sb[:, bb], y_sb[:, bb], x_all[:, bass.ds(bp * (2 * TB) + bb * TB, TB), :],
                                    ALU.add).then_inc(y_ready, 1)


def constants():
    p = np.arange(P)
    c = np.zeros((P, C_END), np.float32)
    c[:, C_ID:C_ID + P] = np.eye(P)
    c[:, C_MASKA:C_MASKA + P] = p[:, None] <= p[None]
    c[:, C_MASKB + SEQ - P:C_MASKB + SEQ] = np.where(p[None] > p[:, None], BIG, 0)
    c[:, C_IOTA:C_IOTA + SEQ] = np.arange(SEQ)
    c[:, C_EIOTA:C_EIOTA + NE] = np.arange(NE)
    c[:, C_KEEP:C_KEEP + NT] = np.arange(NT) % TB != TB - 1
    c[:, C_SIGN] = np.where(p // 32 % 2 == 0, -1, 1)
    sel = (np.arange(3 * NE)[:, None] % NE == np.arange(NE)[None]).astype(np.float32)
    return c, sel


def kernel(**inputs):
    import concourse.bacc as bacc
    from concourse.bass_utils import run_bass_kernel_spmd

    x = {k[3:]: np.asarray(v) for k, v in inputs.items()}
    c, sel = constants()

    def every(row, n=P):
        return np.broadcast_to(row.reshape(1, -1), (n, row.size))

    def halves(w):
        r = w.reshape(w.shape[0], PAIR, 2, 32, 2).transpose(0, 1, 2, 4, 3)
        return [m.reshape(w.shape[0], PAIR, P) for m in (r, r[:, :, :, ::-1])]

    rows = np.zeros((P, R_END), np.float32)
    for at, k in ((R_BQKV, "attn_bqkv"), (R_BOUT, "attn_bout"), (R_G1, "ffn_gamma1"), (R_G2, "ffn_gamma2"),
                  (R_OB, "ffn_o_b"), (R_RB, "ffn_router_b")):
        rows[:, at:at + x[k].size] = every(x[k])
    cols = np.zeros((P, K_END), np.float32)
    node = np.arange(P) // 32 % 2
    cols[:, K_NODE] = x["attn_quad_nodes"][node]
    cols[:, K_WEIGHT] = x["attn_quad_weights"][node]
    cols[:, K_THETA] = x["ffn_theta"][np.arange(P) % 32]
    bias = [m[0] for k in ("q", "k") for m in halves(x[f"ffn_{k}_b"][None])] + [x["ffn_v_b"].reshape(PAIR, P)]
    cols[:, K_QKV:K_QKV + PAIR * 5] = np.stack(bias, -1).transpose(1, 0, 2).reshape(P, -1)
    cols[:, K_B1:K_B1 + NE] = np.concatenate([x["ffn_re_b1"], x["ffn_sh_b1"][None]]).T
    omega = np.zeros((AH, AHD, AH, 2, 32), np.float32)
    for h in range(AH):
        omega[h, :, h] = x["attn_omega"][:, h].transpose(1, 0, 2)
    wqkvb = np.stack([m for k in ("q", "k") for m in halves(x[f"ffn_{k}_w"])] + [x["ffn_v_w"].reshape(D, PAIR, P)], 2)
    arrays = {
        "x": x["attn_x"], "c_t": x["c"].T, "wmod": x["wmod"], "const": c, "sel": sel, "rows": rows, "cols": cols,
        "wa_qkv": x["attn_Wqkv"], "wa_out": x["attn_Wout"], "omega_bd": omega.reshape(P, -1),
        "wqkvb": wqkvb, "wo": x["ffn_o_w"].reshape(PAIR, P, D).transpose(1, 0, 2),
        "wr": x["ffn_router_w"], "b2": np.concatenate([x["ffn_re_b2"], x["ffn_sh_b2"][None]]),
        "w1": np.concatenate([x["ffn_re_w1"], x["ffn_sh_w1"][None]]).transpose(1, 0, 2).reshape(D, -1),
        "w2": np.concatenate([x["ffn_re_w2"], x["ffn_sh_w2"][None]]).transpose(1, 0, 2).reshape(P, -1),
    }
    nc = bacc.Bacc("TRN2", target_bir_lowering=False, num_devices=1)
    aps, given = {}, {}
    for name, v in arrays.items():
        v = np.ascontiguousarray(v)
        given[f"in_{name}"] = v
        aps[name] = nc.dram_tensor(f"in_{name}", v.shape, mybir.dt.from_np(v.dtype), kind="ExternalInput").ap()
    out = nc.dram_tensor("out_y", (NB, SEQ, D), F32, kind="ExternalOutput").ap()
    build_block(nc, aps, out)
    r = run_bass_kernel_spmd(nc, [given], core_ids=[0])
    return r.results[0]["out_y"]
```

```python
from contextlib import ExitStack

import numpy as np

import concourse.bass as bass
from concourse import mybir

F32 = mybir.dt.float32
BF16 = mybir.dt.bfloat16
U32 = mybir.dt.uint32
ALU = mybir.AluOpType
ACT = mybir.ActivationFunctionType
AX = mybir.AxisListType.X

P = 128
D = 128
NB, SEQ = 8, 512
TB = SEQ // P
NT = NB * TB
AH, AHD = 16, 8
FEAT = 64
APAIR = AH // 2
HALF = 2
HP = APAIR // HALF
HH = AH // HALF
PAIR = 8
UNITS = NB * PAIR
NE = 32
TOPK = 3
CLIP = 20.0
EXP_LOW = float(np.exp(-CLIP))
BIG = 1e30

C_ID, C_MASKA, C_MASKB, C_IOTA, C_EIOTA, C_KEEP, C_SIGN, C_END = np.cumsum(
    [0, P, P, SEQ, SEQ, NE, NT, 1]).tolist()
R_BQKV, R_BOUT, R_G1, R_G2, R_OB, R_RB, R_END = np.cumsum([0, 3 * D, D, D, D, D, NE]).tolist()
K_NODE, K_WEIGHT, K_THETA, K_QKV, K_B1, K_END = np.cumsum([0, 1, 1, 1, PAIR * 3, NE]).tolist()

SU_COS, SU_NODE, SU_STEPS = 18, 19, 24
ROUND = 12582912.0
_HI = 6.28125
_MID = float(np.uint32(int(np.float32(2 * np.pi - _HI).view(np.uint32)) & 0xFFFFF000).view(np.float32))
TWO_PI = (_HI, _MID, float(np.float32(2 * np.pi - _HI - _MID)))
PI_UNDER = 3.1415925



def one(t, i):
    return t[:, bass.ds(i, 1), :].squeeze(1)


def wait_apart(eng, sem, value):
    eng.wait_ge(sem, value)
    eng.nop(nofuse=True)


def build_block(nc, a, out):
    ctx = ExitStack()
    with ctx:
        def sb(name, shape, dt=F32, where=ctx):
            return where.enter_context(nc.sbuf_tensor(name, shape, dt))

        def sem(name):
            return ctx.enter_context(nc.semaphore(name))

        bank = [ctx.enter_context(nc.psum_tensor(f"bank{i}", [P, 512], F32)) for i in range(8)]

        x_all = sb("x_all", [P, NT, D])
        mod_all = sb("mod_all", [P, NB, 6, D])
        slab_q = sb("slab_q", [P, NT * P])
        slab_k = sb("slab_k", [P, NT * P])
        slab_v = sb("slab_v", [P, NT * D])
        slab_x = sb("slab_x", [P, NT * P])
        ao_all = sb("ao_all", [P, NT, D])
        const = sb("const", [P, C_END])
        rows = sb("rows", [P, R_END])
        cols = sb("cols", [P, K_END])
        wqkvb = sb("wqkvb", [P, PAIR, 3, P])
        wo = sb("wo", [P, PAIR, D])
        wa_qkv = sb("wa_qkv", [P, 3 * D])
        wa_out = sb("wa_out", [P, D])
        omega_bd = sb("omega_bd", [P, APAIR * P])
        rope = sb("rope", [P, 4, SEQ])
        sel_src = sb("sel_src", [3 * NE, NE])
        ident_bf = sb("ident_bf", [P, P], BF16)
        zeros_bf = sb("zeros_bf", [P, SEQ], BF16)
        wr = sb("wr", [P, NE - 1])
        b2 = sb("b2", [NE, D])
        small = sb("small", [P, 8])

        ident = const[:, C_ID:C_ID + P]
        mask_a = const[:, C_MASKA:C_MASKA + P]
        mask_b = const[:, C_MASKB:C_MASKB + SEQ]
        root2s, neg_s, wfeat, eps_col = (small[:, i:i + 1] for i in range(4))
        top = small[:, 4:5]
        bias_qkv = cols[:, K_QKV:K_QKV + PAIR * 3].rearrange("p (a k) -> p a k", k=3)
        v_all = slab_v[:].rearrange("p (n d) -> p n d", d=D)
        pt = slab_v[:].rearrange("p (h k q) -> p h k q", h=2, k=TB)
        gates3_all = slab_v[0:3 * NE, 0:NT * P // 2].bitcast(BF16)
        sel_all = slab_v[0:3 * NE, NT * P // 2:NT * P].bitcast(BF16).rearrange("p (e m) -> p e m", e=NE)
        w1_all = slab_q
        w2_all = slab_k[:].rearrange("p (e d) -> p e d", e=NE)

        wa = ExitStack()
        c_t = sb("c_t", [P, NB], where=wa)
        c_e = sb("c_e", [P, NB], where=wa)
        sil = sb("sil", [P, NB], where=wa)
        wmod = sb("wmod", [P, 6 * D], where=wa)
        angles = sb("angles", [P, 2, SEQ], where=wa)
        ang, turns = angles[:, 0], angles[:, 1]
        stats = sb("stats", [P, TB, 6], where=wa)
        mv = sb("mv", [P, TB, 2], where=wa)
        std = sb("std", [P, TB], where=wa)
        ms = sb("ms", [P, TB], where=wa)
        hrow = sb("hrow", [P, TB, D], where=wa)
        gabout = sb("gabout", [P, D], where=wa)
        h_t = sb("h_t", [P, SEQ], where=wa)
        qkv = sb("qkv", [P, TB, 3 * D], where=wa)
        sq_qkn = sb("sq_qkn", [P, 2, TB, 2 * D], where=wa)
        sq, qkn = sq_qkn[:, 0], sq_qkn[:, 1]
        ss = sb("ss", [P, TB, 2 * AH], where=wa)
        qf = qkv[:].rearrange("p t d -> p (t d)")[:, 0:HALF * HP * P].rearrange("p (j c q) -> p j c q", j=HALF, c=HP)
        kf = sb("kf", [P, HALF, HP, P], where=wa)
        kf_tok = angles[:].rearrange("p j (c f) -> p j c f", c=HP)
        v_one = sb("v_one", [P, AH, 32], where=wa)
        att_w = sq_qkn.rearrange("p j t d -> p (j t d)").rearrange("p (j r c q) -> p j r c q", j=HALF, r=2, c=HP)
        state = sb("state", [P, APAIR, 32], where=wa)
        o_t = sb("o_t", [P, 2 * P], where=wa)
        den = sb("den", [P, HH], where=wa)
        att = sb("att", [P, D], where=wa)
        att_t = sb("att_t", [P, P], where=wa)
        proj_tmp = sb("proj_tmp", [P, D], where=wa)
        xn_tok = hrow
        wa.close()
        wb = ExitStack()
        x_st = slab_k[:, 0:2 * SEQ].rearrange("p (j q) -> p j q", j=2)
        w_st = slab_k[:, 2 * SEQ:2 * SEQ + 6 * P].rearrange("p (j k d) -> p j k d", j=2, k=3)
        raw = slab_k[:, 2 * SEQ + 6 * P:6 * SEQ + 6 * P].rearrange("p (k q) -> p k q", k=4)
        q_rot = sb("q_rot", [P, 2, SEQ], where=wb)
        k_rot = sb("k_rot", [P, 2, SEQ], where=wb)
        part = sb("part", [P, 4, SEQ], where=wb)
        prob = sb("prob", [P, 4, SEQ], where=wb)
        low = sb("low", [P, 4], where=wb)
        rsum = sb("rsum", [P, 4], where=wb)
        rinv = sb("rinv", [P, 4], where=wb)
        v_sb = sb("v_sb", [P, 2, TB, P], where=wb)
        ctx_t = sb("ctx_t", [P, SEQ], where=wb)
        wb.close()
        wt = ExitStack()
        t_ms = sb("t_ms", [P, TB], where=wt)
        t_tmp = sb("t_tmp", [P, TB, D], where=wt)
        an = sb("an", [P, TB, D], where=wt)
        an_t = sb("an_t", [P, SEQ], where=wt)
        logit = sb("logit", [P, TB, NE - 1], where=wt)
        aff = sb("aff", [P, TB, NE - 1], where=wt)
        red = sb("red", [P, TB], where=wt)
        top8 = sb("top8", [P, TB, 8], where=wt)
        idx8 = sb("idx8", [P, TB, 8], U32, where=wt)
        idxf = sb("idxf", [P, TB, TOPK], where=wt)
        onehot = sb("onehot", [P, TB, TOPK, NE - 1], where=wt)
        chosen = sb("chosen", [P, TB, NE - 1], where=wt)
        gates = sb("gates", [P, TB, NE], where=wt)
        rest = sb("rest", [P, TB, NE], where=wt)
        gates3 = sb("gates3", [P, TB, 3 * NE], BF16, where=wt)
        gates_t = sb("gates_t", [NE, SEQ], where=wt)
        w1_st = sb("w1_st", [P, 2, P], where=wt)
        hid = sb("hid", [P, 2, SEQ], where=wt)
        hid_g = sb("hid_g", [P, 2, SEQ], where=wt)
        y_sb = sb("y_sb", [P, 2, TB, D], where=wt)
        c_dummy = sb("c_dummy", [P, 1], where=wt)
        wt.close()

        ld_const, ld_mod, ld_x, ld_wa, ld_wb, ld_w1, ld_w2 = (
            sem(n) for n in ("ld_const", "ld_mod", "ld_x", "ld_wa", "ld_wb", "ld_w1", "ld_w2"))
        su_exp, su_dve, su_mod_mm, su_mod_ev, su_sin, su_pool, su_modfix = (
            sem(n) for n in ("su_exp", "su_dve", "su_mod_mm", "su_mod_ev", "su_sin", "su_pool", "su_modfix"))
        a_done, b_done, t_done_all = sem("a_done"), sem("b_done"), sem("t_done_all")

        block = ctx.enter_context(nc.Block())

        def phase_end(eng, s):
            eng.drain().then_inc(s, 1)

        a1_dve, ln_var, ln_std, h_ready, hT_done, hT_ready, qkv_done, qkv_ready, ss_ready, nrm_ready, \
            qkn_ready, qknT_done, qknT_saved, x_plus, v_saved = (
                sem("a1_" + n) for n in ("dve", "ln_var", "ln_std", "h_ready", "hT_done", "hT_ready",
                                         "qkv_done", "qkv_ready", "ss_ready", "nrm_ready", "qkn_ready",
                                         "qknT_done", "qknT_saved", "x_plus", "v_saved"))
        A1D = 4
        v_set, feat_done, min_done, exp_done, kf_ready, qw_ready, kT_done, kT_ready, aw_done, aw_ready, oT_done, \
            oT_ready, st_done, st_link, st_ready, o2_done, att_link, att_ready, attT_done, attT_ready, \
            wo_done, x1_link, x1_done = (
                sem("a2_" + n) for n in ("v_set", "feat_done", "min_done", "exp_done", "kf_ready", "qw_ready", "kT_done",
                                         "kT_ready", "aw_done", "aw_ready", "oT_done", "oT_ready", "st_done",
                                         "st_link", "st_ready", "o2_done", "att_link", "att_ready",
                                         "attT_done", "attT_ready", "wo_done", "x1_link", "x1_done"))
        a3_dve, a3_var, a3_std, a3_ms, a3_rms, xn_ready, xnT_done, xnT_saved, ao_set = (
            sem("a3_" + n) for n in ("dve", "var", "std", "ms", "rms", "xn_ready", "xnT_done", "xnT_saved",
                                     "ao_set"))
        a3_inv, qk_link = sem("a3_inv"), sem("a1_qk_link")
        A3D = 5
        st_in = [sem("b_staged0"), sem("b_staged1")]
        raw_saved, swapped = sem("b_raw_saved"), sem("b_swapped")
        q_done, k_done, v_done, q_part, k_part, q_ready, k_ready, v_ready = (
            sem("b_" + n) for n in ("q_done", "k_done", "v_done", "q_part", "k_part", "q_ready", "k_ready",
                                    "v_ready"))
        s_done, s_min, p_exp, p_inv, p_ready, pT_done, pT_ready, c_done, c_ready, o_done, o_added = (
            sem("b_" + n) for n in ("s_done", "s_min", "p_exp", "p_inv", "p_ready", "pT_done", "pT_ready",
                                    "c_done", "c_ready", "o_done", "o_added"))
        t_dve, t_msd, t_rms, an_ready, anT_done, anT_ready, anT_saved, lg_done, lg_ready, ex_ready, g_ready, \
            gT_done, gT_ready, g3_ready, g3T_done, g3T_saved, b2_done = (
                sem("t_" + n) for n in ("dve", "ms", "rms", "an_ready", "anT_done", "anT_ready", "anT_saved",
                                        "lg_done", "lg_ready", "ex_ready", "g_ready", "gT_done", "gT_ready",
                                        "g3_ready", "g3T_done", "g3T_saved", "b2_done"))
        TD = 19
        base_link = sem("t_base_link")
        w1_in = [sem("c_w1_0"), sem("c_w1_1")]
        y_out = [sem("c_stored0"), sem("c_stored1")]
        hd_done, gb_done, gelu_done, hg_ready, y_part, y_done, y_link, y_ready = (
            sem("c_" + n) for n in ("hid_done", "gate_done", "gelu_done", "hg_ready", "y_part", "y_done",
                                    "y_link", "y_ready"))

        x_dram = a["x"].rearrange("b (t p) d -> p (b t) d", p=P)
        out_dram = out.rearrange("b (t p) d -> p (b t) d", p=P)

        @block.sync
        def _(sp):
            sp.dma_start(c_t[:], a["c_t"]).then_inc(ld_mod, 16)
            sp.dma_start(wmod[:], a["wmod"]).then_inc(ld_mod, 16)
            sp.dma_start(const[:], a["const"]).then_inc(ld_const, 16)
            sp.dma_start(rows[:], a["rows"]).then_inc(ld_const, 16)
            sp.dma_start(cols[:], a["cols"]).then_inc(ld_const, 16)
            sp.dma_start(sel_src[:], a["sel"]).then_inc(ld_const, 16)
            for h in range(2):
                sp.dma_start(x_all[:, h * NT // 2:(h + 1) * NT // 2, :],
                             x_dram[:, h * NT // 2:(h + 1) * NT // 2, :]).then_inc(ld_x, 16)
            sp.dma_start(wa_qkv[:], a["wa_qkv"]).then_inc(ld_wa, 16)
            sp.dma_start(wa_out[:], a["wa_out"]).then_inc(ld_wa, 16)
            sp.dma_start(omega_bd[:], a["omega_bd"]).then_inc(ld_wa, 16)
            sp.dma_start(wqkvb[:], a["wqkvb"]).then_inc(ld_wb, 16)
            sp.dma_start(wo[:], a["wo"]).then_inc(ld_wb, 16)
            sp.dma_start(wr[:], a["wr"]).then_inc(ld_wb, 16)
            sp.dma_start(b2[:], a["b2"]).then_inc(ld_wb, 16)
            sp.wait_ge(ld_wb, 64)
            phase_end(sp, a_done)
            sp.wait_ge(a_done, 5)
            sp.dma_start(w1_all[:], a["w1"]).then_inc(ld_w1, 16)
            def stage(u, par):
                sp.dma_start(x_st[:, par, :], slab_x[:, bass.ds(u // PAIR * SEQ, SEQ)]).then_inc(st_in[par], 16)
                sp.dma_start(w_st[:, par], wqkvb[:, bass.ds(u % PAIR, 1)].squeeze(1)).then_inc(st_in[par], 16)

            def swap(u):
                sp.wait_ge(raw_saved, u * 2 + 2)
                for k in range(4):
                    sp.dma_start(raw[32 * k:32 * k + 32, 1::2, :],
                                 raw[32 * (k ^ 1):32 * (k ^ 1) + 32, 0::2, :]).then_inc(swapped, 16)

            def step(u, par):
                sp.wait_ge(v_done, u + 2)
                stage(u + 3, 1 - par)
                swap(u + 2)

            stage(0, 0)
            stage(1, 1)
            swap(0)
            sp.wait_ge(v_done, 1)
            stage(2, 0)
            swap(1)
            with sp.Fori(0, UNITS // 2 - 2) as i:
                step(i * 2, 0)
                step(i * 2 + 1, 1)
            step(UNITS - 4, 0)
            swap(UNITS - 1)
            phase_end(sp, b_done)
            sp.wait_ge(b_done, 5)
            sp.dma_start(slab_k[:], a["w2"]).then_inc(ld_w2, 16)
            sp.wait_ge(t_done_all, 4)
            sp.wait_ge(ld_w1, 16)
            for e in range(2):
                sp.dma_start(w1_st[:, e, :], w1_all[:, e * P:(e + 1) * P]).then_inc(w1_in[e], 16)
            with sp.Fori(0, NB // 2) as bp:
                with sp.Fori(1, NE // 2) as e2:
                    for ee in range(2):
                        sp.wait_ge(hd_done, bp * (2 * NE) + e2 * 4 + (ee * 2 - 2))
                        sp.dma_start(w1_st[:, ee, :], w1_all[:, bass.ds((e2 * 2 + ee) * P, P)]).then_inc(w1_in[ee], 16)
                for ee in range(2):
                    sp.wait_ge(hd_done, bp * (2 * NE) + (2 * NE - 2 + ee * 2))
                    sp.dma_start(w1_st[:, ee, :], w1_all[:, ee * P:(ee + 1) * P]).then_inc(w1_in[ee], 16)
                for bb in range(2):
                    sp.wait_ge(y_ready, bp * 2 + (bb + 1))
                    sp.dma_start(out_dram[:, bass.ds(bp * (2 * TB) + bb * TB, TB), :], y_sb[:, bb]).then_inc(y_out[bb], 16)
            for bb in range(2):
                sp.wait_ge(y_out[bb], 16 * (NB // 2) + 16)
            for ee in range(2):
                sp.wait_ge(w1_in[ee], 16 * (NB // 2 * (NE // 2) + 1))

        @block.gpsimd
        def _(pool):
            nc.gpsimd.memset(state[:], 0.0).then_inc(st_ready, 2)
            nc.gpsimd.memset(v_one[:], 0.0).then_inc(su_pool, 1)
            pool.wait_ge(su_pool, 1)
            nc.gpsimd.memset(v_one[:, :, AHD:AHD + 1], 1.0).then_inc(su_pool, 1)
            nc.gpsimd.memset(zeros_bf[:], 0.0).then_inc(su_pool, 1)
            nc.gpsimd.memset(eps_col, 1e-5).then_inc(su_pool, 1)
            pool.wait_ge(ld_x, 32)
            pool.wait_ge(ld_const, 64)
            pool.wait_ge(su_modfix, 1)
            with pool.Fori(0, NB) as g:
                pool.wait_ge(h_ready, g + 1)
                ga = mod_all[:, bass.ds(g, 1), 2, :].squeeze(1)
                nc.gpsimd.tensor_tensor(gabout[:], ga, rows[:, R_BOUT:R_BOUT + D], ALU.mult).then_inc(x_plus, 1)
                pool.wait_ge(x_plus, g * 2 + 1)
                xg = x_all[:, bass.ds(g * TB, TB), :]
                nc.gpsimd.tensor_tensor(xg, xg, gabout[:].unsqueeze(1).to_broadcast([P, TB, D]), ALU.add).then_inc(x_plus, 1)
                pool.wait_ge(x_plus, g * 2 + 2)
                pool.wait_ge(qkv_ready, g + 1)
                nc.gpsimd.tensor_copy(v_all[:, bass.ds(g * TB, TB), :], qkv[:, :, 2 * D:3 * D]).then_inc(v_saved, 1)

            def set_v(i):
                vt = v_all[:, bass.ds(i, 1), :].rearrange("p o (h d) -> p (o h) d", h=AH)
                nc.gpsimd.tensor_copy(v_one[:, :, 0:AHD], vt).then_inc(v_set, 1)

            pool.wait_ge(v_saved, NB)
            pool.wait_ge(su_dve, SU_STEPS)
            set_v(0)
            with pool.Fori(1, NT) as i:
                pool.wait_ge(st_done, i * 2)
                set_v(i)
            with pool.Fori(0, NB) as g:
                pool.wait_ge(xn_ready, g + 1)
                nc.gpsimd.tensor_tensor(ao_all[:, bass.ds(g * TB, TB), :], xn_tok[:],
                                        rows[:, R_OB:R_OB + D].unsqueeze(1).to_broadcast([P, TB, D]),
                                        ALU.add).then_inc(ao_set, 1)
            phase_end(pool, a_done)
            pool.wait_ge(a_done, 5)
            def add_parts(which, u, par, first=False):
                if not first:
                    pool.wait_ge(s_done, u * 8 - 8)
                pool.wait_ge((q_part, k_part)[which], u + 1)
                nc.gpsimd.tensor_tensor((q_rot, k_rot)[which][:, par, :], part[:, 2 * which, :],
                                        part[:, 2 * which + 1, :], ALU.add).then_inc((q_ready, k_ready)[which], 1)

            for u in range(2):
                for which in range(2):
                    add_parts(which, u, u, True)
            with pool.Fori(1, UNITS // 2) as i:
                for par in range(2):
                    for which in range(2):
                        add_parts(which, i * 2 + par, par)
            phase_end(pool, b_done)
            pool.wait_ge(b_done, 5)
            with pool.Fori(0, NB) as b:
                pool.wait_ge(anT_ready, b + 1)
                nc.gpsimd.tensor_copy(slab_x[:, bass.ds(b * SEQ, SEQ)], an_t[:]).then_inc(anT_saved, 1)
            phase_end(pool, t_done_all)

        @block.scalar
        def _(act):
            act.wait_ge(ld_mod, 32)
            nc.scalar.activation(c_e[:], c_t[:], ACT.Exp, scale=-1.0).then_inc(su_exp, 1)
            for n in range(2 * NB):
                b, half = divmod(n, 2)
                act.wait_ge(su_mod_mm, n + 1)
                nc.scalar.activation(mod_all[:, b, 3 * half:3 * half + 3, :],
                                     bank[n % 8][:, 0:3 * D].rearrange("p (k d) -> p k d", k=3),
                                     ACT.Copy).then_inc(su_mod_ev, 1)
            act.wait_ge(su_dve, SU_COS)
            nc.scalar.activation(rope[:, 2, :], rope[:, 2, :], ACT.Sin).then_inc(su_sin, 1)
            nc.scalar.activation(rope[:, 3, :], rope[:, 3, :], ACT.Sin).then_inc(su_sin, 1)
            act.wait_ge(su_dve, SU_NODE)
            nc.scalar.activation(root2s, root2s, ACT.Sqrt).then_inc(su_sin, 1)
            act.wait_ge(su_pool, 4)
            def save_h(g):
                act.wait_ge(ln_var, g + 1)
                nc.scalar.activation(std[:], mv[:, :, 1], ACT.Sqrt, bias=eps_col).then_inc(ln_std, 1)
                act.wait_ge(hT_done, g + 1)
                nc.scalar.activation(h_t[:], bank[0][:], ACT.Copy).then_inc(hT_ready, 1)

            def norms(g):
                act.wait_ge(ss_ready, g + 1)
                nc.scalar.activation(ss[:], ss[:], ACT.Sqrt).then_inc(nrm_ready, 1)

            def save_qk(g):
                for n, slab in enumerate((slab_q, slab_k)):
                    act.wait_ge(qknT_done, g * 2 + (n + 1))
                    nc.scalar.activation(slab[:, bass.ds(g * SEQ, SEQ)], bank[5 + n][:], ACT.Copy).then_inc(qknT_saved, 1)

            save_h(0)
            with act.Fori(0, NB - 1) as g:
                norms(g)
                save_h(g + 1)
                save_qk(g)
            norms(NB - 1)
            save_qk(NB - 1)

            def exps(u, j):
                for n, f in enumerate((kf, qf)):
                    act.wait_ge(min_done, 2 * u + (n + 1))
                    nc.scalar.activation(f[:, j], f[:, j], ACT.Exp, bias=neg_s).then_inc(exp_done, 1)

            def a2_tile(i, first, last):
                for j in range(HALF):
                    u = i * HALF + j
                    act.wait_ge(kT_done, u + 1)
                    nc.scalar.activation(kf_tok[:, j].rearrange("p a b -> p (a b)"), bank[2][:],
                                         ACT.Copy).then_inc(kT_ready, 1)
                    if j == 0 and not first:
                        project(i - 1)
                    if j == 0 or not last:
                        exps(u + 1, 1 - j)

            def project(i):
                act.wait_ge(attT_done, i + 1)
                nc.scalar.activation(att_t[:], bank[6][:, 0:P], ACT.Copy).then_inc(attT_ready, 1)

            act.wait_ge(su_dve, SU_STEPS)
            act.wait_ge(su_sin, 3)
            act.wait_ge(v_saved, NB)
            exps(0, 0)
            a2_tile(0, True, False)
            with act.Fori(1, NT - 1) as i:
                a2_tile(i, False, False)
            a2_tile(NT - 1, False, True)
            project(NT - 1)
            with act.Fori(0, NB) as g:
                act.wait_ge(a3_var, g + 1)
                nc.scalar.activation(std[:], mv[:, :, 1], ACT.Sqrt, bias=eps_col).then_inc(a3_std, 1)
                act.wait_ge(a3_ms, g + 1)
                nc.scalar.activation(ms[:], ms[:], ACT.Sqrt, bias=eps_col).then_inc(a3_rms, 1)
                act.wait_ge(xnT_done, g + 1)
                nc.scalar.activation(slab_x[:, bass.ds(g * SEQ, SEQ)], bank[0][:], ACT.Copy).then_inc(xnT_saved, 1)
            phase_end(act, a_done)
            act.wait_ge(a_done, 5)
            def exp_p(u, t):
                for h in range(2):
                    s = t % 2 * 2 + h
                    act.wait_ge(s_min, 8 * u + 2 * t + h + 3)
                    pr = prob[:, s, 0:(t + 1) * P]
                    nc.scalar.activation(pr, pr, ACT.Exp, bias=low[:, s:s + 1], scale=-1.0,
                                         accum_out=rsum[:, s:s + 1]).then_inc(p_exp, 1)

            def save_pt(u, t):
                for h in range(2):
                    act.wait_ge(pT_done, 8 * u + 2 * t + h + 5)
                    nc.scalar.activation(pt[:, h, 0:t + 1, t * P:(t + 1) * P],
                                         bank[5 + h][:, 0:(t + 1) * P].rearrange("p (k q) -> p k q", q=P),
                                         ACT.Copy).then_inc(pT_ready, 1)

            def save_v(u, par):
                act.wait_ge(v_done, u + 1)
                nc.scalar.activation(v_sb[:, par].rearrange("p a b -> p (a b)"), bank[2][:],
                                     ACT.Copy).then_inc(v_ready, 1)

            def save_ctx(u):
                wait_apart(act, c_done, u + 1)
                nc.scalar.activation(ctx_t[:], bank[7][:], ACT.Identity, bias=bias_qkv[:, bass.ds(u % PAIR, 1), 2]
                                     ).then_inc(c_ready, 1)

            def save_raw(u, first=False):
                for n in range(2):
                    if not first:
                        act.wait_ge((q_part, k_part)[n], u)
                    wait_apart(act, (q_done, k_done)[n], u + 1)
                    nc.scalar.activation(raw[:, 2 * n, :], bank[n][:], ACT.Identity,
                                         bias=bias_qkv[:, bass.ds(u % PAIR, 1), n]).then_inc(raw_saved, 1)

            def unit(u, par, first=False, last=False, projects=True):
                exp_p(u, 0)
                if not first:
                    save_pt(u - 1, 3)
                exp_p(u, 1)
                if not first:
                    save_ctx(u - 1)
                if not last:
                    save_v(u + 1, 1 - par)
                save_pt(u, 0)
                exp_p(u, 2)
                if projects:
                    save_raw(u + 2)
                save_pt(u, 1)
                exp_p(u, 3)
                save_pt(u, 2)

            save_raw(0, True)
            save_v(0, 0)
            save_raw(1)
            unit(0, 0, first=True)
            with act.Fori(0, UNITS // 2 - 2) as i:
                unit(i * 2 + 1, 1)
                unit(i * 2 + 2, 0)
            unit(UNITS - 3, 1)
            unit(UNITS - 2, 0, projects=False)
            unit(UNITS - 1, 1, last=True, projects=False)
            save_pt(UNITS - 1, 3)
            save_ctx(UNITS - 1)
            phase_end(act, b_done)
            act.wait_ge(b_done, 5)
            with act.Fori(0, NB) as b:
                act.wait_ge(t_msd, b + 1)
                nc.scalar.activation(t_ms[:], t_ms[:], ACT.Sqrt, bias=eps_col, scale=1.0 / D).then_inc(t_rms, 1)
                act.wait_ge(anT_done, b + 1)
                nc.scalar.activation(an_t[:], bank[0][:], ACT.Copy).then_inc(anT_ready, 1)
                act.wait_ge(lg_ready, b + 1)
                nc.scalar.activation(logit[:], logit[:], ACT.Exp).then_inc(ex_ready, 1)
                act.wait_ge(gT_done, b + 1)
                nc.scalar.activation(gates_t[:], bank[3][0:NE, :], ACT.Copy).then_inc(gT_ready, 1)
                act.wait_ge(g3T_done, b + 1)
                nc.scalar.activation(gates3_all[:, bass.ds(b * SEQ, SEQ)], bank[4][0:3 * NE, 0:SEQ // 2].bitcast(BF16),
                                     ACT.Copy).then_inc(g3T_saved, 1)
            phase_end(act, t_done_all)
            act.wait_ge(t_done_all, 4)
            nc.scalar.activation(c_dummy[:], eps_col, ACT.Gelu)
            with act.Fori(0, NB // 2) as bp:
                with act.Fori(0, NE) as e:
                    for bb in range(2):
                        wait_apart(act, hd_done, bp * (2 * NE) + e * 2 + (bb + 1))
                        nc.scalar.activation(hid[:, bb, :], bank[bb][:], ACT.Gelu,
                                             bias=cols[:, bass.ds(K_B1 + e, 1)]).then_inc(gelu_done, 1)

        @block.tensor
        def _(pe):
            def mm(o, l, r, start=True, stop=True, **kw):
                return nc.tensor.matmul(o, l, r, start=start, stop=stop, **kw)

            pe.wait_ge(su_dve, 3)
            for n in range(2 * NB):
                b, half = divmod(n, 2)
                if n >= 8:
                    pe.wait_ge(su_mod_ev, n - 7)
                mm(bank[n % 8][:, 0:3 * D], sil[:, b:b + 1].to_broadcast([P, P]),
                   wmod[:, 3 * D * half:3 * D * (half + 1)]).then_inc(su_mod_mm, 1)
            pe.wait_ge(su_mod_ev, 2 * NB)
            pe.wait_ge(ld_wa, 48)
            def turn_h(g):
                pe.wait_ge(h_ready, g + 1)
                for t in range(TB):
                    m = nc.tensor.transpose(bank[0][:, t * P:(t + 1) * P], hrow[:, t, :], ident)
                m.then_inc(hT_done, 1)

            def make_qkv(g):
                pe.wait_ge(hT_ready, g + 1)
                for t in range(TB):
                    mm(bank[1 + t][:, 0:3 * D], h_t[:, t * P:(t + 1) * P], wa_qkv[:]).then_inc(qkv_done, 1)

            def turn_qk(g):
                pe.wait_ge(qkn_ready, g + 1)
                for n in range(2):
                    for t in range(TB):
                        m = nc.tensor.transpose(bank[5 + n][:, t * P:(t + 1) * P], qkn[:, t, n * D:(n + 1) * D], ident)
                    m.then_inc(qknT_done, 1)

            turn_h(0)
            make_qkv(0)
            with pe.Fori(0, NB - 1) as g:
                turn_h(g + 1)
                turn_qk(g)
                make_qkv(g + 1)
            turn_qk(NB - 1)

            def feats(i, j):
                for n, src in enumerate((slab_k, slab_q)):
                    for c in range(HP):
                        p = j * HP + c
                        m = mm(bank[n][:, c * P:(c + 1) * P], omega_bd[:, p * P:(p + 1) * P],
                               src[:, bass.ds(i * P, P)])
                    m.then_inc(feat_done, 1)

            def a2_tile(i, first, last):
                for j in range(HALF):
                    u = i * HALF + j
                    pe.wait_ge(kf_ready, u + 1)
                    for c in range(HP):
                        m = nc.tensor.transpose(bank[2][:, c * P:(c + 1) * P], kf[:, j, c, :], ident)
                    m.then_inc(kT_done, 1)
                    pe.wait_ge(qw_ready, u + 1)
                    for par in range(2):
                        rs = slice(64 * par, 64 * par + 64)
                        for c in range(HP):
                            m = mm(bank[3 + par][:, c * P:(c + 1) * P], kf[rs, j, c, :], qf[rs, j, c, :])
                        m.then_inc(aw_done, 1)
                    if j == 0 and not first:
                        turn_att(i - 1)
                    if j == 0:
                        feats(i, 1)
                    elif not last:
                        feats(i + 1, 0)
                    pe.wait_ge(v_set, i + 1)
                    pe.wait_ge(st_ready, u + 1)
                    pe.wait_ge(aw_ready, 2 * u + 2)
                    wait_apart(pe, att_ready, u + 1)
                    for slot in range(2):
                        for g in range(4):
                            h = slot * 4 + g
                            c, par = divmod(h, 2)
                            rs = slice(64 * par, 64 * par + 64)
                            mm(bank[5][32 * g:32 * g + 32, slot * P:(slot + 1) * P], state[rs, j * HP + c, :],
                               qf[rs, j, c, :], stop=False)
                        for g in range(4):
                            h = slot * 4 + g
                            c, par = divmod(h, 2)
                            m = mm(bank[5][32 * g:32 * g + 32, slot * P:(slot + 1) * P], v_one[:, j * HH + h, :],
                                   att_w[:, j, par, c, :], start=False)
                    m.then_inc(oT_done, 1)
                    pe.wait_ge(kT_ready, u + 1)
                    pe.wait_ge(st_ready, u + 2)
                    for c in range(HP):
                        h = j * HH + 2 * c
                        m = mm(bank[7][:, c * 18:(c + 1) * 18], kf_tok[:, j, c, :], v_one[:, h:h + 2, 0:9])
                    m.then_inc(st_done, 1)
                    if j == 0 and not first:
                        project(i - 1)
                    pe.wait_ge(oT_ready, u + 1)
                    for slot in range(2):
                        m = nc.tensor.transpose(bank[5][:, (2 + slot) * P:(3 + slot) * P],
                                                o_t[:, slot * P:(slot + 1) * P], ident)
                    m.then_inc(o2_done, 1)

            def turn_att(i):
                pe.wait_ge(att_ready, i * 2 + 3)
                pe.wait_ge(x1_done, i + 1)
                nc.tensor.transpose(bank[6][:, 0:P], att[:], ident).then_inc(attT_done, 1)

            def project(i):
                pe.wait_ge(attT_ready, i + 1)
                mm(bank[6][:, P:2 * P], att_t[:], wa_out[:]).then_inc(wo_done, 1)

            pe.wait_ge(qknT_saved, 2 * NB)
            feats(0, 0)
            a2_tile(0, True, False)
            with pe.Fori(1, NT - 1) as i:
                a2_tile(i, False, False)
            a2_tile(NT - 1, False, True)
            turn_att(NT - 1)
            project(NT - 1)
            with pe.Fori(0, NB) as g:
                pe.wait_ge(xn_ready, g + 1)
                for t in range(TB):
                    m = nc.tensor.transpose(bank[0][:, t * P:(t + 1) * P], xn_tok[:, t, :], ident)
                m.then_inc(xnT_done, 1)
            phase_end(pe, a_done)
            pe.wait_ge(a_done, 5)
            pe.wait_ge(ld_wb, 64)

            def project_qk(u, par, uh, first=False):
                pe.wait_ge(st_in[par], uh * 32 + 32)
                if not first:
                    pe.wait_ge(raw_saved, u * 2)
                for n, done in enumerate((q_done, k_done)):
                    mm(bank[n][:], w_st[:, par, n, :], x_st[:, par, :]).then_inc(done, 1)

            def project_v(u, par, first=False):
                if not first:
                    pe.wait_ge(v_ready, u)
                    pe.wait_ge(o_added, u - 1)
                for t in range(TB):
                    m = mm(bank[2][:, t * P:(t + 1) * P], x_st[:, par, t * P:(t + 1) * P], w_st[:, par, 2, :])
                m.then_inc(v_done, 1)

            def scores(u, par, t):
                for h in range(2):
                    pe.wait_ge(s_min, 8 * u + 2 * t + h + 1)
                    rs = slice(64 * h, 64 * h + 64)
                    mm(bank[3 + h][:, 0:(t + 1) * P], q_rot[rs, par, t * P:(t + 1) * P],
                       k_rot[rs, par, 0:(t + 1) * P]).then_inc(s_done, 1)

            def turn(u, t):
                for h in range(2):
                    pe.wait_ge(p_ready, 8 * u + 2 * t + h + 1)
                    pe.wait_ge(pT_ready, 8 * u + 2 * t + h + 1)
                    for k in range(t + 1):
                        m = nc.tensor.transpose(bank[5 + h][:, k * P:(k + 1) * P],
                                                prob[:, t % 2 * 2 + h, k * P:(k + 1) * P], ident)
                    m.then_inc(pT_done, 1)

            def context(u, par):
                pe.wait_ge(v_ready, u + 1)
                pe.wait_ge(pT_ready, 8 * u + 10)
                pe.wait_ge(c_ready, u + 1)
                for k in range(TB):
                    for h in range(2):
                        m = mm(bank[7][64 * h:64 * h + 64, k * P:SEQ], v_sb[:, par, k, 64 * h:64 * h + 64],
                               pt[:, h, k, k * P:SEQ], start=k == 0, stop=k == TB - 1)
                m.then_inc(c_done, 1)

            def output(u, last=False):
                pe.wait_ge(c_ready, u + 2)
                if last:
                    pe.wait_ge(o_added, u + 1)
                else:
                    pe.wait_ge(v_ready, u + 3)
                for t in range(TB):
                    m = mm(bank[2][:, t * P:(t + 1) * P], ctx_t[:, t * P:(t + 1) * P],
                           wo[:, bass.ds(u % PAIR, 1), :].squeeze(1))
                m.then_inc(o_done, 1)

            def unit(u, par, uh_next=0, first=False, last=False, projects=True):
                q_and_k_ready(u)
                scores(u, par, 0)
                scores(u, par, 1)
                if not first:
                    turn(u - 1, 3)
                if not last:
                    project_v(u + 1, 1 - par)
                scores(u, par, 2)
                if not first:
                    context(u - 1, 1 - par)
                turn(u, 0)
                if projects:
                    project_qk(u + 2, par, uh_next)
                scores(u, par, 3)
                turn(u, 1)
                if not first:
                    output(u - 1, last)
                turn(u, 2)

            def q_and_k_ready(u):
                pe.wait_ge(q_ready, u + 1)
                pe.wait_ge(k_ready, u + 1)

            project_qk(0, 0, 0, True)
            project_v(0, 0, True)
            project_qk(1, 1, 0)
            unit(0, 0, 1, first=True)
            with pe.Fori(0, UNITS // 2 - 2) as i:
                unit(i * 2 + 1, 1, i + 1)
                unit(i * 2 + 2, 0, i + 2)
            unit(UNITS - 3, 1, UNITS // 2 - 1)
            unit(UNITS - 2, 0, projects=False)
            unit(UNITS - 1, 1, last=True, projects=False)
            turn(UNITS - 1, 3)
            context(UNITS - 1, 1)
            output(UNITS - 1, True)
            phase_end(pe, b_done)
            pe.wait_ge(b_done, 5)
            with pe.Fori(0, NB) as b:
                pe.wait_ge(an_ready, b + 1)
                for t in range(TB):
                    m = nc.tensor.transpose(bank[0][:, t * P:(t + 1) * P], an[:, t, :], ident)
                m.then_inc(anT_done, 1)
                pe.wait_ge(anT_ready, b + 1)
                for t in range(TB):
                    m = mm(bank[1][:, t * NE:t * NE + NE - 1], an_t[:, t * P:(t + 1) * P], wr[:])
                m.then_inc(lg_done, 1)
                pe.wait_ge(g_ready, b + 1)
                for t in range(TB):
                    m = nc.tensor.transpose(bank[3][0:NE, t * P:(t + 1) * P], gates[:, t, :], ident)
                m.then_inc(gT_done, 1)
                pe.wait_ge(g3_ready, b + 1)
                for t in range(TB):
                    m = nc.tensor.transpose(bank[4][0:3 * NE, t * P // 2:(t + 1) * P // 2].bitcast(BF16),
                                            gates3[:, t, :], ident_bf[:])
                m.then_inc(g3T_done, 1)
                pe.wait_ge(gT_ready, b + 1)
                for t in range(TB):
                    m = mm(bank[2][:, t * P:(t + 1) * P], gates_t[:, t * P:(t + 1) * P], b2[:])
                m.then_inc(b2_done, 1)
            phase_end(pe, t_done_all)
            pe.wait_ge(t_done_all, 4)
            pe.wait_ge(ld_w2, 16)

            def up(bp, e, eh, ee, bb):
                n = bp * (2 * NE) + e * 2 + bb
                pe.wait_ge(w1_in[ee], bp * (16 * NE // 2) + eh * 16 + 16)
                pe.wait_ge(gelu_done, n + 1)
                pe.wait_ge(hg_ready, n + 1)
                mm(bank[bb][:], w1_st[:, ee, :], slab_x[:, bass.ds(bp * (2 * SEQ) + bb * SEQ, SEQ)]).then_inc(hd_done, 1)
                mm(bank[2 + bb][:], one(sel_all, e),
                   gates3_all[:, bass.ds(bp * (2 * SEQ) + bb * SEQ, SEQ)]).then_inc(gb_done, 1)

            def down(bp, e, bb):
                n = bp * (2 * NE) + e * 2 + bb
                pe.wait_ge(hg_ready, n + 3)
                for t in range(TB):
                    m = mm(bank[4 + bb][:, t * P:(t + 1) * P], hid_g[:, bb, t * P:(t + 1) * P],
                           one(w2_all, e), start=False, stop=False, skip_group_check=True)
                m.then_inc(y_part, 1)

            with pe.Fori(0, NB // 2) as bp:
                for bb in range(2):
                    pe.wait_ge(y_link, bp * 2 + (bb + 1))
                    mm(bank[4 + bb][:], zeros_bf[:, 0:P], zeros_bf[:], stop=False, skip_group_check=True)
                up(bp, 0, 0, 0, 0)
                up(bp, 0, 0, 0, 1)
                with pe.Fori(0, NE // 2 - 1) as e2:
                    for ee in range(2):
                        for bb in range(2):
                            down(bp, e2 * 2 + ee, bb)
                            up(bp, e2 * 2 + (ee + 1), e2 + (ee + 1) // 2, 1 - ee, bb)
                for bb in range(2):
                    down(bp, NE - 2, bb)
                    up(bp, NE - 1, NE // 2 - 1, 1, bb)
                for bb in range(2):
                    down(bp, NE - 1, bb)
                    mm(bank[4 + bb][:], zeros_bf[:, 0:P], zeros_bf[:], start=False, skip_group_check=True).then_inc(y_done, 1)

        @block.vector
        def _(dve):
            v = nc.vector

            def link(ins, s, at):
                ins.then_inc(s, 1)
                dve.wait_ge(s, at)

            dve.wait_ge(ld_mod, 32)
            dve.wait_ge(su_exp, 1)
            link(v.tensor_scalar(c_e[:], c_e[:], 1.0, None, ALU.add), su_dve, 1)
            link(v.reciprocal(c_e[:], c_e[:]), su_dve, 2)
            link(v.tensor_tensor(sil[:], c_t[:], c_e[:], ALU.mult), su_dve, 3)
            dve.wait_ge(ld_const, 64)
            link(v.tensor_scalar(ang, const[:, C_IOTA:C_IOTA + SEQ], cols[:, K_THETA:K_THETA + 1], None, ALU.mult), su_dve, 4)
            n = 4
            for k, quarter in ((2, 0.25), (3, 0.0)):
                r = rope[:, k, :]
                for src, s1, s2, o0, o1 in ((ang, 1 / (2 * np.pi), quarter, ALU.mult, ALU.add),
                                            (turns, ROUND, ROUND, ALU.add, ALU.subtract)):
                    n += 1
                    link(v.tensor_scalar(turns, src, float(s1), float(s2), o0, o1), su_dve, n)
                for w, part_2pi in enumerate(TWO_PI):
                    n += 1
                    link(v.scalar_tensor_tensor(r, turns, -part_2pi, ang if w == 0 else r, ALU.mult, ALU.add), su_dve, n)
                n += 1
                link(v.tensor_scalar(r, r, float(2 * np.pi * quarter), PI_UNDER, ALU.add, ALU.min), su_dve, n)
                n += 1
                link(v.tensor_scalar(r, r, -PI_UNDER, None, ALU.max), su_dve, n)
            assert n == SU_COS
            link(v.tensor_scalar(root2s, cols[:, K_NODE:K_NODE + 1], 0.0, 2.0, ALU.max, ALU.mult), su_dve, SU_NODE)
            link(v.tensor_scalar(neg_s, cols[:, K_NODE:K_NODE + 1], -1.0, None, ALU.mult), su_dve, SU_NODE + 1)
            link(v.tensor_scalar(wfeat, cols[:, K_WEIGHT:K_WEIGHT + 1], 0.0, 1.0 / 32, ALU.max, ALU.mult), su_dve, SU_NODE + 2)
            link(v.tensor_scalar(top, cols[:, K_NODE:K_NODE + 1], CLIP, None, ALU.add), su_dve, SU_NODE + 3)
            v.tensor_copy(ident_bf[:], ident)
            dve.wait_ge(su_sin, 2)
            link(v.tensor_scalar(rope[:, 3, :], rope[:, 3, :], const[:, C_SIGN:C_SIGN + 1], None, ALU.mult), su_dve, SU_NODE + 4)
            link(v.tensor_scalar(rope[:, 0:2, :], rope[:, 2:4, :], -0.125, None, ALU.mult), su_dve, SU_STEPS)
            dve.wait_ge(su_mod_ev, 2 * NB)
            v.tensor_scalar(mod_all[:, :, 1, :], mod_all[:, :, 1, :], 1.0, None, ALU.add)
            v.tensor_scalar(mod_all[:, :, 4, :], mod_all[:, :, 4, :], 1.0, None, ALU.add)
            sg = qkv[:].rearrange("p t d -> p (t d)")[:, 0:NB * D].rearrange("p (b d) -> p b d", d=D)
            mg = sq.rearrange("p t d -> p (t d)")[:, 0:NB * D].rearrange("p (b d) -> p b d", d=D)
            for w, k in enumerate((2, 5)):
                g = mod_all[:, :, k, :]
                link(v.tensor_scalar(sg, g, 0.0, 2.0, ALU.is_ge, ALU.mult), su_dve, SU_STEPS + 5 * w + 1)
                link(v.tensor_scalar(sg, sg, 1.0, None, ALU.subtract), su_dve, SU_STEPS + 5 * w + 2)
                link(v.scalar_tensor_tensor(mg, g, -1.0, g, ALU.mult, ALU.max), su_dve, SU_STEPS + 5 * w + 3)
                link(v.tensor_scalar(mg, mg, 0.25, None, ALU.max), su_dve, SU_STEPS + 5 * w + 4)
                link(v.tensor_tensor(g, mg, sg, ALU.mult), su_dve, SU_STEPS + 5 * w + 5)
            v.engine_nop().then_inc(su_modfix, 1)

            def layer_norm(g, chain, per, var, stdsem, shift, scale1):
                for t in range(TB):
                    m = v.bn_stats(stats[:, t, :], x_all[:, bass.ds(g * TB + t, 1), :].squeeze(1))
                m.then_inc(chain, 1)
                wait_apart(dve, chain, g * per + 1)
                for t in range(TB):
                    m = v.bn_aggr(mv[:, t, :], stats[:, t, :])
                m.then_inc(var, 1)
                dve.wait_ge(stdsem, g + 1)
                link(v.reciprocal(std[:], std[:]), chain, g * per + 2)
                for t in range(TB):
                    m = v.tensor_scalar(hrow[:, t, :], x_all[:, bass.ds(g * TB + t, 1), :].squeeze(1),
                                        mv[:, t, 0:1], std[:, t:t + 1], ALU.subtract, ALU.mult)
                link(m, chain, g * per + 3)
                link(v.tensor_tensor(hrow[:], hrow[:], mod_all[:, bass.ds(g, 1), scale1, :].to_broadcast([P, TB, D]),
                                     ALU.mult), chain, g * per + 4)
                return v.tensor_tensor(hrow[:], hrow[:], mod_all[:, bass.ds(g, 1), shift, :].to_broadcast([P, TB, D]), ALU.add)

            dve.wait_ge(ld_x, 32)
            def make_h(g):
                layer_norm(g, a1_dve, A1D, ln_var, ln_std, 0, 1).then_inc(h_ready, 1)

            qk = qkv[:, :, 0:2 * D]

            def save_qkv(g):
                for t in range(TB):
                    dve.wait_ge(qkv_done, g * TB + (t + 1))
                    m = v.tensor_tensor(qkv[:, t, :], bank[1 + t][:, 0:3 * D], rows[:, R_BQKV:R_BQKV + 3 * D], ALU.add)
                m.then_inc(qkv_ready, 1)
                dve.wait_ge(qkv_ready, g + 1)
                link(v.tensor_tensor(sq, qk, qk, ALU.mult), qk_link, g * 3 + 1)
                link(v.tensor_reduce(ss[:], sq.rearrange("p t (h d) -> p t h d", d=AHD), AX, ALU.add), qk_link, g * 3 + 2)
                v.tensor_scalar(ss[:], ss[:], 1e-24, None, ALU.max).then_inc(ss_ready, 1)

            def unit_qk(g):
                dve.wait_ge(nrm_ready, g + 1)
                link(v.reciprocal(ss[:], ss[:]), qk_link, g * 3 + 3)
                v.tensor_tensor(qkn.rearrange("p t (h d) -> p t h d", d=AHD), qk.rearrange("p t (h d) -> p t h d", d=AHD),
                                ss[:].unsqueeze(3).to_broadcast([P, TB, 2 * AH, AHD]), ALU.mult).then_inc(qkn_ready, 1)
                dve.wait_ge(v_saved, g + 1)
                dve.wait_ge(qkn_ready, g + 1)

            make_h(0)
            with dve.Fori(0, NB - 1) as g:
                save_qkv(g)
                make_h(g + 1)
                unit_qk(g)
            save_qkv(NB - 1)
            unit_qk(NB - 1)

            dve.sem_inc(att_ready, 1)
            dve.sem_inc(x1_done, 1)
            dve.wait_ge(v_saved, NB)
            dve.wait_ge(su_sin, 3)

            def clip_above(u, j):
                for n, f in enumerate((kf, qf)):
                    dve.wait_ge(feat_done, 2 * u + (n + 1))
                    v.tensor_scalar(f[:, j], bank[n][:].rearrange("p (c q) -> p c q", q=P), root2s, top,
                                    ALU.mult, ALU.min).then_inc(min_done, 1)

            def clip_below(u, j):
                dve.wait_ge(exp_done, 2 * u + 1)
                v.tensor_scalar(kf[:, j], kf[:, j], EXP_LOW, None, ALU.max).then_inc(kf_ready, 1)
                dve.wait_ge(exp_done, 2 * u + 2)
                v.tensor_scalar(qf[:, j], qf[:, j], EXP_LOW, wfeat, ALU.max, ALU.mult).then_inc(qw_ready, 1)

            def residual(i):
                dve.wait_ge(wo_done, i + 1)
                ga = mod_all[:, bass.ds(i // TB, 1), 2, :].squeeze(1)
                link(v.tensor_tensor(proj_tmp[:], bank[6][:, P:2 * P], ga, ALU.mult), x1_link, i + 1)
                xi = x_all[:, bass.ds(i, 1), :].squeeze(1)
                v.tensor_tensor(xi, xi, proj_tmp[:], ALU.add).then_inc(x1_done, 1)

            def a2_tile(i, first, last):
                for j in range(HALF):
                    u = i * HALF + j
                    for par in range(2):
                        dve.wait_ge(aw_done, 2 * u + (par + 1))
                        v.tensor_tensor(att_w[:, j, par], bank[3 + par][:].rearrange("p (c q) -> p c q", q=P),
                                        mask_a.unsqueeze(1).to_broadcast([P, HP, P]), ALU.mult).then_inc(aw_ready, 1)
                    if j == 0 or not last:
                        clip_above(u + 1, 1 - j)
                    dve.wait_ge(oT_done, u + 1)
                    v.tensor_copy(o_t[:], bank[5][:, 0:2 * P]).then_inc(oT_ready, 1)
                    dve.wait_ge(st_done, u + 1)
                    new = bank[7][:, 0:HP * 18].rearrange("p (c k) -> p c k", k=18)
                    for par in range(2):
                        rs = slice(64 * par, 64 * par + 64)
                        s = state[rs, j * HP:(j + 1) * HP, 0:9]
                        m = v.tensor_tensor(s, s, new[rs, :, 9 * par:9 * par + 9], ALU.add)
                    link(m, st_link, u + 1)
                    s = state[:, j * HP:(j + 1) * HP, 0:9]
                    v.tensor_scalar(s, s, const[:, bass.ds(C_KEEP + i, 1)], None, ALU.mult).then_inc(st_ready, 1)
                    if j == 0 or not last:
                        clip_below(u + 1, 1 - j)
                    if j == 0 and not first:
                        residual(i - 1)
                    if j == 0 and not first:
                        dve.wait_ge(attT_done, i)
                    dve.wait_ge(o2_done, u + 1)
                    o2 = bank[5][:, 2 * P:4 * P].rearrange("p (h k) -> p h k", k=32)
                    link(v.tensor_scalar(den[:], o2[:, :, AHD], 1e-6, None, ALU.max), att_link, 2 * u + 1)
                    link(v.reciprocal(den[:], den[:]), att_link, 2 * u + 2)
                    v.tensor_tensor(att[:, j * HH * AHD:(j + 1) * HH * AHD].rearrange("p (h d) -> p h d", d=AHD),
                                    o2[:, :, 0:AHD], den[:].unsqueeze(2).to_broadcast([P, HH, AHD]),
                                    ALU.mult).then_inc(att_ready, 1)

            clip_above(0, 0)
            clip_below(0, 0)
            a2_tile(0, True, False)
            with dve.Fori(1, NT - 1) as i:
                a2_tile(i, False, False)
            a2_tile(NT - 1, False, True)
            residual(NT - 1)
            dve.wait_ge(x1_done, NT + 1)
            with dve.Fori(0, NB) as g:
                link(layer_norm(g, a3_dve, A3D, a3_var, a3_std, 3, 4), a3_dve, g * A3D + 5)
                for t in range(TB):
                    m = v.tensor_tensor_reduce(out=sq[:, t, 0:D], in0=hrow[:, t, :], in1=hrow[:, t, :], scale=1.0 / D,
                                               scalar=0.0, op0=ALU.mult, op1=ALU.add, accum_out=ms[:, t:t + 1])
                m.then_inc(a3_ms, 1)
                dve.wait_ge(a3_rms, g + 1)
                link(v.reciprocal(ms[:], ms[:]), a3_inv, g + 1)
                for t in range(TB):
                    m = v.scalar_tensor_tensor(xn_tok[:, t, :], hrow[:, t, :], ms[:, t:t + 1], rows[:, R_G1:R_G1 + D],
                                               ALU.mult, ALU.mult)
                m.then_inc(xn_ready, 1)
                dve.wait_ge(xnT_done, g + 1)
                dve.wait_ge(ao_set, g + 1)
            phase_end(dve, a_done)
            dve.wait_ge(a_done, 5)
            dve.sem_inc(s_min, 2)
            dve.sem_inc(o_added, 1)
            dve.sem_inc(pT_ready, 2)
            dve.sem_inc(c_ready, 1)
            dve.sem_inc(pT_done, 4)

            def rotate(which, u, first=False):
                dve.wait_ge(swapped, u * 64 + 64)
                if not first:
                    dve.wait_ge((q_ready, k_ready)[which], u)
                k = slice(2 * which, 2 * which + 2)
                v.tensor_tensor(part[:, k, :], raw[:, k, :], rope[:, k, :], ALU.mult).then_inc(
                    (q_part, k_part)[which], 1)

            def minimum(u, t):
                for h in range(2):
                    s = t % 2 * 2 + h
                    dve.wait_ge(s_done, 8 * u + 2 * t + h + 1)
                    wait_apart(dve, pT_done, 8 * u + 2 * t + h + 1)
                    n = (t + 1) * P
                    v.tensor_tensor_reduce(out=prob[:, s, 0:n], in0=bank[3 + h][:, 0:n], in1=mask_b[:, SEQ - n:SEQ],
                                           scale=1.0, scalar=3e38, op0=ALU.add, op1=ALU.min,
                                           accum_out=low[:, s:s + 1]).then_inc(s_min, 1)

            def invert(u, t):
                dve.wait_ge(p_exp, 8 * u + 2 * t + 2)
                s = t % 2 * 2
                v.reciprocal(rinv[:, s:s + 2], rsum[:, s:s + 2]).then_inc(p_inv, 1)
                dve.wait_ge(p_inv, 4 * u + t + 1)
                for h in range(2):
                    pr = prob[:, s + h, 0:(t + 1) * P]
                    v.tensor_scalar(pr, pr, rinv[:, s + h:s + h + 1], None, ALU.mult).then_inc(p_ready, 1)

            def add_output(u):
                dve.wait_ge(o_done, u + 1)
                d = ao_all[:, bass.ds(u // PAIR * TB, TB), :]
                v.tensor_tensor(d, d, bank[2][:].rearrange("p (t d) -> p t d", d=D), ALU.add).then_inc(o_added, 1)

            def unit(u, par, first, last):
                minimum(u, 0)
                if not first:
                    invert(u - 1, 3)
                minimum(u, 1)
                invert(u, 0)
                if not last:
                    rotate(0, u + 1)
                invert(u, 1)
                minimum(u, 2)
                if not last:
                    rotate(1, u + 1)
                invert(u, 2)
                minimum(u, 3)
                if not first:
                    add_output(u - 1)

            rotate(0, 0, True)
            rotate(1, 0, True)
            unit(0, 0, True, False)
            with dve.Fori(0, UNITS // 2 - 1) as i:
                unit(i * 2 + 1, 1, False, False)
                unit(i * 2 + 2, 0, False, False)
            unit(UNITS - 1, 1, False, True)
            invert(UNITS - 1, 3)
            add_output(UNITS - 1)
            phase_end(dve, b_done)
            dve.wait_ge(b_done, 5)
            v.memset(gates[:, :, NE - 1:NE], 1.0)
            v.tensor_copy(sel_all, sel_src[:].unsqueeze(2).to_broadcast([3 * NE, NE, P]))
            with dve.Fori(0, NB) as b:
                base = b * TD
                ao_b = ao_all[:, bass.ds(b * TB, TB), :]
                ao_t = [ao_all[:, bass.ds(b * TB + t, 1), :].squeeze(1) for t in range(TB)]
                link(v.tensor_tensor(t_tmp[:], ao_b, ao_b, ALU.mult), t_dve, base + 1)
                v.tensor_reduce(t_ms[:], t_tmp[:], AX, ALU.add).then_inc(t_msd, 1)
                dve.wait_ge(t_rms, b + 1)
                link(v.reciprocal(t_ms[:], t_ms[:]), t_dve, base + 2)
                for t in range(TB):
                    m = v.scalar_tensor_tensor(an[:, t, :], ao_t[t], t_ms[:, t:t + 1], rows[:, R_G2:R_G2 + D],
                                               ALU.mult, ALU.mult)
                m.then_inc(an_ready, 1)
                dve.wait_ge(lg_done, b + 1)
                link(v.tensor_tensor(logit[:], bank[1][:, 0:TB * NE].rearrange("p (t e) -> p t e", e=NE)[:, :, 0:NE - 1],
                                     rows[:, R_RB:R_RB + NE - 1].unsqueeze(1).to_broadcast([P, TB, NE - 1]), ALU.add),
                     t_dve, base + 3)
                link(v.tensor_reduce(red[:], logit[:], AX, ALU.max), t_dve, base + 4)
                v.tensor_tensor(logit[:], logit[:], red[:].unsqueeze(2).to_broadcast([P, TB, NE - 1]),
                                ALU.subtract).then_inc(lg_ready, 1)
                dve.wait_ge(ex_ready, b + 1)
                link(v.tensor_reduce(red[:], logit[:], AX, ALU.add), t_dve, base + 5)
                link(v.reciprocal(red[:], red[:]), t_dve, base + 6)
                link(v.tensor_tensor(aff[:], logit[:], red[:].unsqueeze(2).to_broadcast([P, TB, NE - 1]), ALU.mult),
                     t_dve, base + 7)
                dve.nop(nofuse=True)
                for t in range(TB):
                    m = v.max(top8[:, t, :], aff[:, t, :])
                m.then_inc(t_dve, 1)
                wait_apart(dve, t_dve, base + 8)
                for t in range(TB):
                    m = v.max_index(idx8[:, t, :], top8[:, t, :], aff[:, t, :])
                link(m, t_dve, base + 9)
                link(v.tensor_copy(idxf[:], idx8[:, :, 0:TOPK]), t_dve, base + 10)
                for t in range(TB):
                    m = v.tensor_tensor(onehot[:, t],
                                        const[:, C_EIOTA:C_EIOTA + NE - 1].unsqueeze(1).to_broadcast([P, TOPK, NE - 1]),
                                        idxf[:, t, :].unsqueeze(2).to_broadcast([P, TOPK, NE - 1]), ALU.is_equal)
                link(m, t_dve, base + 11)
                link(v.tensor_tensor(chosen[:], onehot[:, :, 0, :], onehot[:, :, 1, :], ALU.add), t_dve, base + 12)
                link(v.tensor_tensor(chosen[:], chosen[:], onehot[:, :, 2, :], ALU.add), t_dve, base + 13)
                v.tensor_tensor(gates[:, :, 0:NE - 1], aff[:], chosen[:], ALU.mult).then_inc(g_ready, 1)
                dve.wait_ge(g_ready, b + 1)
                g3 = [gates3[:, :, k * NE:(k + 1) * NE] for k in range(3)]
                link(v.tensor_copy(g3[0], gates[:]), t_dve, base + 14)
                link(v.tensor_tensor(rest[:], gates[:], g3[0], ALU.subtract), t_dve, base + 15)
                link(v.tensor_copy(g3[1], rest[:]), t_dve, base + 16)
                link(v.tensor_tensor(rest[:], rest[:], g3[1], ALU.subtract), t_dve, base + 17)
                v.tensor_copy(g3[2], rest[:]).then_inc(g3_ready, 1)
                link(v.tensor_tensor(t_tmp[:], ao_b, an[:], ALU.add), t_dve, base + 18)
                dve.wait_ge(b2_done, b + 1)
                link(v.tensor_tensor(t_tmp[:], t_tmp[:], bank[2][:].rearrange("p (t d) -> p t d", d=D), ALU.add),
                     t_dve, base + 19)
                v.tensor_tensor(t_tmp[:], t_tmp[:], mod_all[:, bass.ds(b, 1), 5, :].to_broadcast([P, TB, D]),
                                ALU.mult).then_inc(base_link, 1)
                dve.wait_ge(base_link, b * 2 + 1)
                xb = x_all[:, bass.ds(b * TB, TB), :]
                link(v.tensor_tensor(xb, xb, t_tmp[:], ALU.add), base_link, b * 2 + 2)
                dve.wait_ge(anT_saved, b + 1)
            phase_end(dve, t_done_all)
            dve.wait_ge(t_done_all, 4)
            dve.sem_inc(hg_ready, 2)
            dve.sem_inc(gelu_done, 2)
            for bb in range(2):
                dve.sem_inc(y_out[bb], 16)
            dve.sem_inc(y_link, 2)
            with dve.Fori(0, NB // 2) as bp:
                with dve.Fori(0, NE) as e:
                    for bb in range(2):
                        n = bp * (2 * NE) + e * 2 + bb
                        dve.wait_ge(gelu_done, n + 3)
                        dve.wait_ge(gb_done, n + 1)
                        v.tensor_tensor(hid_g[:, bb, :], hid[:, bb, :], bank[2 + bb][:], ALU.mult).then_inc(hg_ready, 1)
                for bb in range(2):
                    dve.wait_ge(y_done, bp * 2 + (bb + 1))
                    dve.wait_ge(y_out[bb], bp * 16 + 16)
                    v.tensor_tensor(y_sb[:, bb], bank[4 + bb][:].rearrange("p (t d) -> p t d", d=D),
                                    mod_all[:, bass.ds(bp * 2 + bb, 1), 5, :].to_broadcast([P, TB, D]),
                                    ALU.mult).then_inc(y_link, 1)
                    dve.wait_ge(y_link, bp * 2 + (bb + 3))
                    v.tensor_tensor(y_sb[:, bb], y_sb[:, bb], x_all[:, bass.ds(bp * (2 * TB) + bb * TB, TB), :],
                                    ALU.add).then_inc(y_ready, 1)


def constants():
    p = np.arange(P)
    c = np.zeros((P, C_END), np.float32)
    c[:, C_ID:C_ID + P] = np.eye(P)
    c[:, C_MASKA:C_MASKA + P] = p[:, None] <= p[None]
    c[:, C_MASKB + SEQ - P:C_MASKB + SEQ] = np.where(p[None] > p[:, None], BIG, 0)
    c[:, C_IOTA:C_IOTA + SEQ] = np.arange(SEQ)
    c[:, C_EIOTA:C_EIOTA + NE] = np.arange(NE)
    c[:, C_KEEP:C_KEEP + NT] = np.arange(NT) % TB != TB - 1
    c[:, C_SIGN] = np.where(p // 32 % 2 == 0, -1, 1)
    sel = (np.arange(3 * NE)[:, None] % NE == np.arange(NE)[None]).astype(np.float32)
    return c, sel


def kernel(**inputs):
    import concourse.bacc as bacc
    from concourse.bass_utils import run_bass_kernel_spmd

    x = {k[3:]: np.asarray(v) for k, v in inputs.items()}
    c, sel = constants()

    def every(row, n=P):
        return np.broadcast_to(row.reshape(1, -1), (n, row.size))

    def halves(w):
        return w.reshape(w.shape[0], PAIR, 2, 32, 2).transpose(0, 1, 2, 4, 3).reshape(w.shape[0], PAIR, P)

    rows = np.zeros((P, R_END), np.float32)
    for at, k in ((R_BQKV, "attn_bqkv"), (R_BOUT, "attn_bout"), (R_G1, "ffn_gamma1"), (R_G2, "ffn_gamma2"),
                  (R_OB, "ffn_o_b"), (R_RB, "ffn_router_b")):
        rows[:, at:at + x[k].size] = every(x[k])
    cols = np.zeros((P, K_END), np.float32)
    node = np.arange(P) // 32 % 2
    cols[:, K_NODE] = x["attn_quad_nodes"][node]
    cols[:, K_WEIGHT] = x["attn_quad_weights"][node]
    cols[:, K_THETA] = x["ffn_theta"][np.arange(P) % 32]
    bias = [halves(x["ffn_q_b"][None])[0], halves(x["ffn_k_b"][None])[0], x["ffn_v_b"].reshape(PAIR, P)]
    cols[:, K_QKV:K_QKV + PAIR * 3] = np.stack(bias, -1).transpose(1, 0, 2).reshape(P, -1)
    cols[:, K_B1:K_B1 + NE] = np.concatenate([x["ffn_re_b1"], x["ffn_sh_b1"][None]]).T
    omega = np.zeros((AH, AHD, AH, 2, 32), np.float32)
    for h in range(AH):
        omega[h, :, h] = x["attn_omega"][:, h].transpose(1, 0, 2)
    wqkvb = np.stack([halves(x["ffn_q_w"]), halves(x["ffn_k_w"]), x["ffn_v_w"].reshape(D, PAIR, P)], 2)
    arrays = {
        "x": x["attn_x"], "c_t": x["c"].T, "wmod": x["wmod"], "const": c, "sel": sel, "rows": rows, "cols": cols,
        "wa_qkv": x["attn_Wqkv"], "wa_out": x["attn_Wout"], "omega_bd": omega.reshape(P, -1),
        "wqkvb": wqkvb, "wo": x["ffn_o_w"].reshape(PAIR, P, D).transpose(1, 0, 2),
        "wr": x["ffn_router_w"], "b2": np.concatenate([x["ffn_re_b2"], x["ffn_sh_b2"][None]]),
        "w1": np.concatenate([x["ffn_re_w1"], x["ffn_sh_w1"][None]]).transpose(1, 0, 2).reshape(D, -1),
        "w2": np.concatenate([x["ffn_re_w2"], x["ffn_sh_w2"][None]]).transpose(1, 0, 2).reshape(P, -1),
    }
    nc = bacc.Bacc("TRN2", target_bir_lowering=False, num_devices=1)
    aps, given = {}, {}
    for name, v in arrays.items():
        v = np.ascontiguousarray(v)
        given[f"in_{name}"] = v
        aps[name] = nc.dram_tensor(f"in_{name}", v.shape, mybir.dt.from_np(v.dtype), kind="ExternalInput").ap()
    out = nc.dram_tensor("out_y", (NB, SEQ, D), F32, kind="ExternalOutput").ap()
    build_block(nc, aps, out)
    r = run_bass_kernel_spmd(nc, [given], core_ids=[0])
    return r.results[0]["out_y"]
```

```python
from contextlib import ExitStack

import numpy as np

import concourse.bass as bass
from concourse import mybir

F32 = mybir.dt.float32
BF16 = mybir.dt.bfloat16
U32 = mybir.dt.uint32
F32R = mybir.dt.float32r
ALU = mybir.AluOpType
ACT = mybir.ActivationFunctionType
AX = mybir.AxisListType.X

P = 128
D = 128
NB, SEQ = 8, 512
TB = SEQ // P
NT = NB * TB
TT = 2 * TB
AH, AHD = 16, 8
APAIR = AH // 2
HALF = 2
HP = APAIR // HALF
HH = AH // HALF
PAIR = 8
UNITS = NB * PAIR
NE = 32
TOPK = 3
CLIP = 20.0
EXP_LOW = float(np.exp(-CLIP))
SLOTS = 2 * NE
RING = 4
BIG = 1e30

C_ID, C_MASKA, C_MASKB, C_IOTA, C_EIOTA, C_KEEP, C_SIGN, C_END = np.cumsum(
    [0, P, P, SEQ, SEQ, NE, NT, 1]).tolist()
R_BQKV, R_BOUT, R_G1, R_G2, R_OB, R_RB, R_END = np.cumsum([0, 3 * D, D, D, D, D, NE]).tolist()
K_NODE, K_WEIGHT, K_THETA, K_QKV, K_B1, K_END = np.cumsum([0, 1, 1, 1, PAIR * 3, NE]).tolist()

SU_COS, SU_NODE, SU_MOD, SU_STEPS = 18, 19, 22, 34
ROUND = 12582912.0
_HI = 6.28125
_MID = float(np.uint32(int(np.float32(2 * np.pi - _HI).view(np.uint32)) & 0xFFFFF000).view(np.float32))
TWO_PI = (_HI, _MID, float(np.float32(2 * np.pi - _HI - _MID)))
PI_UNDER = 3.1415925



def one(t, i):
    return t[:, bass.ds(i, 1), :].squeeze(1)


def wait_apart(eng, sem, value):
    eng.wait_ge(sem, value)
    eng.nop(nofuse=True)


def build_block(nc, a, out):
    ctx = ExitStack()
    with ctx:
        def sb(name, shape, dt=F32, where=ctx):
            return where.enter_context(nc.sbuf_tensor(name, shape, dt))

        def sem(name):
            return ctx.enter_context(nc.semaphore(name))

        bank = [ctx.enter_context(nc.psum_tensor(f"bank{i}", [P, 512], F32)) for i in range(8)]

        x_all = sb("x_all", [P, NT, D])
        mod_all = sb("mod_all", [P, NB, 6, D])
        slab_q = sb("slab_q", [P, NT * P])
        slab_k = sb("slab_k", [P, NT * P])
        slab_v = sb("slab_v", [P, NT * D])
        slab_x = sb("slab_x", [P, NT * P])
        ao_all = sb("ao_all", [P, NT, D])
        const = sb("const", [P, C_END])
        rows = sb("rows", [P, R_END])
        cols = sb("cols", [P, K_END])
        sel_src = sb("sel_src", [3 * NE, NE])
        ident_bf = sb("ident_bf", [P, P], BF16)
        wr = sb("wr", [P, NE - 1])
        b2 = sb("b2", [NE, D])
        small = sb("small", [P, 8])

        ident = const[:, C_ID:C_ID + P]
        mask_a = const[:, C_MASKA:C_MASKA + P]
        mask_b = const[:, C_MASKB:C_MASKB + SEQ]
        root2s, neg_s, wfeat, eps_col = (small[:, i:i + 1] for i in range(4))
        top = small[:, 4:5]
        bias_qkv = cols[:, K_QKV:K_QKV + PAIR * 3].rearrange("p (a k) -> p a k", k=3)
        v_all = slab_v[:].rearrange("p (n d) -> p n d", d=D)
        pt = slab_v[:].rearrange("p (h k q) -> p h k q", h=2, k=TB)
        gates3_all = slab_v[0:3 * NE, 0:NT * P // 2].bitcast(BF16)
        sel_all = slab_v[0:3 * NE, NT * P // 2:NT * P].bitcast(BF16).rearrange("p (e m) -> p e m", e=NE)
        w1_all = slab_q[:].rearrange("p (e d) -> p e d", e=NE)
        w2_all = slab_k[:].rearrange("p (e d) -> p e d", e=NE)

        wab = ExitStack()
        wqkvb = sb("wqkvb", [P, PAIR, 3, P], where=wab)
        wo = sb("wo", [P, PAIR, D], where=wab)
        wa_qkv = sb("wa_qkv", [P, 3 * D], where=wab)
        wa_out = sb("wa_out", [P, D], where=wab)
        omega_bd = sb("omega_bd", [P, APAIR * P], where=wab)
        rope = sb("rope", [P, 4, SEQ], where=wab)

        wa = ExitStack()
        c_t = sb("c_t", [P, NB], where=wa)
        c_e = sb("c_e", [P, NB], where=wa)
        sil = sb("sil", [P, NB], where=wa)
        wmod = sb("wmod", [P, 6 * D], where=wa)
        angles = sb("angles", [P, 2, SEQ], where=wa)
        ang, turns = angles[:, 0], angles[:, 1]
        stats = sb("stats", [P, NT, 6], where=wa)
        mv = sb("mv", [P, NT, 2], where=wa)
        std = sb("std", [P, NT], where=wa)
        ms = sb("ms", [P, TT], where=wa)
        hrow = sb("hrow", [P, TT, D], where=wa)
        bias_hl = sb("bias_hl", [64, 3 * D], where=wa)
        thirty2nds = sb("thirty2nds", [64, P], where=wa)
        gabout = sb("gabout", [P, D], where=wa)
        h_t = sb("h_t", [P, SEQ], where=wa)
        qkv = sb("qkv", [P, TB, 3 * D], where=wa)
        sq_qkn = sb("sq_qkn", [P, 2, TB, 2 * D], where=wa)
        sq, qkn = sq_qkn[:, 0], sq_qkn[:, 1]
        ss = sb("ss", [P, TB, 2 * AH], where=wa)
        qf = qkv[:].rearrange("p t d -> p (t d)")[:, 0:HALF * HP * P].rearrange("p (j c q) -> p j c q", j=HALF, c=HP)
        kf = sb("kf", [P, HALF, HP, P], where=wa)
        kf_tok = angles[:].rearrange("p j (c f) -> p j c f", c=HP)
        v_one = sb("v_one", [P, AH, 32], where=wa)
        att_w = sq_qkn.rearrange("p j t d -> p (j t d)").rearrange("p (j r c q) -> p j r c q", j=HALF, r=2, c=HP)
        state = sb("state", [P, APAIR, 32], where=wa)
        o_t = sb("o_t", [P, 2 * P], where=wa)
        den = sb("den", [P, HH], where=wa)
        att = sb("att", [P, D], where=wa)
        att_t = sb("att_t", [P, P], where=wa)
        proj_tmp = sb("proj_tmp", [P, D], where=wa)
        xn_tok = qkn.rearrange("p t (k d) -> p (t k) d", d=D)
        wa.close()
        wb = ExitStack()
        x_st = slab_k[:, 0:2 * SEQ].rearrange("p (j q) -> p j q", j=2)
        w_st = slab_k[:, 2 * SEQ:2 * SEQ + 6 * P].rearrange("p (j k d) -> p j k d", j=2, k=3)
        raw = slab_k[:, 2 * SEQ + 6 * P:6 * SEQ + 6 * P].rearrange("p (k q) -> p k q", k=4)
        q_rot = sb("q_rot", [P, 2, SEQ], where=wb)
        k_rot = sb("k_rot", [P, 2, SEQ], where=wb)
        q_hl = sb("q_hl", [P, 2, 2, SEQ], where=wb)
        k_hl = sb("k_hl", [P, 2, 2, SEQ], where=wb)
        part = slab_q[:, 0:4 * SEQ].rearrange("p (k q) -> p k q", k=4)
        prob = slab_q[:, 4 * SEQ:8 * SEQ].rearrange("p (k q) -> p k q", k=4)
        low = sb("low", [P, 4], where=wb)
        rsum = sb("rsum", [P, 4], where=wb)
        rinv = sb("rinv", [P, 4], where=wb)
        v_sb = sb("v_sb", [P, 2, TB, P], where=wb)
        ctx_t = sb("ctx_t", [P, SEQ], where=wb)
        wb.close()
        wab.close()
        an_hi = sb("an_hi", [P, NT * P])
        an_lo = sb("an_lo", [P, NT * P])
        t_tmp = sb("t_tmp", [P, TT, D])
        wt = ExitStack()
        t_ms = sb("t_ms", [P, TT], where=wt)
        t_sq = sb("t_sq", [P, TT, D], where=wt)
        an = sb("an", [P, TT, D], where=wt)
        an_t = sb("an_t", [P, 2, SEQ], where=wt)
        logit = sb("logit", [P, TT, NE - 1], where=wt)
        aff = sb("aff", [P, TT, NE - 1], where=wt)
        red = sb("red", [P, TT], where=wt)
        top8 = sb("top8", [P, TT, 8], where=wt)
        idx8 = sb("idx8", [P, TT, 8], U32, where=wt)
        idxf = sb("idxf", [P, TT, TOPK], where=wt)
        onehot = sb("onehot", [P, TT, TOPK, NE - 1], where=wt)
        chosen = sb("chosen", [P, TT, NE - 1], where=wt)
        gates = sb("gates", [P, TT, NE], where=wt)
        rest = sb("rest", [P, TT, NE], where=wt)
        gates3 = sb("gates3", [P, TT, 3 * NE], BF16, where=wt)
        gates_t = sb("gates_t", [NE, 2, SEQ], where=wt)
        wt.close()
        wc = ExitStack()
        gelu_first = sb("gelu_first", [P, 1], where=wc)
        w1_hl = sb("w1_hl", [P, 2, 2, P], where=wc)
        w2_hl = sb("w2_hl", [P, 2, 2, P], where=wc)
        hid = sb("hid", [P, RING, SEQ], where=wc)
        hid_hi = sb("hid_hi", [P, RING, SEQ], where=wc)
        hid_lo = sb("hid_lo", [P, RING, SEQ], where=wc)
        yt_sb = sb("yt_sb", [P, 2, SEQ], where=wc)
        y_sb = sb("y_sb", [P, 2, TB, D], where=wc)
        wc.close()

        ld_const, ld_mod, ld_x, ld_wa, ld_wb, ld_w1, ld_w2 = (
            sem(n) for n in ("ld_const", "ld_mod", "ld_x", "ld_wa", "ld_wb", "ld_w1", "ld_w2"))
        su_exp, su_dve, su_mod_mm, su_mod_ev, su_sin, su_pool, su_modfix = (
            sem(n) for n in ("su_exp", "su_dve", "su_mod_mm", "su_mod_ev", "su_sin", "su_pool", "su_modfix"))
        a_done, b_done, t_done_all = sem("a_done"), sem("b_done"), sem("t_done_all")

        block = ctx.enter_context(nc.Block())

        def phase_end(eng, s):
            eng.drain().then_inc(s, 1)

        a1_dve, ln_var, ln_std, h_ready, hT_done, hT_ready, qkv_done, qkv_ready, ss_ready, nrm_ready, \
            qkn_ready, qknT_done, qknT_saved, x_plus, v_saved = (
                sem("a1_" + n) for n in ("dve", "ln_var", "ln_std", "h_ready", "hT_done", "hT_ready",
                                         "qkv_done", "qkv_ready", "ss_ready", "nrm_ready", "qkn_ready",
                                         "qknT_done", "qknT_saved", "x_plus", "v_saved"))
        v_set, feat_done, min_done, exp_done, kf_ready, qw_ready, kT_done, kT_ready, aw_done, aw_ready, oT_done, \
            oT_ready, st_done, st_link, st_ready, o2_done, att_link, att_ready, attT_done, attT_ready, \
            wo_done, x1_link, x1_done = (
                sem("a2_" + n) for n in ("v_set", "feat_done", "min_done", "exp_done", "kf_ready", "qw_ready", "kT_done",
                                         "kT_ready", "aw_done", "aw_ready", "oT_done", "oT_ready", "st_done",
                                         "st_link", "st_ready", "o2_done", "att_link", "att_ready",
                                         "attT_done", "attT_ready", "wo_done", "x1_link", "x1_done"))
        a3_dve, a3_var, a3_std, a3_ms, a3_rms, xn_ready, xnT_done, xnT_saved, ao_set = (
            sem("a3_" + n) for n in ("dve", "var", "std", "ms", "rms", "xn_ready", "xnT_done", "xnT_saved",
                                     "ao_set"))
        a3_inv, qk_link, sq_ready, bias_link = (
            sem("a3_inv"), sem("a1_qk_link"), sem("a1_sq_ready"), sem("a1_bias_link"))
        A3D = 5
        st_in = [sem("b_staged0"), sem("b_staged1")]
        raw_saved, swapped = sem("b_raw_saved"), sem("b_swapped")
        qk_hi, qk_lo = sem("b_qk_hi"), sem("b_qk_lo")
        q_done, k_done, v_done, q_part, k_part, q_ready, k_ready, v_ready = (
            sem("b_" + n) for n in ("q_done", "k_done", "v_done", "q_part", "k_part", "q_ready", "k_ready",
                                    "v_ready"))
        s_done, s_min, p_exp, p_inv, p_ready, pT_done, pT_ready, c_done, c_ready, o_done, o_added = (
            sem("b_" + n) for n in ("s_done", "s_min", "p_exp", "p_inv", "p_ready", "pT_done", "pT_ready",
                                    "c_done", "c_ready", "o_done", "o_added"))
        t_dve, t_msd, t_rms, an_ready, anT_done, anT_ready, anT_saved, lg_done, lg_ready, ex_ready, g_ready, \
            gT_done, gT_ready, g3_ready, g3T_done, g3T_saved, b2_done = (
                sem("t_" + n) for n in ("dve", "ms", "rms", "an_ready", "anT_done", "anT_ready", "anT_saved",
                                        "lg_done", "lg_ready", "ex_ready", "g_ready", "gT_done", "gT_ready",
                                        "g3_ready", "g3T_done", "g3T_saved", "b2_done"))
        TD = 15
        base_link, b2_added = sem("t_base_link"), sem("t_b2_added")
        y_out = [sem("c_stored0"), sem("c_stored1")]
        hd_done, gb_done, gelu_done, gated, hi_ready, lo_ready, w_hi, w1_ready, w2_ready = (
            sem("c_" + n) for n in ("hid_done", "gate_done", "gelu_done", "gated", "hi_ready", "lo_ready", "w_hi",
                                    "w1_ready", "w2_ready"))
        y_part, y_copied, y_turned, y_link, y_ready = (
            sem("c_" + n) for n in ("y_part", "y_copied", "y_turned", "y_link", "y_ready"))
        an_split, sum_link, an_link = sem("t_an_split"), sem("t_sum_link"), sem("t_an_link")

        x_dram = a["x"].rearrange("b (t p) d -> p (b t) d", p=P)
        out_dram = out.rearrange("b (t p) d -> p (b t) d", p=P)

        @block.sync
        def _(sp):
            sp.dma_start(c_t[:], a["c_t"]).then_inc(ld_mod, 16)
            sp.dma_start(wmod[:], a["wmod"]).then_inc(ld_mod, 16)
            sp.dma_start(const[:], a["const"]).then_inc(ld_const, 16)
            sp.dma_start(rows[:], a["rows"]).then_inc(ld_const, 16)
            sp.dma_start(cols[:], a["cols"]).then_inc(ld_const, 16)
            sp.dma_start(sel_src[:], a["sel"]).then_inc(ld_const, 16)
            for h in range(2):
                sp.dma_start(x_all[:, h * NT // 2:(h + 1) * NT // 2, :],
                             x_dram[:, h * NT // 2:(h + 1) * NT // 2, :]).then_inc(ld_x, 16)
            sp.dma_start(wa_qkv[:], a["wa_qkv"]).then_inc(ld_wa, 16)
            sp.dma_start(wa_out[:], a["wa_out"]).then_inc(ld_wa, 16)
            sp.dma_start(omega_bd[:], a["omega_bd"]).then_inc(ld_wa, 16)
            sp.dma_start(wqkvb[:], a["wqkvb"]).then_inc(ld_wb, 16)
            sp.dma_start(wo[:], a["wo"]).then_inc(ld_wb, 16)
            sp.dma_start(wr[:], a["wr"]).then_inc(ld_wb, 16)
            sp.dma_start(b2[:], a["b2"]).then_inc(ld_wb, 16)
            sp.wait_ge(ld_wb, 64)
            phase_end(sp, a_done)
            def stage(u, par):
                sp.dma_start(x_st[:, par, :], slab_x[:, bass.ds(u // PAIR * SEQ, SEQ)]).then_inc(st_in[par], 16)
                sp.dma_start(w_st[:, par], wqkvb[:, bass.ds(u % PAIR, 1)].squeeze(1)).then_inc(st_in[par], 16)

            def swap(u):
                sp.wait_ge(raw_saved, u * 2 + 2)
                for k in range(4):
                    sp.dma_start(raw[32 * k:32 * k + 32, 1::2, :],
                                 raw[32 * (k ^ 1):32 * (k ^ 1) + 32, 0::2, :]).then_inc(swapped, 16)

            def step(u, par):
                sp.wait_ge(v_done, u + 2)
                stage(u + 3, 1 - par)
                swap(u + 2)

            sp.wait_ge(xnT_saved, 4)
            stage(0, 0)
            stage(1, 1)
            swap(0)
            sp.wait_ge(v_done, 1)
            stage(2, 0)
            swap(1)
            with sp.Fori(0, UNITS // 2 - 2) as i:
                step(i * 2, 0)
                step(i * 2 + 1, 1)
            step(UNITS - 4, 0)
            swap(UNITS - 1)
            phase_end(sp, b_done)
            sp.wait_ge(b_done, 5)
            sp.dma_start(slab_q[:], a["w1"]).then_inc(ld_w1, 16)
            sp.dma_start(slab_k[:], a["w2"]).then_inc(ld_w2, 16)
            with sp.Fori(0, NB // 2) as bp:
                for bb in range(2):
                    sp.wait_ge(y_ready, bp * 2 + (bb + 1))
                    sp.dma_start(out_dram[:, bass.ds(bp * (2 * TB) + bb * TB, TB), :], y_sb[:, bb]).then_inc(y_out[bb], 16)
            for bb in range(2):
                sp.wait_ge(y_out[bb], 16 * (NB // 2) + 16)

        @block.gpsimd
        def _(pool):
            nc.gpsimd.memset(state[:], 0.0).then_inc(st_ready, 2)
            nc.gpsimd.memset(v_one[:], 0.0).then_inc(su_pool, 1)
            pool.wait_ge(su_pool, 1)
            nc.gpsimd.memset(v_one[:, :, AHD:AHD + 1], 1.0).then_inc(su_pool, 1)
            nc.gpsimd.memset(eps_col, 1e-5).then_inc(su_pool, 1)
            pool.wait_ge(ld_x, 32)
            pool.wait_ge(ld_const, 64)
            pool.wait_ge(su_modfix, 1)
            with pool.Fori(0, NB) as g:
                pool.wait_ge(h_ready, g + 1)
                ga = mod_all[:, bass.ds(g, 1), 2, :].squeeze(1)
                nc.gpsimd.tensor_tensor(gabout[:], ga, rows[:, R_BOUT:R_BOUT + D], ALU.mult).then_inc(x_plus, 1)
                pool.wait_ge(x_plus, g * 2 + 1)
                xg = x_all[:, bass.ds(g * TB, TB), :]
                nc.gpsimd.tensor_tensor(xg, xg, gabout[:].unsqueeze(1).to_broadcast([P, TB, D]), ALU.add).then_inc(x_plus, 1)
                pool.wait_ge(x_plus, g * 2 + 2)
                pool.wait_ge(qkv_ready, g + 1)
                nc.gpsimd.tensor_copy(v_all[:, bass.ds(g * TB, TB), :], qkv[:, :, 2 * D:3 * D]).then_inc(v_saved, 1)

            def set_v(i):
                vt = v_all[:, bass.ds(i, 1), :].rearrange("p o (h d) -> p (o h) d", h=AH)
                nc.gpsimd.tensor_copy(v_one[:, :, 0:AHD], vt).then_inc(v_set, 1)

            pool.wait_ge(v_saved, NB)
            pool.wait_ge(su_dve, SU_STEPS)
            set_v(0)
            with pool.Fori(1, NT) as i:
                pool.wait_ge(st_done, i * 2)
                set_v(i)
            with pool.Fori(0, NB // 2) as g:
                pool.wait_ge(xn_ready, g + 1)
                nc.gpsimd.tensor_tensor(ao_all[:, bass.ds(g * TT, TT), :], xn_tok,
                                        rows[:, R_OB:R_OB + D].unsqueeze(1).to_broadcast([P, TT, D]),
                                        ALU.add).then_inc(ao_set, 1)
            phase_end(pool, a_done)
            pool.wait_ge(a_done, 5)
            def add_parts(which, u, par, first=False):
                if not first:
                    pool.wait_ge(s_done, u * 8 - 8)
                pool.wait_ge((q_part, k_part)[which], u + 1)
                nc.gpsimd.tensor_tensor((q_rot, k_rot)[which][:, par, :], part[:, 2 * which, :],
                                        part[:, 2 * which + 1, :], ALU.add).then_inc((q_ready, k_ready)[which], 1)

            def low_part(which, u, par):
                pool.wait_ge(qk_hi, u * 2 + (which + 1))
                hl = (q_hl, k_hl)[which][:, par]
                nc.gpsimd.tensor_tensor(hl[:, 1].bitcast(F32R), (q_rot, k_rot)[which][:, par, :], hl[:, 0],
                                        ALU.subtract).then_inc(qk_lo, 1)

            def unit(u, par, first=False):
                for which in range(2):
                    add_parts(which, u, par, first)
                for which in range(2):
                    low_part(which, u, par)

            for u in range(2):
                unit(u, u, True)
            with pool.Fori(1, UNITS // 2) as i:
                for par in range(2):
                    unit(i * 2 + par, par)
            phase_end(pool, b_done)
            pool.wait_ge(b_done, 5)
            def split_an(b):
                pool.wait_ge(an_ready, b + 1)
                nc.gpsimd.tensor_tensor(t_tmp[:], ao_all[:, bass.ds(b * TT, TT), :], an[:], ALU.add).then_inc(sum_link, 1)
                pool.wait_ge(an_split, b + 1)
                nc.gpsimd.tensor_tensor(an_lo[:, bass.ds(b * 2 * SEQ, 2 * SEQ)].bitcast(F32R), an_t[:].rearrange("p j q -> p (j q)"),
                                        an_hi[:, bass.ds(b * 2 * SEQ, 2 * SEQ)],
                                        ALU.subtract).then_inc(anT_saved, 1)

            def residual(b):
                pool.wait_ge(b2_added, b * 2 + 2)
                for j in range(2):
                    tj = t_tmp[:, j * TB:(j + 1) * TB]
                    nc.gpsimd.tensor_tensor(tj, tj, mod_all[:, bass.ds(b * 2 + j, 1), 5, :].to_broadcast([P, TB, D]),
                                            ALU.mult).then_inc(base_link, 1)
                pool.wait_ge(base_link, b * 3 + 2)
                xb = x_all[:, bass.ds(b * TT, TT), :]
                nc.gpsimd.tensor_tensor(xb, xb, t_tmp[:], ALU.add).then_inc(base_link, 1)
                pool.wait_ge(base_link, b * 3 + 3)

            with pool.Fori(0, NB // 2 - 1) as b:
                split_an(b)
                residual(b)
            split_an(NB // 2 - 1)
            phase_end(pool, t_done_all)
            residual(NB // 2 - 1)
            pool.wait_ge(t_done_all, 4)

            def low_part(n, r):
                pool.wait_ge(hi_ready, n + 1)
                pool.wait_ge(y_part, n + 1)
                nc.gpsimd.tensor_tensor(hid_lo[:, r].bitcast(F32R), hid[:, r], hid_hi[:, r], ALU.subtract).then_inc(lo_ready, 1)

            with pool.Fori(0, NB // 2 * SLOTS // RING) as i:
                for r in range(RING):
                    low_part(i * RING + r, r)

        @block.scalar
        def _(act):
            act.wait_ge(ld_mod, 32)
            nc.scalar.activation(c_e[:], c_t[:], ACT.Exp, scale=-1.0).then_inc(su_exp, 1)
            for n in range(2 * NB):
                b, half = divmod(n, 2)
                act.wait_ge(su_mod_mm, n + 1)
                nc.scalar.activation(mod_all[:, b, 3 * half:3 * half + 3, :],
                                     bank[n % 8][:, 0:3 * D].rearrange("p (k d) -> p k d", k=3),
                                     ACT.Copy).then_inc(su_mod_ev, 1)
            act.wait_ge(su_dve, SU_COS)
            nc.scalar.activation(rope[:, 2, :], rope[:, 2, :], ACT.Sin).then_inc(su_sin, 1)
            nc.scalar.activation(rope[:, 3, :], rope[:, 3, :], ACT.Sin).then_inc(su_sin, 1)
            act.wait_ge(su_dve, SU_NODE)
            nc.scalar.activation(root2s, root2s, ACT.Sqrt).then_inc(su_sin, 1)
            act.wait_ge(su_pool, 3)
            act.wait_ge(ln_var, 1)
            nc.scalar.activation(std[:], mv[:, :, 1], ACT.Sqrt, bias=eps_col).then_inc(ln_std, 1)
            def save_h(g):
                act.wait_ge(hT_done, g + 1)
                nc.scalar.activation(h_t[:], bank[0][:], ACT.Copy).then_inc(hT_ready, 1)

            def save_qkv(g):
                for t in range(TB):
                    act.wait_ge(qkv_done, g * TB + (t + 1))
                    m = nc.scalar.activation(qkv[:, t, :], bank[1 + t][:, 0:3 * D], ACT.Copy)
                m.then_inc(qkv_ready, 1)
                act.wait_ge(qkv_ready, g + 1)
                nc.scalar.activation(sq, qkv[:, :, 0:2 * D], ACT.Square).then_inc(sq_ready, 1)

            def norms(g):
                act.wait_ge(ss_ready, g + 1)
                nc.scalar.activation(ss[:], ss[:], ACT.Sqrt).then_inc(nrm_ready, 1)

            def save_qk(g):
                for n, slab in enumerate((slab_q, slab_k)):
                    act.wait_ge(qknT_done, g * 2 + (n + 1))
                    nc.scalar.activation(slab[:, bass.ds(g * SEQ, SEQ)], bank[5 + n][:], ACT.Copy).then_inc(qknT_saved, 1)

            save_h(0)
            save_qkv(0)
            with act.Fori(0, NB - 1) as g:
                save_h(g + 1)
                norms(g)
                act.wait_ge(qkn_ready, g + 1)
                act.wait_ge(v_saved, g + 1)
                save_qkv(g + 1)
                save_qk(g)
            norms(NB - 1)
            save_qk(NB - 1)

            def exps(u, j):
                for n, f in enumerate((kf, qf)):
                    act.wait_ge(min_done, 2 * u + (n + 1))
                    nc.scalar.activation(f[:, j], f[:, j], ACT.Exp, bias=neg_s).then_inc(exp_done, 1)

            def a2_tile(i, first, last):
                for j in range(HALF):
                    u = i * HALF + j
                    act.wait_ge(kT_done, u + 1)
                    nc.scalar.activation(kf_tok[:, j].rearrange("p a b -> p (a b)"), bank[2][:],
                                         ACT.Copy).then_inc(kT_ready, 1)
                    if j == 0 and not first:
                        project(i - 1)
                    if j == 0 or not last:
                        exps(u + 1, 1 - j)

            def project(i):
                act.wait_ge(attT_done, i + 1)
                nc.scalar.activation(att_t[:], bank[6][:, 0:P], ACT.Copy).then_inc(attT_ready, 1)

            act.wait_ge(su_dve, SU_STEPS)
            act.wait_ge(su_sin, 3)
            act.wait_ge(v_saved, NB)
            exps(0, 0)
            a2_tile(0, True, False)
            with act.Fori(1, NT - 1) as i:
                a2_tile(i, False, False)
            a2_tile(NT - 1, False, True)
            project(NT - 1)
            def deviation(g):
                act.wait_ge(a3_var, g + 1)
                nc.scalar.activation(std[:, 0:TT], mv[:, 0:TT, 1], ACT.Sqrt, bias=eps_col).then_inc(a3_std, 1)

            deviation(0)
            with act.Fori(0, NB // 2) as g:
                act.wait_ge(a3_dve, g * A3D + 5)
                for t in range(TT):
                    m = nc.scalar.activation(sq.rearrange("p t (k d) -> p (t k) d", d=D)[:, t, :], hrow[:, t, :],
                                             ACT.Square, accum_out=ms[:, t:t + 1])
                m.then_inc(a3_ms, 1)
                act.wait_ge(a3_ms, g + 1)
                nc.scalar.activation(ms[:], ms[:], ACT.Sqrt, bias=eps_col, scale=1.0 / D).then_inc(a3_rms, 1)
                deviation(g + 1)
                for j in range(2):
                    act.wait_ge(xnT_done, g * 2 + (j + 3))
                    nc.scalar.activation(slab_x[:, bass.ds(g * (2 * SEQ) + j * SEQ, SEQ)], bank[j][:],
                                         ACT.Copy).then_inc(xnT_saved, 1)
            def exp_p(u, t):
                for h in range(2):
                    s = t % 2 * 2 + h
                    act.wait_ge(s_min, 8 * u + 2 * t + h + 3)
                    pr = prob[:, s, 0:(t + 1) * P]
                    nc.scalar.activation(pr, pr, ACT.Exp, bias=low[:, s:s + 1], scale=-1.0,
                                         accum_out=rsum[:, s:s + 1]).then_inc(p_exp, 1)

            def save_pt(u, t):
                for h in range(2):
                    act.wait_ge(pT_done, 8 * u + 2 * t + h + 5)
                    nc.scalar.activation(pt[:, h, 0:t + 1, t * P:(t + 1) * P],
                                         bank[5 + h][:, 0:(t + 1) * P].rearrange("p (k q) -> p k q", q=P),
                                         ACT.Copy).then_inc(pT_ready, 1)

            def save_v(u, par):
                act.wait_ge(v_done, u + 1)
                nc.scalar.activation(v_sb[:, par].rearrange("p a b -> p (a b)"), bank[2][:],
                                     ACT.Copy).then_inc(v_ready, 1)

            def save_ctx(u):
                wait_apart(act, c_done, u + 1)
                nc.scalar.activation(ctx_t[:], bank[7][:], ACT.Identity, bias=bias_qkv[:, bass.ds(u % PAIR, 1), 2]
                                     ).then_inc(c_ready, 1)

            def save_raw(u, first=False):
                for n in range(2):
                    if not first:
                        act.wait_ge((q_part, k_part)[n], u)
                    wait_apart(act, (q_done, k_done)[n], u + 1)
                    nc.scalar.activation(raw[:, 2 * n, :], bank[n][:], ACT.Identity,
                                         bias=bias_qkv[:, bass.ds(u % PAIR, 1), n]).then_inc(raw_saved, 1)

            def unit(u, par, first=False, last=False, projects=True):
                exp_p(u, 0)
                if not first:
                    save_pt(u - 1, 3)
                exp_p(u, 1)
                save_pt(u, 0)
                if not first:
                    save_ctx(u - 1)
                exp_p(u, 2)
                if projects:
                    save_raw(u + 2)
                if not last:
                    save_v(u + 1, 1 - par)
                save_pt(u, 1)
                exp_p(u, 3)
                save_pt(u, 2)

            save_raw(0, True)
            phase_end(act, a_done)
            act.wait_ge(a_done, 5)
            save_v(0, 0)
            save_raw(1)
            unit(0, 0, first=True)
            with act.Fori(0, UNITS // 2 - 2) as i:
                unit(i * 2 + 1, 1)
                unit(i * 2 + 2, 0)
            unit(UNITS - 3, 1)
            unit(UNITS - 2, 0, projects=False)
            unit(UNITS - 1, 1, last=True, projects=False)
            save_pt(UNITS - 1, 3)
            save_ctx(UNITS - 1)
            phase_end(act, b_done)
            act.wait_ge(b_done, 5)
            def norm(b, first=False):
                if not first:
                    act.wait_ge(an_ready, b)
                for t in range(TT):
                    m = nc.scalar.activation(t_sq[:, t, :], one(ao_all, b * TT + t), ACT.Square, accum_out=t_ms[:, t:t + 1])
                m.then_inc(t_msd, 1)
                act.wait_ge(t_msd, b + 1)
                nc.scalar.activation(t_ms[:], t_ms[:], ACT.Sqrt, bias=eps_col, scale=1.0 / D).then_inc(t_rms, 1)

            def save_an(b, first=False):
                if not first:
                    act.wait_ge(anT_saved, b)
                for j in range(2):
                    act.wait_ge(anT_done, b * 2 + (j + 1))
                    nc.scalar.activation(an_t[:, j], bank[j][:], ACT.Copy).then_inc(anT_ready, 1)

            def two_batches(b, last=False):
                act.wait_ge(lg_ready, b + 1)
                nc.scalar.activation(logit[:], logit[:], ACT.Exp).then_inc(ex_ready, 1)
                if not last:
                    norm(b + 1)
                for j in range(2):
                    act.wait_ge(gT_done, b * 2 + (j + 1))
                    nc.scalar.activation(gates_t[:, j], bank[3 + j][0:NE, :], ACT.Copy).then_inc(gT_ready, 1)
                act.wait_ge(g3T_done, b + 1)
                nc.scalar.activation(gates3_all[:, bass.ds(b * 2 * SEQ, 2 * SEQ)], bank[5][0:3 * NE, :].bitcast(BF16),
                                     ACT.Copy).then_inc(g3T_saved, 1)
                if not last:
                    save_an(b + 1)

            norm(0, True)
            save_an(0, True)
            with act.Fori(0, NB // 2 - 1) as b:
                two_batches(b)
            two_batches(NB // 2 - 1, True)
            phase_end(act, t_done_all)
            act.wait_ge(t_done_all, 4)
            nc.scalar.activation(gelu_first[:], eps_col, ACT.Gelu)

            def high_weights(parts, src):
                nc.scalar.activation(parts[:, 0].bitcast(F32R), src, ACT.Copy).then_inc(w_hi, 1)

            def gelu(n, e, r):
                if r % 2 == 0:
                    act.nop(nofuse=True)
                    high_weights(w1_hl[:, 1 - r // 2], one(w1_all, (e + 1) % NE))
                else:
                    wait_apart(act, y_part, n + 1)
                    high_weights(w2_hl[:, r // 2], one(w2_all, e))
                wait_apart(act, hd_done, n + 1)
                nc.scalar.activation(hid[:, r], bank[r % 2][:], ACT.Gelu,
                                     bias=cols[:, bass.ds(K_B1 + e, 1)]).then_inc(gelu_done, 1)

            def copy_y(bp, bb):
                act.wait_ge(y_part, bp * SLOTS + (SLOTS - 1 + bb + RING))
                act.wait_ge(y_turned, bp * 2 + (bb + 1))
                nc.scalar.activation(yt_sb[:, bb], bank[4 + bb][:], ACT.Copy).then_inc(y_copied, 1)

            def pair_of_batches(bp, first):
                for r in range(RING):
                    gelu(bp * SLOTS + r, r // 2, r)
                    if r in (1, 2) and not first:
                        copy_y(bp - 1, r - 1)
                with act.Fori(1, NE // 2) as e2:
                    for r in range(RING):
                        gelu(bp * SLOTS + e2 * RING + r, e2 * 2 + r // 2, r)

            act.wait_ge(ld_w1, 16)
            act.wait_ge(ld_w2, 16)
            high_weights(w1_hl[:, 0], w1_all[:, 0, :])
            pair_of_batches(0, True)
            with act.Fori(1, NB // 2) as bp:
                pair_of_batches(bp, False)
            for bb in range(2):
                copy_y(NB // 2 - 1, bb)

        @block.tensor
        def _(pe):
            def mm(o, l, r, start=True, stop=True, **kw):
                return nc.tensor.matmul(o, l, r, start=start, stop=stop, **kw)

            pe.wait_ge(su_dve, 3)
            for n in range(2 * NB):
                b, half = divmod(n, 2)
                if n >= 8:
                    pe.wait_ge(su_mod_ev, n - 7)
                mm(bank[n % 8][:, 0:3 * D], sil[:, b:b + 1].to_broadcast([P, P]),
                   wmod[:, 3 * D * half:3 * D * (half + 1)]).then_inc(su_mod_mm, 1)
            pe.wait_ge(su_mod_ev, 2 * NB)
            pe.wait_ge(ld_wa, 48)
            def turn_h(g):
                pe.wait_ge(h_ready, g + 1)
                for t in range(TB):
                    m = nc.tensor.transpose(bank[0][:, t * P:(t + 1) * P], hrow[:, t, :], ident)
                m.then_inc(hT_done, 1)

            def make_qkv(g):
                pe.wait_ge(hT_ready, g + 1)
                for t in range(TB):
                    out = bank[1 + t][:, 0:3 * D]
                    mm(out, thirty2nds[:].bitcast(F32R), bias_hl[:].bitcast(F32R), stop=False)
                    mm(out, h_t[:, t * P:(t + 1) * P], wa_qkv[:], start=False).then_inc(qkv_done, 1)

            def turn_qk(g):
                pe.wait_ge(qkn_ready, g + 1)
                for n in range(2):
                    for t in range(TB):
                        m = nc.tensor.transpose(bank[5 + n][:, t * P:(t + 1) * P], qkn[:, t, n * D:(n + 1) * D], ident)
                    m.then_inc(qknT_done, 1)

            turn_h(0)
            pe.wait_ge(bias_link, 2)
            make_qkv(0)
            with pe.Fori(0, NB - 1) as g:
                turn_h(g + 1)
                pe.wait_ge(qkv_ready, g + 1)
                make_qkv(g + 1)
                turn_qk(g)
            turn_qk(NB - 1)

            def feats(i, j):
                for n, src in enumerate((slab_k, slab_q)):
                    for c in range(HP):
                        p = j * HP + c
                        m = mm(bank[n][:, c * P:(c + 1) * P], omega_bd[:, p * P:(p + 1) * P],
                               src[:, bass.ds(i * P, P)])
                    m.then_inc(feat_done, 1)

            def a2_tile(i, first, last):
                for j in range(HALF):
                    u = i * HALF + j
                    pe.wait_ge(kf_ready, u + 1)
                    for c in range(HP):
                        m = nc.tensor.transpose(bank[2][:, c * P:(c + 1) * P], kf[:, j, c, :], ident)
                    m.then_inc(kT_done, 1)
                    pe.wait_ge(qw_ready, u + 1)
                    for par in range(2):
                        rs = slice(64 * par, 64 * par + 64)
                        for c in range(HP):
                            m = mm(bank[3 + par][:, c * P:(c + 1) * P], kf[rs, j, c, :], qf[rs, j, c, :])
                        m.then_inc(aw_done, 1)
                    if j == 0 and not first:
                        turn_att(i - 1)
                    if j == 0:
                        feats(i, 1)
                    elif not last:
                        feats(i + 1, 0)
                    pe.wait_ge(v_set, i + 1)
                    pe.wait_ge(st_ready, u + 1)
                    pe.wait_ge(aw_ready, 2 * u + 2)
                    wait_apart(pe, att_ready, u + 1)
                    for slot in range(2):
                        for g in range(4):
                            h = slot * 4 + g
                            c, par = divmod(h, 2)
                            rs = slice(64 * par, 64 * par + 64)
                            mm(bank[5][32 * g:32 * g + 32, slot * P:(slot + 1) * P], state[rs, j * HP + c, :],
                               qf[rs, j, c, :], stop=False)
                        for g in range(4):
                            h = slot * 4 + g
                            c, par = divmod(h, 2)
                            m = mm(bank[5][32 * g:32 * g + 32, slot * P:(slot + 1) * P], v_one[:, j * HH + h, :],
                                   att_w[:, j, par, c, :], start=False)
                    m.then_inc(oT_done, 1)
                    pe.wait_ge(kT_ready, u + 1)
                    pe.wait_ge(st_ready, u + 2)
                    for c in range(HP):
                        h = j * HH + 2 * c
                        m = mm(bank[7][:, c * 18:(c + 1) * 18], kf_tok[:, j, c, :], v_one[:, h:h + 2, 0:9])
                    m.then_inc(st_done, 1)
                    if j == 0 and not first:
                        project(i - 1)
                    pe.wait_ge(oT_ready, u + 1)
                    for slot in range(2):
                        m = nc.tensor.transpose(bank[5][:, (2 + slot) * P:(3 + slot) * P],
                                                o_t[:, slot * P:(slot + 1) * P], ident)
                    m.then_inc(o2_done, 1)

            def turn_att(i):
                pe.wait_ge(att_ready, i * 2 + 3)
                pe.wait_ge(x1_done, i + 1)
                nc.tensor.transpose(bank[6][:, 0:P], att[:], ident).then_inc(attT_done, 1)

            def project(i):
                pe.wait_ge(attT_ready, i + 1)
                mm(bank[6][:, P:2 * P], att_t[:], wa_out[:]).then_inc(wo_done, 1)

            pe.wait_ge(qknT_saved, 2 * NB)
            feats(0, 0)
            a2_tile(0, True, False)
            with pe.Fori(1, NT - 1) as i:
                a2_tile(i, False, False)
            a2_tile(NT - 1, False, True)
            turn_att(NT - 1)
            project(NT - 1)
            pe.sem_inc(xnT_saved, 2)
            with pe.Fori(0, NB // 2) as g:
                pe.wait_ge(xn_ready, g + 1)
                for j in range(2):
                    pe.wait_ge(xnT_saved, g * 2 + (j + 1))
                    for t in range(TB):
                        m = nc.tensor.transpose(bank[j][:, t * P:(t + 1) * P], xn_tok[:, j * TB + t, :], ident)
                    m.then_inc(xnT_done, 1)
            pe.wait_ge(ld_wb, 64)

            def project_qk(u, par, uh, first=False, added=0):
                pe.wait_ge(st_in[par], uh * 32 + 32)
                if not first:
                    pe.wait_ge(raw_saved, u * 2)
                if not isinstance(added, int) or added:
                    pe.wait_ge(o_added, added)
                for n, done in enumerate((q_done, k_done)):
                    mm(bank[n][:], w_st[:, par, n, :], x_st[:, par, :]).then_inc(done, 1)

            def project_v(u, par, first=False):
                if not first:
                    pe.wait_ge(v_ready, u)
                for t in range(TB):
                    m = mm(bank[2][:, t * P:(t + 1) * P], x_st[:, par, t * P:(t + 1) * P], w_st[:, par, 2, :])
                m.then_inc(v_done, 1)

            def scores(u, par, t):
                for h in range(2):
                    pe.wait_ge(s_min, 8 * u + 2 * t + h + 1)
                    rs = slice(64 * h, 64 * h + 64)
                    out = bank[3 + h][:, 0:(t + 1) * P]
                    if t == 0:
                        mm(out, q_rot[rs, par, 0:P], k_rot[rs, par, 0:P]).then_inc(s_done, 1)
                        continue
                    for n, (qp, kp) in enumerate(((0, 0), (0, 1), (1, 0))):
                        m = mm(out, q_hl[rs, par, qp, t * P:(t + 1) * P].bitcast(F32R),
                               k_hl[rs, par, kp, 0:(t + 1) * P].bitcast(F32R), start=n == 0, stop=n == 2)
                    m.then_inc(s_done, 1)

            def turn(u, t):
                for h in range(2):
                    pe.wait_ge(p_ready, 8 * u + 2 * t + h + 1)
                    pe.wait_ge(pT_ready, 8 * u + 2 * t + h + 1)
                    for k in range(t + 1):
                        m = nc.tensor.transpose(bank[5 + h][:, k * P:(k + 1) * P],
                                                prob[:, t % 2 * 2 + h, k * P:(k + 1) * P], ident)
                    m.then_inc(pT_done, 1)

            def context(u, par):
                pe.wait_ge(v_ready, u + 1)
                pe.wait_ge(pT_ready, 8 * u + 10)
                pe.wait_ge(c_ready, u + 1)
                for k in range(TB):
                    for h in range(2):
                        m = mm(bank[7][64 * h:64 * h + 64, k * P:SEQ], v_sb[:, par, k, 64 * h:64 * h + 64],
                               pt[:, h, k, k * P:SEQ], start=k == 0, stop=k == TB - 1)
                m.then_inc(c_done, 1)

            def output(u, last=False):
                pe.wait_ge(c_ready, u + 2)
                pe.wait_ge(raw_saved, 2 * UNITS if last else u * 2 + 7)
                pe.wait_ge(o_added, u + 1)
                for t in range(TB):
                    m = mm(bank[0][:, t * P:(t + 1) * P], ctx_t[:, t * P:(t + 1) * P],
                           wo[:, bass.ds(u % PAIR, 1), :].squeeze(1))
                m.then_inc(o_done, 1)

            def unit(u, par, uh_next=0, first=False, last=False, projects=True):
                q_and_k_ready(u)
                scores(u, par, 0)
                if not last:
                    project_v(u + 1, 1 - par)
                pe.wait_ge(qk_lo, u * 2 + 2)
                scores(u, par, 1)
                if not first:
                    turn(u - 1, 3)
                scores(u, par, 2)
                if not first:
                    context(u - 1, 1 - par)
                turn(u, 0)
                if projects:
                    project_qk(u + 2, par, uh_next, added=0 if first else u)
                scores(u, par, 3)
                turn(u, 1)
                if not first:
                    output(u - 1, not projects)
                turn(u, 2)

            def q_and_k_ready(u):
                pe.wait_ge(q_ready, u + 1)
                pe.wait_ge(k_ready, u + 1)

            pe.wait_ge(xnT_saved, NB + 2)
            project_qk(0, 0, 0, True)
            phase_end(pe, a_done)
            pe.wait_ge(a_done, 5)
            project_v(0, 0, True)
            project_qk(1, 1, 0)
            unit(0, 0, 1, first=True)
            with pe.Fori(0, UNITS // 2 - 2) as i:
                unit(i * 2 + 1, 1, i + 1)
                unit(i * 2 + 2, 0, i + 2)
            unit(UNITS - 3, 1, UNITS // 2 - 1)
            unit(UNITS - 2, 0, projects=False)
            unit(UNITS - 1, 1, last=True, projects=False)
            turn(UNITS - 1, 3)
            context(UNITS - 1, 1)
            output(UNITS - 1, True)
            phase_end(pe, b_done)
            pe.wait_ge(b_done, 5)
            def turn_an(b):
                pe.wait_ge(an_ready, b + 1)
                for j in range(2):
                    for t in range(TB):
                        m = nc.tensor.transpose(bank[j][:, t * P:(t + 1) * P], an[:, j * TB + t, :], ident)
                    m.then_inc(anT_done, 1)

            def two_batches(b, last=False):
                for j in range(2):
                    pe.wait_ge(anT_ready, b * 2 + (j + 1))
                    for t in range(TB):
                        at = (j * TB + t) * NE
                        m = mm(bank[2][:, at:at + NE - 1], an_t[:, j, t * P:(t + 1) * P], wr[:])
                m.then_inc(lg_done, 1)
                pe.wait_ge(g_ready, b + 1)
                for j in range(2):
                    for t in range(TB):
                        m = nc.tensor.transpose(bank[3 + j][0:NE, t * P:(t + 1) * P], gates[:, j * TB + t, :], ident)
                    m.then_inc(gT_done, 1)
                pe.wait_ge(g3_ready, b + 1)
                for t in range(TT):
                    m = nc.tensor.transpose(bank[5][0:3 * NE, t * P // 2:(t + 1) * P // 2].bitcast(BF16),
                                            gates3[:, t, :], ident_bf[:])
                m.then_inc(g3T_done, 1)
                for j in range(2):
                    pe.wait_ge(gT_ready, b * 2 + (j + 1))
                    for t in range(TB):
                        m = mm(bank[6 + j][:, t * P:(t + 1) * P], gates_t[:, j, t * P:(t + 1) * P], b2[:])
                    m.then_inc(b2_done, 1)
                if not last:
                    turn_an(b + 1)

            turn_an(0)
            with pe.Fori(0, NB // 2 - 1) as b:
                two_batches(b)
            two_batches(NB // 2 - 1, True)
            phase_end(pe, t_done_all)
            pe.wait_ge(t_done_all, 4)
            pe.wait_ge(ld_w2, 16)

            def up(bp, s):
                n, e = bp * SLOTS + s[0] * RING + s[1], s[1] // 2
                bb = s[1] % 2
                pe.wait_ge(w1_ready, bp * NE + s[0] * 2 + (e + 1))
                pe.wait_ge(gelu_done, n + 1)
                x_at = bass.ds(bp * (2 * SEQ) + bb * SEQ, SEQ)
                parts = ((0, an_hi), (1, an_hi), (0, an_lo))
                for k, (w, x) in enumerate(parts):
                    m = mm(bank[bb][:], w1_hl[:, e, w, :].bitcast(F32R), x[:, x_at].bitcast(F32R), start=k == 0, stop=k == 2)
                m.then_inc(hd_done, 1)
                pe.wait_ge(gated, n + 1)
                mm(bank[2 + bb][:], one(sel_all, s[0] * 2 + e), gates3_all[:, x_at]).then_inc(gb_done, 1)

            def down(bp, s, start=False, stop=False):
                n, e, r = bp * SLOTS + s[0] * RING + s[1], s[1] // 2, s[1]
                bb = r % 2
                pe.wait_ge(w2_ready, bp * NE + s[0] * 2 + (e + 1))
                pe.wait_ge(hi_ready, n + 1)
                if start:
                    pe.wait_ge(y_copied, bp * 2 + (bb + 1))
                for k, (w, h) in enumerate(((0, hid_hi), (1, hid_hi), (0, hid_lo))):
                    if k == 2:
                        pe.wait_ge(lo_ready, n + (RING + 1))
                    m = mm(bank[4 + bb][:], w2_hl[:, e, w, :].bitcast(F32R), h[:, r].bitcast(F32R),
                           start=start and k == 0, stop=stop and k == 2, skip_group_check=True)
                m.then_inc(y_part, 1)

            def turn_y(bp, bb):
                pe.wait_ge(y_copied, bp * 2 + (bb + 3))
                pe.wait_ge(y_link, bp * 2 + (bb + 1))
                for t in range(TB):
                    m = nc.tensor.transpose(bank[6 + bb][:, t * P:(t + 1) * P], yt_sb[:, bb, t * P:(t + 1) * P], ident)
                m.then_inc(y_turned, 1)

            def pair_of_batches(bp, first=False, last=False):
                for r in range(RING):
                    down(bp, (0, r), start=r < 2)
                    up(bp, (1, r))
                    if r < 2 and not first:
                        turn_y(bp - 1, r)
                with pe.Fori(1, NE // 2 - 1) as e2:
                    for r in range(RING):
                        down(bp, (e2, r))
                        up(bp, (e2 + 1, r))
                for r in range(RING):
                    down(bp, (NE // 2 - 1, r), stop=r >= 2)
                    if not last:
                        up(bp + 1, (0, r))

            for r in range(RING):
                up(0, (0, r))
            pair_of_batches(0, first=True)
            with pe.Fori(1, NB // 2 - 1) as bp:
                pair_of_batches(bp)
            pair_of_batches(NB // 2 - 1, last=True)
            for bb in range(2):
                turn_y(NB // 2 - 1, bb)

        @block.vector
        def _(dve):
            v = nc.vector

            def link(ins, s, at):
                ins.then_inc(s, 1)
                dve.wait_ge(s, at)

            dve.wait_ge(ld_mod, 32)
            dve.wait_ge(su_exp, 1)
            link(v.tensor_scalar(c_e[:], c_e[:], 1.0, None, ALU.add), su_dve, 1)
            link(v.reciprocal(c_e[:], c_e[:]), su_dve, 2)
            link(v.tensor_tensor(sil[:], c_t[:], c_e[:], ALU.mult), su_dve, 3)
            dve.wait_ge(ld_const, 64)
            link(v.tensor_scalar(ang, const[:, C_IOTA:C_IOTA + SEQ], cols[:, K_THETA:K_THETA + 1], None, ALU.mult), su_dve, 4)
            n = 4
            for k, quarter in ((2, 0.25), (3, 0.0)):
                r = rope[:, k, :]
                for src, s1, s2, o0, o1 in ((ang, 1 / (2 * np.pi), quarter, ALU.mult, ALU.add),
                                            (turns, ROUND, ROUND, ALU.add, ALU.subtract)):
                    n += 1
                    link(v.tensor_scalar(turns, src, float(s1), float(s2), o0, o1), su_dve, n)
                for w, part_2pi in enumerate(TWO_PI):
                    n += 1
                    link(v.scalar_tensor_tensor(r, turns, -part_2pi, ang if w == 0 else r, ALU.mult, ALU.add), su_dve, n)
                n += 1
                link(v.tensor_scalar(r, r, float(2 * np.pi * quarter), PI_UNDER, ALU.add, ALU.min), su_dve, n)
                n += 1
                link(v.tensor_scalar(r, r, -PI_UNDER, None, ALU.max), su_dve, n)
            assert n == SU_COS
            link(v.tensor_scalar(root2s, cols[:, K_NODE:K_NODE + 1], 0.0, 2.0, ALU.max, ALU.mult), su_dve, SU_NODE)
            link(v.tensor_scalar(neg_s, cols[:, K_NODE:K_NODE + 1], -1.0, None, ALU.mult), su_dve, SU_NODE + 1)
            link(v.tensor_scalar(wfeat, cols[:, K_WEIGHT:K_WEIGHT + 1], 0.0, 1.0 / 32, ALU.max, ALU.mult), su_dve, SU_NODE + 2)
            link(v.tensor_scalar(top, cols[:, K_NODE:K_NODE + 1], CLIP, None, ALU.add), su_dve, SU_NODE + 3)
            v.tensor_copy(ident_bf[:], ident)
            brow = rows[0:64, R_BQKV:R_BQKV + 3 * D]
            link(v.tensor_copy(bias_hl[:].bitcast(F32R), brow), bias_link, 1)
            v.tensor_tensor(bias_hl[32:64, :].bitcast(F32R), brow[32:64], bias_hl[32:64, :], ALU.subtract)
            v.tensor_scalar(thirty2nds[:].bitcast(F32R), brow[:, 0:P], 0.0, 1.0 / 32, ALU.mult, ALU.add).then_inc(bias_link, 1)
            def moments(first, tiles, chain, at, var):
                for t in range(tiles):
                    m = v.bn_stats(stats[:, t, :], x_all[:, t, :] if first is None else one(x_all, first + t))
                m.then_inc(chain, 1)
                wait_apart(dve, chain, at)
                for t in range(tiles):
                    m = v.bn_aggr(mv[:, t, :], stats[:, t, :])
                m.then_inc(var, 1)

            dve.wait_ge(ld_x, 32)
            moments(None, NT, a1_dve, 1, ln_var)
            dve.wait_ge(su_mod_ev, 2 * NB)
            v.tensor_scalar(mod_all[:, :, 1, :], mod_all[:, :, 1, :], 1.0, None, ALU.add)
            link(v.tensor_scalar(mod_all[:, :, 4, :], mod_all[:, :, 4, :], 1.0, None, ALU.add), bias_link, 3)

            def normalise(g, batches, mean, rstd, chain, count, shift, scale1):
                tiles = batches * TB
                for t in range(tiles):
                    m = v.tensor_scalar(hrow[:, t, :], one(x_all, g * tiles + t), mean(t), rstd(t), ALU.subtract, ALU.mult)
                link(m, chain, count)
                for k, op in ((scale1, ALU.mult), (shift, ALU.add)):
                    for b in range(batches):
                        h = hrow[:, b * TB:(b + 1) * TB]
                        m = v.tensor_tensor(h, h, mod_all[:, bass.ds(g * batches + b, 1), k, :].to_broadcast([P, TB, D]), op)
                    if k == scale1:
                        link(m, chain, count + 1)
                return m

            def make_h(g):
                flat = mv[:].rearrange("p t k -> p (t k)")
                normalise(g, 1, lambda t: flat[:, bass.ds(g * (2 * TB) + 2 * t, 1)],
                          lambda t: std[:, bass.ds(g * TB + t, 1)], a1_dve, g * 2 + 3, 0, 1).then_inc(h_ready, 1)

            qk = qkv[:, :, 0:2 * D]

            def squares(g):
                dve.wait_ge(sq_ready, g + 1)
                link(v.tensor_reduce(ss[:], sq.rearrange("p t (h d) -> p t h d", d=AHD), AX, ALU.add), qk_link, g * 2 + 1)
                v.tensor_scalar(ss[:], ss[:], 1e-24, None, ALU.max).then_inc(ss_ready, 1)

            def unit_qk(g, first=False):
                dve.wait_ge(nrm_ready, g + 1)
                link(v.reciprocal(ss[:], ss[:]), qk_link, g * 2 + 2)
                if not first:
                    dve.wait_ge(qknT_done, g * 2)
                v.tensor_tensor(qkn.rearrange("p t (h d) -> p t h d", d=AHD), qk.rearrange("p t (h d) -> p t h d", d=AHD),
                                ss[:].unsqueeze(3).to_broadcast([P, TB, 2 * AH, AHD]), ALU.mult).then_inc(qkn_ready, 1)
                dve.wait_ge(qkn_ready, g + 1)

            def batch(g, first=False):
                dve.wait_ge(hT_done, g + 1)
                make_h(g + 1)
                squares(g)
                unit_qk(g, first)

            dve.wait_ge(ln_std, 1)
            link(v.reciprocal(std[:], std[:]), a1_dve, 2)
            make_h(0)
            sg = kf[:].rearrange("p j c q -> p (j c q)").rearrange("p (b d) -> p b d", d=D)
            mg = angles[:].rearrange("p j q -> p (j q)").rearrange("p (b d) -> p b d", d=D)
            for w, k in enumerate((2, 5)):
                g = mod_all[:, :, k, :]
                link(v.tensor_scalar(sg, g, 0.0, 2.0, ALU.is_ge, ALU.mult), su_dve, SU_MOD + 5 * w + 1)
                link(v.tensor_scalar(sg, sg, 1.0, None, ALU.subtract), su_dve, SU_MOD + 5 * w + 2)
                link(v.scalar_tensor_tensor(mg, g, -1.0, g, ALU.mult, ALU.max), su_dve, SU_MOD + 5 * w + 3)
                link(v.tensor_scalar(mg, mg, 0.25, None, ALU.max), su_dve, SU_MOD + 5 * w + 4)
                link(v.tensor_tensor(g, mg, sg, ALU.mult), su_dve, SU_MOD + 5 * w + 5)
            v.engine_nop().then_inc(su_modfix, 1)
            batch(0, True)
            with dve.Fori(1, NB - 1) as g:
                batch(g)
            squares(NB - 1)
            unit_qk(NB - 1)
            dve.wait_ge(su_sin, 2)
            link(v.tensor_scalar(rope[:, 3, :], rope[:, 3, :], const[:, C_SIGN:C_SIGN + 1], None, ALU.mult), su_dve, SU_STEPS - 1)
            link(v.tensor_scalar(rope[:, 0:2, :], rope[:, 2:4, :], -0.125, None, ALU.mult), su_dve, SU_STEPS)

            dve.sem_inc(att_ready, 1)
            dve.sem_inc(x1_done, 1)
            dve.wait_ge(v_saved, NB)
            dve.wait_ge(su_sin, 3)

            def clip_above(u, j):
                for n, f in enumerate((kf, qf)):
                    dve.wait_ge(feat_done, 2 * u + (n + 1))
                    v.tensor_scalar(f[:, j], bank[n][:].rearrange("p (c q) -> p c q", q=P), root2s, top,
                                    ALU.mult, ALU.min).then_inc(min_done, 1)

            def clip_below(n, u, j):
                dve.wait_ge(exp_done, 2 * u + (n + 1))
                if n == 0:
                    v.tensor_scalar(kf[:, j], kf[:, j], EXP_LOW, None, ALU.max).then_inc(kf_ready, 1)
                else:
                    v.tensor_scalar(qf[:, j], qf[:, j], EXP_LOW, wfeat, ALU.max, ALU.mult).then_inc(qw_ready, 1)

            def residual(i):
                dve.wait_ge(wo_done, i + 1)
                ga = mod_all[:, bass.ds(i // TB, 1), 2, :].squeeze(1)
                link(v.tensor_tensor(proj_tmp[:], bank[6][:, P:2 * P], ga, ALU.mult), x1_link, i + 1)
                xi = x_all[:, bass.ds(i, 1), :].squeeze(1)
                v.tensor_tensor(xi, xi, proj_tmp[:], ALU.add).then_inc(x1_done, 1)

            def a2_tile(i, first, last):
                for j in range(HALF):
                    u = i * HALF + j
                    for par in range(2):
                        dve.wait_ge(aw_done, 2 * u + (par + 1))
                        v.tensor_tensor(att_w[:, j, par], bank[3 + par][:].rearrange("p (c q) -> p c q", q=P),
                                        mask_a.unsqueeze(1).to_broadcast([P, HP, P]), ALU.mult).then_inc(aw_ready, 1)
                    if j == 0 or not last:
                        clip_above(u + 1, 1 - j)
                    dve.wait_ge(oT_done, u + 1)
                    v.tensor_copy(o_t[:], bank[5][:, 0:2 * P]).then_inc(oT_ready, 1)
                    if j == 0 or not last:
                        clip_below(0, u + 1, 1 - j)
                    if j == 0 or not last:
                        clip_below(1, u + 1, 1 - j)
                    dve.wait_ge(st_done, u + 1)
                    new = bank[7][:, 0:HP * 18].rearrange("p (c k) -> p c k", k=18)
                    for par in range(2):
                        rs = slice(64 * par, 64 * par + 64)
                        s = state[rs, j * HP:(j + 1) * HP, 0:9]
                        m = v.tensor_tensor(s, s, new[rs, :, 9 * par:9 * par + 9], ALU.add)
                    link(m, st_link, u + 1)
                    s = state[:, j * HP:(j + 1) * HP, 0:9]
                    v.tensor_scalar(s, s, const[:, bass.ds(C_KEEP + i, 1)], None, ALU.mult).then_inc(st_ready, 1)
                    if j == 0 and not first:
                        residual(i - 1)
                    if j == 0 and not first:
                        dve.wait_ge(attT_done, i)
                    dve.wait_ge(o2_done, u + 1)
                    o2 = bank[5][:, 2 * P:4 * P].rearrange("p (h k) -> p h k", k=32)
                    link(v.tensor_scalar(den[:], o2[:, :, AHD], 1e-6, None, ALU.max), att_link, 2 * u + 1)
                    link(v.reciprocal(den[:], den[:]), att_link, 2 * u + 2)
                    v.tensor_tensor(att[:, j * HH * AHD:(j + 1) * HH * AHD].rearrange("p (h d) -> p h d", d=AHD),
                                    o2[:, :, 0:AHD], den[:].unsqueeze(2).to_broadcast([P, HH, AHD]),
                                    ALU.mult).then_inc(att_ready, 1)

            clip_above(0, 0)
            clip_below(0, 0, 0)
            clip_below(1, 0, 0)
            a2_tile(0, True, False)
            with dve.Fori(1, NT - 1) as i:
                a2_tile(i, False, False)
            a2_tile(NT - 1, False, True)
            residual(NT - 1)
            dve.wait_ge(x1_done, NT + 1)
            dve.sem_inc(xnT_done, 2)
            dve.sem_inc(ao_set, 1)

            def inverse_deviation(g):
                moments(g % (NB // 2) * TT, TT, a3_dve, g * A3D + 1, a3_var)
                dve.wait_ge(a3_std, g + 1)
                link(v.reciprocal(std[:, 0:TT], std[:, 0:TT]), a3_dve, g * A3D + 2)

            inverse_deviation(0)
            with dve.Fori(0, NB // 2) as g:
                link(normalise(g, 2, lambda t: mv[:, t, 0:1], lambda t: std[:, t:t + 1], a3_dve, g * A3D + 3, 3, 4),
                     a3_dve, g * A3D + 5)
                inverse_deviation(g + 1)
                dve.wait_ge(a3_rms, g + 1)
                link(v.reciprocal(ms[:], ms[:]), a3_inv, g + 1)
                dve.wait_ge(xnT_done, g * 2 + 2)
                dve.wait_ge(ao_set, g + 1)
                for t in range(TT):
                    m = v.scalar_tensor_tensor(xn_tok[:, t, :], hrow[:, t, :], ms[:, t:t + 1], rows[:, R_G1:R_G1 + D],
                                               ALU.mult, ALU.mult)
                m.then_inc(xn_ready, 1)
                dve.wait_ge(xn_ready, g + 1)
            phase_end(dve, a_done)
            dve.wait_ge(a_done, 5)
            dve.sem_inc(s_min, 2)
            dve.sem_inc(o_added, 1)
            dve.sem_inc(pT_ready, 2)
            dve.sem_inc(c_ready, 1)
            dve.sem_inc(pT_done, 4)

            def rotate(which, u, first=False):
                dve.wait_ge(swapped, u * 64 + 64)
                if not first:
                    dve.wait_ge((q_ready, k_ready)[which], u)
                k = slice(2 * which, 2 * which + 2)
                v.tensor_tensor(part[:, k, :], raw[:, k, :], rope[:, k, :], ALU.mult).then_inc(
                    (q_part, k_part)[which], 1)

            def high_part(which, u, par):
                dve.wait_ge((q_ready, k_ready)[which], u + 1)
                v.tensor_copy((q_hl, k_hl)[which][:, par, 0].bitcast(F32R), (q_rot, k_rot)[which][:, par, :]
                              ).then_inc(qk_hi, 1)

            def minimum(u, t):
                for h in range(2):
                    s = t % 2 * 2 + h
                    dve.wait_ge(s_done, 8 * u + 2 * t + h + 1)
                    wait_apart(dve, pT_done, 8 * u + 2 * t + h + 1)
                    n = (t + 1) * P
                    v.tensor_tensor_reduce(out=prob[:, s, 0:n], in0=bank[3 + h][:, 0:n], in1=mask_b[:, SEQ - n:SEQ],
                                           scale=1.0, scalar=3e38, op0=ALU.add, op1=ALU.min,
                                           accum_out=low[:, s:s + 1]).then_inc(s_min, 1)

            def invert(u, t):
                dve.wait_ge(p_exp, 8 * u + 2 * t + 2)
                s = t % 2 * 2
                v.reciprocal(rinv[:, s:s + 2], rsum[:, s:s + 2]).then_inc(p_inv, 1)
                dve.wait_ge(p_inv, 4 * u + t + 1)
                for h in range(2):
                    pr = prob[:, s + h, 0:(t + 1) * P]
                    v.tensor_scalar(pr, pr, rinv[:, s + h:s + h + 1], None, ALU.mult).then_inc(p_ready, 1)

            def add_output(u):
                dve.wait_ge(o_done, u + 1)
                d = ao_all[:, bass.ds(u // PAIR * TB, TB), :]
                v.tensor_tensor(d, d, bank[0][:].rearrange("p (t d) -> p t d", d=D), ALU.add).then_inc(o_added, 1)

            def unit(u, par, first, last):
                minimum(u, 0)
                if not first:
                    invert(u - 1, 3)
                minimum(u, 1)
                invert(u, 0)
                if not last:
                    rotate(0, u + 1)
                if not last:
                    rotate(1, u + 1)
                minimum(u, 2)
                if not last:
                    high_part(0, u + 1, 1 - par)
                invert(u, 1)
                if not last:
                    high_part(1, u + 1, 1 - par)
                invert(u, 2)
                minimum(u, 3)
                if not first:
                    add_output(u - 1)

            for which in range(2):
                rotate(which, 0, True)
            for which in range(2):
                high_part(which, 0, 0)
            unit(0, 0, True, False)
            with dve.Fori(0, UNITS // 2 - 1) as i:
                unit(i * 2 + 1, 1, False, False)
                unit(i * 2 + 2, 0, False, False)
            unit(UNITS - 1, 1, False, True)
            invert(UNITS - 1, 3)
            add_output(UNITS - 1)
            phase_end(dve, b_done)
            dve.wait_ge(b_done, 5)
            v.memset(gates[:, :, NE - 1:NE], 1.0)
            v.tensor_copy(sel_all, sel_src[:].unsqueeze(2).to_broadcast([3 * NE, NE, P]))
            def make_an(b, first=False):
                ao_t = [ao_all[:, bass.ds(b * TT + t, 1), :].squeeze(1) for t in range(TT)]
                dve.wait_ge(t_rms, b + 1)
                link(v.reciprocal(t_ms[:], t_ms[:]), an_link, b + 1)
                if not first:
                    dve.wait_ge(sum_link, b)
                    dve.wait_ge(anT_done, b * 2)
                for t in range(TT):
                    m = v.scalar_tensor_tensor(an[:, t, :], ao_t[t], t_ms[:, t:t + 1], rows[:, R_G2:R_G2 + D],
                                               ALU.mult, ALU.mult)
                m.then_inc(an_ready, 1)

            def two_batches(b, last=False):
                base = b * TD
                dve.wait_ge(an_ready, b + 1)
                dve.wait_ge(anT_ready, b * 2 + 2)
                v.tensor_copy(an_hi[:, bass.ds(b * 2 * SEQ, 2 * SEQ)].bitcast(F32R),
                              an_t[:].rearrange("p j q -> p (j q)")).then_inc(an_split, 1)
                dve.wait_ge(lg_done, b + 1)
                link(v.tensor_tensor(logit[:], bank[2][:, 0:TT * NE].rearrange("p (t e) -> p t e", e=NE)[:, :, 0:NE - 1],
                                     rows[:, R_RB:R_RB + NE - 1].unsqueeze(1).to_broadcast([P, TT, NE - 1]), ALU.add),
                     t_dve, base + 1)
                link(v.tensor_reduce(red[:], logit[:], AX, ALU.max), t_dve, base + 2)
                v.tensor_tensor(logit[:], logit[:], red[:].unsqueeze(2).to_broadcast([P, TT, NE - 1]),
                                ALU.subtract).then_inc(lg_ready, 1)
                dve.wait_ge(ex_ready, b + 1)
                link(v.tensor_reduce(red[:], logit[:], AX, ALU.add), t_dve, base + 3)
                link(v.reciprocal(red[:], red[:]), t_dve, base + 4)
                link(v.tensor_tensor(aff[:], logit[:], red[:].unsqueeze(2).to_broadcast([P, TT, NE - 1]), ALU.mult),
                     t_dve, base + 5)
                dve.nop(nofuse=True)
                for t in range(TT):
                    m = v.max(top8[:, t, :], aff[:, t, :])
                m.then_inc(t_dve, 1)
                wait_apart(dve, t_dve, base + 6)
                for t in range(TT):
                    m = v.max_index(idx8[:, t, :], top8[:, t, :], aff[:, t, :])
                link(m, t_dve, base + 7)
                link(v.tensor_copy(idxf[:], idx8[:, :, 0:TOPK]), t_dve, base + 8)
                m = v.tensor_tensor(onehot[:].rearrange("p t k e -> p (t k) e"),
                                    const[:, C_EIOTA:C_EIOTA + NE - 1].unsqueeze(1).to_broadcast([P, TT * TOPK, NE - 1]),
                                    idxf[:].rearrange("p t k -> p (t k)").unsqueeze(2).to_broadcast([P, TT * TOPK, NE - 1]),
                                    ALU.is_equal)
                link(m, t_dve, base + 9)
                link(v.tensor_tensor(chosen[:], onehot[:, :, 0, :], onehot[:, :, 1, :], ALU.add), t_dve, base + 10)
                link(v.tensor_tensor(chosen[:], chosen[:], onehot[:, :, 2, :], ALU.add), t_dve, base + 11)
                v.tensor_tensor(gates[:, :, 0:NE - 1], aff[:], chosen[:], ALU.mult).then_inc(g_ready, 1)
                dve.wait_ge(g_ready, b + 1)
                g3 = [gates3[:, :, k * NE:(k + 1) * NE] for k in range(3)]
                link(v.tensor_copy(g3[0], gates[:]), t_dve, base + 12)
                link(v.tensor_tensor(rest[:], gates[:], g3[0], ALU.subtract), t_dve, base + 13)
                link(v.tensor_copy(g3[1], rest[:]), t_dve, base + 14)
                link(v.tensor_tensor(rest[:], rest[:], g3[1], ALU.subtract), t_dve, base + 15)
                v.tensor_copy(g3[2], rest[:]).then_inc(g3_ready, 1)
                if not last:
                    make_an(b + 1)
                dve.wait_ge(sum_link, b + 1)
                for j in range(2):
                    dve.wait_ge(b2_done, b * 2 + (j + 1))
                    tj = t_tmp[:, j * TB:(j + 1) * TB]
                    v.tensor_tensor(tj, tj, bank[6 + j][:].rearrange("p (t d) -> p t d", d=D), ALU.add).then_inc(b2_added, 1)

            make_an(0, True)
            with dve.Fori(0, NB // 2 - 1) as b:
                two_batches(b)
            two_batches(NB // 2 - 1, True)
            phase_end(dve, t_done_all)
            dve.wait_ge(t_done_all, 4)
            dve.sem_inc(gated, 2)
            dve.sem_inc(gelu_done, 2)
            dve.sem_inc(y_part, RING)
            dve.sem_inc(lo_ready, RING)
            for bb in range(2):
                dve.sem_inc(y_out[bb], 16)
            for credit in (y_link, y_copied, y_turned):
                dve.sem_inc(credit, 2)

            def low_weights(ready, parts, at, src):
                dve.wait_ge(w_hi, at)
                v.tensor_tensor(parts[:, 1].bitcast(F32R), src, parts[:, 0], ALU.subtract).then_inc(ready, 1)

            def slot(bp, e2, r):
                n = bp * SLOTS + e2 * RING + r
                e = bp * NE + e2 * 2 + r // 2
                if r % 2 == 0:
                    dve.wait_ge(gelu_done, n + 2)
                    low_weights(w1_ready, w1_hl[:, 1 - r // 2], e * 2 + 2, one(w1_all, (e2 * 2 + (r // 2 + 1)) % NE))
                else:
                    dve.wait_ge(y_part, n + 1)
                    low_weights(w2_ready, w2_hl[:, r // 2], e * 2 + 3, one(w2_all, e2 * 2 + r // 2))
                dve.wait_ge(gelu_done, n + 3)
                dve.wait_ge(gb_done, n + 1)
                v.tensor_tensor(hid[:, r], hid[:, r], bank[2 + r % 2][:], ALU.mult).then_inc(gated, 1)
                dve.wait_ge(gated, n + 3)
                dve.wait_ge(lo_ready, n + 1)
                dve.wait_ge(y_part, n + 1)
                v.tensor_copy(hid_hi[:, r].bitcast(F32R), hid[:, r]).then_inc(hi_ready, 1)

            def store_y(bp, bb):
                dve.wait_ge(y_turned, bp * 2 + (bb + 3))
                dve.wait_ge(y_out[bb], bp * 16 + 16)
                v.tensor_tensor(y_sb[:, bb], bank[6 + bb][:].rearrange("p (t d) -> p t d", d=D),
                                mod_all[:, bass.ds(bp * 2 + bb, 1), 5, :].to_broadcast([P, TB, D]),
                                ALU.mult).then_inc(y_link, 1)
                dve.wait_ge(y_link, bp * 2 + (bb + 3))
                dve.wait_ge(base_link, NB // 2 * 3)
                v.tensor_tensor(y_sb[:, bb], y_sb[:, bb], x_all[:, bass.ds(bp * (2 * TB) + bb * TB, TB), :],
                                ALU.add).then_inc(y_ready, 1)

            def pair_of_batches(bp, first):
                for e2 in range(2):
                    for r in range(RING):
                        slot(bp, e2, r)
                        if e2 == 1 and r < 2 and not first:
                            store_y(bp - 1, r)
                with dve.Fori(2, NE // 2) as e2:
                    for r in range(RING):
                        slot(bp, e2, r)

            dve.wait_ge(ld_w1, 16)
            dve.wait_ge(ld_w2, 16)
            low_weights(w1_ready, w1_hl[:, 0], 1, w1_all[:, 0, :])
            pair_of_batches(0, True)
            with dve.Fori(1, NB // 2) as bp:
                pair_of_batches(bp, False)
            for bb in range(2):
                store_y(NB // 2 - 1, bb)


def constants():
    p = np.arange(P)
    c = np.zeros((P, C_END), np.float32)
    c[:, C_ID:C_ID + P] = np.eye(P)
    c[:, C_MASKA:C_MASKA + P] = p[:, None] <= p[None]
    c[:, C_MASKB + SEQ - P:C_MASKB + SEQ] = np.where(p[None] > p[:, None], BIG, 0)
    c[:, C_IOTA:C_IOTA + SEQ] = np.arange(SEQ)
    c[:, C_EIOTA:C_EIOTA + NE] = np.arange(NE)
    c[:, C_KEEP:C_KEEP + NT] = np.arange(NT) % TB != TB - 1
    c[:, C_SIGN] = np.where(p // 32 % 2 == 0, -1, 1)
    sel = (np.arange(3 * NE)[:, None] % NE == np.arange(NE)[None]).astype(np.float32)
    return c, sel


def kernel(**inputs):
    import concourse.bacc as bacc
    from concourse.bass_utils import run_bass_kernel_spmd

    x = {k[3:]: np.asarray(v) for k, v in inputs.items()}
    c, sel = constants()

    def every(row, n=P):
        return np.broadcast_to(row.reshape(1, -1), (n, row.size))

    def halves(w):
        return w.reshape(w.shape[0], PAIR, 2, 32, 2).transpose(0, 1, 2, 4, 3).reshape(w.shape[0], PAIR, P)

    rows = np.zeros((P, R_END), np.float32)
    for at, k in ((R_BQKV, "attn_bqkv"), (R_BOUT, "attn_bout"), (R_G1, "ffn_gamma1"), (R_G2, "ffn_gamma2"),
                  (R_OB, "ffn_o_b"), (R_RB, "ffn_router_b")):
        rows[:, at:at + x[k].size] = every(x[k])
    cols = np.zeros((P, K_END), np.float32)
    node = np.arange(P) // 32 % 2
    cols[:, K_NODE] = x["attn_quad_nodes"][node]
    cols[:, K_WEIGHT] = x["attn_quad_weights"][node]
    cols[:, K_THETA] = x["ffn_theta"][np.arange(P) % 32]
    bias = [halves(x["ffn_q_b"][None])[0], halves(x["ffn_k_b"][None])[0], x["ffn_v_b"].reshape(PAIR, P)]
    cols[:, K_QKV:K_QKV + PAIR * 3] = np.stack(bias, -1).transpose(1, 0, 2).reshape(P, -1)
    cols[:, K_B1:K_B1 + NE] = np.concatenate([x["ffn_re_b1"], x["ffn_sh_b1"][None]]).T
    omega = np.zeros((AH, AHD, AH, 2, 32), np.float32)
    for h in range(AH):
        omega[h, :, h] = x["attn_omega"][:, h].transpose(1, 0, 2)
    wqkvb = np.stack([halves(x["ffn_q_w"]), halves(x["ffn_k_w"]), x["ffn_v_w"].reshape(D, PAIR, P)], 2)
    arrays = {
        "x": x["attn_x"], "c_t": x["c"].T, "wmod": x["wmod"], "const": c, "sel": sel, "rows": rows, "cols": cols,
        "wa_qkv": x["attn_Wqkv"], "wa_out": x["attn_Wout"], "omega_bd": omega.reshape(P, -1),
        "wqkvb": wqkvb, "wo": x["ffn_o_w"].reshape(PAIR, P, D).transpose(1, 0, 2),
        "wr": x["ffn_router_w"], "b2": np.concatenate([x["ffn_re_b2"], x["ffn_sh_b2"][None]]),
        "w1": np.concatenate([x["ffn_re_w1"], x["ffn_sh_w1"][None]]).transpose(1, 0, 2).reshape(D, -1),
        "w2": np.concatenate([x["ffn_re_w2"], x["ffn_sh_w2"][None]]).transpose(1, 0, 2).reshape(P, -1),
    }
    nc = bacc.Bacc("TRN2", target_bir_lowering=False, num_devices=1)
    aps, given = {}, {}
    for name, v in arrays.items():
        v = np.ascontiguousarray(v)
        given[f"in_{name}"] = v
        aps[name] = nc.dram_tensor(f"in_{name}", v.shape, mybir.dt.from_np(v.dtype), kind="ExternalInput").ap()
    out = nc.dram_tensor("out_y", (NB, SEQ, D), F32, kind="ExternalOutput").ap()
    build_block(nc, aps, out)
    r = run_bass_kernel_spmd(nc, [given], core_ids=[0])
    return r.results[0]["out_y"]
```
